# Optimizing a Trainium2 kernel written in Bass

```python
import numpy as np
import jax
import jax.numpy as jnp

def _softmax(x, axis=-1):
    return jax.nn.softmax(x, axis=axis)

def _gelu(x):
    return jax.nn.gelu(x, approximate=True)

def _silu(x):
    return jax.nn.silu(x)

def _sigmoid(x):
    return jax.nn.sigmoid(x)

def _layernorm(x, axis=-1, eps=1e-05):
    m = jnp.mean(x, axis=axis, keepdims=True)
    v = jnp.var(x, axis=axis, keepdims=True)
    return (x - m) / jnp.sqrt(v + eps)

def _scatter_add(tgt, idx, src, axis=0):
    return tgt.at[idx].add(src)

def _segment_sum(src, seg, n):
    return jax.ops.segment_sum(src, seg, n)
kernel_name = 'mk_xattn_ffn_d1_seqx_r4_b6be1d'

def setup_inputs(seed: int=0):
    np.random.seed(seed)
    _w = jnp.asarray

    def _rec_inputs():
        import jax
        import jax.numpy as jnp
        _rk = jax.random.key(seed)
        x = -0.0001231 + 1 * jax.random.normal(jax.random.fold_in(_rk, 1), (8, 512, 256), jnp.float32)
        _lenS = 512 - jax.random.randint(jax.random.fold_in(_rk, 7), (8,), 0, max(1, 512 // 4) + 1, jnp.int32)
        _lenS2 = 64 - jax.random.randint(jax.random.fold_in(_rk, 8), (8,), 0, max(1, 64 // 4) + 1, jnp.int32)
        _ctx_1024P = jax.random.normal(jax.random.fold_in(_rk, 11), (8, 16, 256), jnp.float32)
        _ctx_1024c = jax.random.dirichlet(jax.random.fold_in(_rk, 511), 0.3 * jnp.ones((16,), jnp.float32), (8, 64))
        _ctx_1024t = jnp.einsum('bsk,bkd->bsd', _ctx_1024c, _ctx_1024P)
        _ctx_1024t = _ctx_1024t * jax.lax.rsqrt(jnp.mean(jnp.square(_ctx_1024t)) + 1e-12) * 0.953939
        ctx_1024 = -0.000137203 + 0.999727 * (_ctx_1024t + 0.3 * jax.random.normal(jax.random.fold_in(_rk, 611), (8, 64, 256), jnp.float32))
        return (x, ctx_1024)
    x, ctx_1024 = _rec_inputs()

    def _L0_xattn_setup():
        import jax, jax.numpy as jnp
        import numpy as np
        B, Q, K, D = (4, 375, 375, 256)
        H, HD = (16, 64)
        key = jax.random.key(seed)
        ks = jax.random.split(key, 10)
        s = 0.02
        return {'inputs_q': jax.random.normal(ks[0], (B, Q, D), jnp.float32), 'inputs_kv': jax.random.normal(ks[1], (B, K, D), jnp.float32), 'Wq': jax.random.normal(ks[2], (D, H, HD), jnp.float32) * s, 'bq': jnp.zeros((H, HD), jnp.float32), 'Wk': jax.random.normal(ks[3], (D, H, HD), jnp.float32) * s, 'bk': jnp.zeros((H, HD), jnp.float32), 'Wv': jax.random.normal(ks[4], (D, H, HD), jnp.float32) * s, 'bv': jnp.zeros((H, HD), jnp.float32), 'Wo': jax.random.normal(ks[5], (H, HD, D), jnp.float32) * s, 'bo': jnp.zeros((D,), jnp.float32)}
    _L0_xattn_all = _L0_xattn_setup()
    _L0_xattn_in = {k: v for k, v in _L0_xattn_all.items() if k in ('Wq', 'bq', 'Wk', 'bk', 'Wv', 'bv', 'Wo', 'bo')}
    del _L0_xattn_all

    def _L0_ffn_setup():
        import jax, jax.numpy as jnp
        import numpy as np
        D = 256
        H = 16
        FF = 1024
        E = 8
        K = 2
        EH = 256
        B, S = (2, 512)
        EPS = 1e-05

        def rmsnorm(x, w):
            v = jnp.mean(jnp.square(x), axis=-1, keepdims=True)
            return x * jax.lax.rsqrt(v + EPS) * w

        def _dense_path(x, wq, wk, wv, wo, w1, w2, w3, attn_norm_w, ff_norm_w):
            b, s, d = x.shape
            hd = d // H
            q = (x @ wq).reshape(b, s, H, hd)
            k = (x @ wk).reshape(b, s, H, hd)
            v = (x @ wv).reshape(b, s, H, hd)
            scores = jnp.einsum('bqhd,bkhd->bhqk', q, k) / np.sqrt(hd).astype(np.float32)
            causal = jnp.tril(jnp.ones((s, s), bool))
            scores = jnp.where(causal, scores, jnp.finfo(scores.dtype).min)
            attn = jax.nn.softmax(scores, axis=-1)
            o = jnp.einsum('bhqk,bkhd->bqhd', attn, v).reshape(b, s, d)
            h = x + rmsnorm(o @ wo, attn_norm_w)
            ffn = jax.nn.silu(h @ w1) * (h @ w3) @ w2
            return h + rmsnorm(ffn, ff_norm_w)

        def _sparse_path(x, router_w, ew1, ew2, ew3, moe_norm_w):
            b, s, d = x.shape
            xt = x.reshape(-1, d)
            probs = jax.nn.softmax(xt @ router_w, axis=-1)
            topw, topi = jax.lax.top_k(probs, K)
            g = jax.nn.silu(jnp.einsum('td,edh->eth', xt, ew1)) * jnp.einsum('td,edh->eth', xt, ew3)
            eo = jnp.einsum('eth,ehd->ted', g, ew2)
            sel = jnp.take_along_axis(eo, topi[:, :, None], axis=1)
            moe_out = jnp.sum(topw[:, :, None] * sel, axis=1).reshape(b, s, d)
            return rmsnorm(moe_out, moe_norm_w)
        key = jax.random.key(seed)
        ks = jax.random.split(key, 16)
        s = 0.02
        return {'x': jax.random.normal(ks[0], (B, S, D), jnp.float32), 'wq': jax.random.normal(ks[1], (D, D), jnp.float32) * s, 'wk': jax.random.normal(ks[2], (D, D), jnp.float32) * s, 'wv': jax.random.normal(ks[3], (D, D), jnp.float32) * s, 'wo': jax.random.normal(ks[4], (D, D), jnp.float32) * s, 'w1': jax.random.normal(ks[5], (D, FF), jnp.float32) * s, 'w2': jax.random.normal(ks[6], (FF, D), jnp.float32) * s, 'w3': jax.random.normal(ks[7], (D, FF), jnp.float32) * s, 'attn_norm_w': jnp.ones((D,), jnp.float32), 'ff_norm_w': jnp.ones((D,), jnp.float32), 'moe_norm_w': jnp.ones((D,), jnp.float32), 'router_w': jax.random.normal(ks[8], (D, E), jnp.float32) * s, 'ew1': jax.random.normal(ks[9], (E, D, EH), jnp.float32) * s, 'ew2': jax.random.normal(ks[10], (E, EH, D), jnp.float32) * s, 'ew3': jax.random.normal(ks[11], (E, D, EH), jnp.float32) * s}
    _L0_ffn_all = _L0_ffn_setup()
    _L0_ffn_in = {k: v for k, v in _L0_ffn_all.items() if k in ('wq', 'wk', 'wv', 'wo', 'w1', 'w2', 'w3', 'attn_norm_w', 'ff_norm_w', 'moe_norm_w', 'router_w', 'ew1', 'ew2', 'ew3')}
    del _L0_ffn_all
    return {'x': x, 'ctx_1024': ctx_1024, 'L0_xattn_Wq': _L0_xattn_in['Wq'], 'L0_xattn_bq': _L0_xattn_in['bq'], 'L0_xattn_Wk': _L0_xattn_in['Wk'], 'L0_xattn_bk': _L0_xattn_in['bk'], 'L0_xattn_Wv': _L0_xattn_in['Wv'], 'L0_xattn_bv': _L0_xattn_in['bv'], 'L0_xattn_Wo': _L0_xattn_in['Wo'], 'L0_xattn_bo': _L0_xattn_in['bo'], 'L0_ffn_wq': _L0_ffn_in['wq'], 'L0_ffn_wk': _L0_ffn_in['wk'], 'L0_ffn_wv': _L0_ffn_in['wv'], 'L0_ffn_wo': _L0_ffn_in['wo'], 'L0_ffn_w1': _L0_ffn_in['w1'], 'L0_ffn_w2': _L0_ffn_in['w2'], 'L0_ffn_w3': _L0_ffn_in['w3'], 'L0_ffn_attn_norm_w': _L0_ffn_in['attn_norm_w'], 'L0_ffn_ff_norm_w': _L0_ffn_in['ff_norm_w'], 'L0_ffn_moe_norm_w': _L0_ffn_in['moe_norm_w'], 'L0_ffn_router_w': _L0_ffn_in['router_w'], 'L0_ffn_ew1': _L0_ffn_in['ew1'], 'L0_ffn_ew2': _L0_ffn_in['ew2'], 'L0_ffn_ew3': _L0_ffn_in['ew3']}

def reference(x, ctx_1024, L0_xattn_Wq, L0_xattn_bq, L0_xattn_Wk, L0_xattn_bk, L0_xattn_Wv, L0_xattn_bv, L0_xattn_Wo, L0_xattn_bo, L0_ffn_wq, L0_ffn_wk, L0_ffn_wv, L0_ffn_wo, L0_ffn_w1, L0_ffn_w2, L0_ffn_w3, L0_ffn_attn_norm_w, L0_ffn_ff_norm_w, L0_ffn_moe_norm_w, L0_ffn_router_w, L0_ffn_ew1, L0_ffn_ew2, L0_ffn_ew3):
    import jax
    import jax.numpy as jnp

    def _L0_xattn_ref(inputs_q, inputs_kv, Wq, bq, Wk, bk, Wv, bv, Wo, bo):
        import jax, jax.numpy as jnp
        import numpy as np
        B, Q, K, D = (4, 375, 375, 256)
        H, HD = (16, 64)
        q = jnp.einsum('bqm,mhd->bqhd', inputs_q, Wq) + bq
        k = jnp.einsum('bkm,mhd->bkhd', inputs_kv, Wk) + bk
        v = jnp.einsum('bkm,mhd->bkhd', inputs_kv, Wv) + bv
        q = q / jnp.sqrt(jnp.asarray(HD, q.dtype))
        attn = jnp.einsum('bqhd,bkhd->bhqk', q, k)
        attn = jax.nn.softmax(attn, axis=-1)
        out = jnp.einsum('bhqk,bkhd->bqhd', attn, v)
        return jnp.einsum('bqhd,hdm->bqm', out, Wo) + bo

    def _L0_ffn_ref(x, wq, wk, wv, wo, w1, w2, w3, attn_norm_w, ff_norm_w, moe_norm_w, router_w, ew1, ew2, ew3):
        import jax, jax.numpy as jnp
        import numpy as np
        D = 256
        H = 16
        FF = 1024
        E = 8
        K = 2
        EH = 256
        B, S = (2, 512)
        EPS = 1e-05

        def rmsnorm(x, w):
            v = jnp.mean(jnp.square(x), axis=-1, keepdims=True)
            return x * jax.lax.rsqrt(v + EPS) * w

        def _dense_path(x, wq, wk, wv, wo, w1, w2, w3, attn_norm_w, ff_norm_w):
            b, s, d = x.shape
            hd = d // H
            q = (x @ wq).reshape(b, s, H, hd)
            k = (x @ wk).reshape(b, s, H, hd)
            v = (x @ wv).reshape(b, s, H, hd)
            scores = jnp.einsum('bqhd,bkhd->bhqk', q, k) / np.sqrt(hd).astype(np.float32)
            causal = jnp.tril(jnp.ones((s, s), bool))
            scores = jnp.where(causal, scores, jnp.finfo(scores.dtype).min)
            attn = jax.nn.softmax(scores, axis=-1)
            o = jnp.einsum('bhqk,bkhd->bqhd', attn, v).reshape(b, s, d)
            h = x + rmsnorm(o @ wo, attn_norm_w)
            ffn = jax.nn.silu(h @ w1) * (h @ w3) @ w2
            return h + rmsnorm(ffn, ff_norm_w)

        def _sparse_path(x, router_w, ew1, ew2, ew3, moe_norm_w):
            b, s, d = x.shape
            xt = x.reshape(-1, d)
            probs = jax.nn.softmax(xt @ router_w, axis=-1)
            topw, topi = jax.lax.top_k(probs, K)
            g = jax.nn.silu(jnp.einsum('td,edh->eth', xt, ew1)) * jnp.einsum('td,edh->eth', xt, ew3)
            eo = jnp.einsum('eth,ehd->ted', g, ew2)
            sel = jnp.take_along_axis(eo, topi[:, :, None], axis=1)
            moe_out = jnp.sum(topw[:, :, None] * sel, axis=1).reshape(b, s, d)
            return rmsnorm(moe_out, moe_norm_w)
        dense_out = _dense_path(x, wq, wk, wv, wo, w1, w2, w3, attn_norm_w, ff_norm_w)
        sparse_out = _sparse_path(x, router_w, ew1, ew2, ew3, moe_norm_w)
        return dense_out + sparse_out
    x = x + _L0_xattn_ref(_layernorm(x, axis=-1), ctx_1024, L0_xattn_Wq, L0_xattn_bq, L0_xattn_Wk, L0_xattn_bk, L0_xattn_Wv, L0_xattn_bv, L0_xattn_Wo, L0_xattn_bo)
    x = x + _L0_ffn_ref(_layernorm(x, axis=-1), L0_ffn_wq, L0_ffn_wk, L0_ffn_wv, L0_ffn_wo, L0_ffn_w1, L0_ffn_w2, L0_ffn_w3, L0_ffn_attn_norm_w, L0_ffn_ff_norm_w, L0_ffn_moe_norm_w, L0_ffn_router_w, L0_ffn_ew1, L0_ffn_ew2, L0_ffn_ew3)
    return x

_drawn_inputs = setup_inputs


def setup_inputs(seed=0):
    import zlib

    import numpy as np

    out = dict(_drawn_inputs(seed))
    spreads = {'L0_xattn_bq': (0.0, 0.669),
     'L0_xattn_bk': (0.0, 0.8),
     'L0_xattn_bv': (0.0, 0.1),
     'L0_xattn_bo': (0.0, 0.1),
     'L0_ffn_attn_norm_w': (1.0, 0.2),
     'L0_ffn_ff_norm_w': (1.0, 0.2),
     'L0_ffn_moe_norm_w': (1.0, 0.2)}
    factors = {'L0_xattn_Wq': 3.327, 'L0_xattn_Wk': 3.206}
    for name, (base, spread) in spreads.items():
        noise = np.random.default_rng([zlib.crc32(name.encode()), seed]).standard_normal(out[name].shape)
        drawn = base * np.exp(spread * noise) if base else spread * noise
        out[name] = jnp.asarray(drawn.astype(out[name].dtype))
    for name, factor in factors.items():
        out[name] = (out[name] * factor).astype(out[name].dtype)
    return out
```

```python
from contextlib import ExitStack

import concourse.bass as bass
from concourse import mybir

ALU = mybir.AluOpType
ACT = mybir.ActivationFunctionType
AX = mybir.AxisListType
F32 = mybir.dt.float32
BF16 = mybir.dt.bfloat16

P = 128
B, S, D = 8, 512, 256
T = S // P
KD = D // P
CH, CHD, CK = 16, 64, 64
PAIRS = CH // 2
H, HD = 16, 16
HB = P // HD
NREP = 6
KREP = NREP * HD
MROWS = 3
G = H // 4
FF = 1024
FB = FF // P
E, EH = 8, 256
EB = EH // P
EPS = 1e-5
MASKED = -1e30
Q_PART = (0, 0, 1, 1, 0, 2)
K_PART = (0, 1, 0, 1, 2, 0)

PER = dict(
    x_in=16, kv_in=64, mv1=1, rstd1=1, xn1=4, xT1=2, xnT=2,
    m_ps=4, m_act=2, m_dve=2, bqk_ps=2, bqk_sb=2, vw_ps=4, vw_act=2, vw_dve=2,
    sc_ps=4, sc_add=4, sc_max=4, sc_sub=4, sc_exp=4, sc_sum=4, sc_rec=4, sc_nrm=4,
    pT_ps=8, pT_sb=8, pv_ps=4, xb=1, x1=4, mv2=4, rstd2=4, xn2=4, xT2=2, xn2T=2,
    qk_ps=4, part1=4, rest1=4, part2=4, part3=4, v_ps=4, v_sb=4, lg=4, q_out=96, k_out=96, rep_q=96, rep_k=96,
    gmax=1, gexp=1, gate=1,
    a_ps=32, a_max=32, m_part=1, mT_ps=1, mT_sb=1, m_row=48,
    b_ps=20, b_exp=20, av_ps=4, av_sb=4, avT_ps=4, o_rec=4, o_nrm=4,
    oT_ps=2, oT_sb=2, wo_ps=4, wo_sq=4, wo_ri=4, wo_n=4, h=4, hT_ps=2, hT_sb=2,
    mu_ps=16, mu_th=16, mu_u=16, mu_g=16, md_ps=16, md_acc=16,
    mo_sq=1, mo_ri=1, mo_y=4,
    fu_ps=8, fu_th=8, fu_u=8, fu_g=8, fd_ps=4, fd_sq=4, fd_ri=4, fd_n=4, y=4, out=16,
    pool_step=22, dve_step=11, stats=5,
)
AHEAD = dict(vw_ps=1, out=16, fd_ps=1, fd_n=1, av_ps=1, y=1, md_ps=1)


def moe_steps():
    ups = [("up", e, m) for e in range(E) for m in range(EB)]
    downs = [("down", e, t2) for e in range(E) for t2 in range(2)]
    steps = ups[:3]
    for u, d in zip(ups[3:] + [None] * 3, downs):
        steps.append(d)
        if u:
            steps.append(u)
    return steps + downs[len(ups):]


def attention_schedule():
    moe = moe_steps()
    steps = []

    def experts(n):
        for _ in range(min(n, len(moe))):
            steps.append(moe.pop(0))

    for hp in range(H // 2):
        steps.append(("max", hp))
        experts(1)
    steps.append(("shift",))
    experts(3)
    steps.append(("shift_rows",))
    experts(2)
    for g in range(G):
        for u in range(5):
            steps.append(("score", g, u))
            if g and u == 1:
                steps.append(("out_t", g - 1))
            if u % 2 == 0 or g == 0:
                experts(1)
        steps.append(("value", g))
    experts(2)
    steps.append(("out_t", G - 1))
    experts(len(moe))
    return steps


STEPS = attention_schedule()


def score_segments(j):
    order = (0, 1, 3, 2) if j % 2 == 0 else (2, 0, 1, 3)
    at = j * 1280
    found = []
    for kb in order:
        n = S - kb * P
        found.append((kb, at, n))
        at += n
    return found


def xattn_ffn(nc, A, out):
    per = PER
    counted = {}
    with ExitStack() as ctx:
        def sb(name, shape, dt=F32):
            return ctx.enter_context(nc.sbuf_tensor(name, shape, dt))

        sems = {n: ctx.enter_context(nc.semaphore(n)) for n in per}
        kv_out = [ctx.enter_context(nc.semaphore(f"p0_kv_out{i}")) for i in range(4)]
        p0 = {n: ctx.enter_context(nc.semaphore("p0_" + n)) for n in (
            "w_early", "w_late", "ident", "const", "tr_ps", "tr_sb", "kv_ps", "kv_sb", "bq", "bk")}
        e_in = [ctx.enter_context(nc.semaphore(f"e_in{i}")) for i in range(2)]

        wo_c = sb("wo_c", [P, PAIRS, D])
        wqT = sb("wqT", [P, PAIRS, D])
        wq = sb("wq", [P, KD, D])
        wk = sb("wk", [P, KD, D])
        wv = sb("wv", [P, KD, D + E])
        wo = sb("wo", [P, KD, D])
        w1 = sb("w1", [P, KD, FF])
        w3 = sb("w3", [P, KD, FF])
        w2 = sb("w2", [P, FB, D])
        ew = sb("ew", [P, 2, 3, KD, D])
        bq = sb("bq", [P, PAIRS])
        bk = sb("bk", [P, PAIRS])
        bv = sb("bv", [P, PAIRS])
        bo_bc = sb("bo_bc", [P, D])
        aw_bc = sb("aw_bc", [P, D])
        fw_bc = sb("fw_bc", [P, D])
        mw_bc = sb("mw_bc", [P, D])
        ident = sb("ident", [P, P])
        ident_b = sb("ident_b", [P, P], BF16)
        mask_qk = sb("mask_qk", [P, P], BF16)
        mask_kq = sb("mask_kq", [P, P], BF16)
        neg_half = sb("neg_half", [P, T])
        k_bd = sb("k_bd", [P, PAIRS, P])
        v_bd = sb("v_bd", [P, PAIRS, P])
        big = sb("big", [P, 2 * 5120])
        bigf = big[:, :]

        def part(a, n):
            return bigf[:, a:a + n]

        m_sb = part(0, 2048).rearrange("p (k n) -> p k n", k=KD)
        vw = part(2048, 2048).rearrange("p (a n) -> p a n", a=PAIRS)
        bqk = part(4096, 1024)
        s_sb = part(5120, 2048).rearrange("p (i n) -> p i n", i=2)
        pT = part(7168, 2048).rearrange("p (i n) -> p i n", i=2)
        bq_bc = part(9216, 1024).rearrange("p (a n) -> p a n", a=PAIRS)
        prob = bigf.rearrange("p (i n) -> p i n", i=2)
        wq_c = part(0, 2048).rearrange("p (k n) -> p k n", k=KD)
        wk_c = part(2048, 2048).rearrange("p (k n) -> p k n", k=KD)
        wv_c = part(4096, 2048).rearrange("p (k n) -> p k n", k=KD)
        ctx_in = part(6144, 1024).rearrange("p (t n) -> p t n", t=4)
        ctxT = part(7168, 1024).rearrange("p (k n) -> p k n", k=KD)
        kv_st = part(8192, 2048).rearrange("p (i n) -> p i n", i=4)

        x1 = sb("x1", [P, T, D])
        xn = sb("xn", [P, T, D])
        acc = sb("acc", [P, T, D])
        xn2T = sb("xn2T", [P, KD, S])
        hT = sb("hT", [P, KD, S])
        o_tok = sb("o_tok", [P, T, D])
        oT = sb("oT", [P, KD, S])
        xnT = hT
        pieces = [hT[:, :, :].bitcast(BF16), o_tok[:, :, :].rearrange("p t n -> p (t n)").bitcast(BF16),
                  oT[:, :, :].bitcast(BF16)]
        parts = [hT[:, :, :].rearrange("p k n -> p (k n)").bitcast(BF16).rearrange("p (a n) -> p a n", a=4),
                 pieces[1].rearrange("p (a n) -> p a n", a=4),
                 oT[:, :, :].rearrange("p k n -> p (k n)").bitcast(BF16).rearrange("p (a n) -> p a n", a=4)]
        rest = sb("rest", [P, 2, S])
        q_rep = sb("q_rep", [P, H, S], BF16)
        k_rep = sb("k_rep", [P, H, S], BF16)
        gT = q_rep[:, :, :].rearrange("p h n -> p (h n)").bitcast(F32).rearrange("p (m n) -> p m n", m=FB)
        v_aug = sb("v_aug", [P, T, H, 32])
        mg = sb("mg", [P, 2, EB, S])
        th = sb("th", [P, 2, S])
        uu = sb("uu", [P, 2, S])
        av = sb("av", [P, S])
        st1 = sb("st1", [P, T, 6])
        st2 = sb("st2", [P, T, 6])
        mv1 = sb("mv1", [P, T, 2])
        mv2 = sb("mv2", [P, T, 2])
        rs1 = sb("rs1", [P, T])
        rs2 = sb("rs2", [P, T])
        ve = sb("ve", [P, 24, T])
        cmax = sb("cmax", [P, 2, CH])
        csum = sb("csum", [P, 2, CH])
        crec = sb("crec", [P, 2, CH])
        lg = sb("lg", [P, T, E])
        g_a = sb("g_a", [P, T, E])
        g_b = sb("g_b", [P, T, E])
        g_s = sb("g_s", [P, T, 8])
        gate = sb("gate", [P, T, E])
        g1 = sb("g1", [P, T])
        g2 = sb("g2", [P, T])
        nm = sb("nm", [P, T, H])
        nr = sb("nr", [P, T, H])
        nparts = sb("nparts", [P, T, P], BF16)
        npart = nparts[:, :, 0:MROWS * H].rearrange("p t (r h) -> p t r h", r=MROWS)
        eps = sb("eps", [P, 2, T])
        spare = sb("spare", [P, 1])
        mT = sb("mT", [MROWS * H, S], BF16)
        orec = sb("orec", [P, T, 4])
        ss = sb("ss", [P, 3, T])
        ri = sb("ri", [P, 3, T])
        squares = th[:, :, :].rearrange("p i n -> p (i n)").rearrange("p (t d) -> p t d", t=T)

        ps = ctx.enter_context(nc.psum_tensor("ps", [P, 8 * 512], F32))

        def bank(i, n=512, at=0, count=1):
            return ps[:, i * 512 + at:i * 512 + at + n]

        kt_d = nc.dram_tensor("kt_d", (PAIRS, P, B * CK), F32, kind="Internal").ap()
        parts_d = nc.dram_tensor("parts_d", (3, 2, KD, P, S), BF16, kind="Internal").ap()
        vt_d = nc.dram_tensor("vt_d", (PAIRS, P, B * CK), F32, kind="Internal").ap()

        def done(ins, name, n=1):
            counted[name] = counted.get(name, 0) + n
            return ins.then_inc(sems[name], n)

        def need(eng, b, name, k):
            eng.wait_ge(sems[name], b * per[name] + k + AHEAD.get(name, 0))

        def before(eng, b, name):
            eng.wait_ge(sems[name], b * per[name] + AHEAD[name])

        def carry_wait():
            nc.vector.memset(spare[:, :], 0.0)

        x_v = A["x"].rearrange("b (t p) d -> b p t d", p=P)
        y_v = out.rearrange("b (t p) d -> b p t d", p=P)

        block = ctx.enter_context(nc.Block())

        @block.sync
        def _(sp):
            for k in range(KD):
                rows = slice(k * P, (k + 1) * P)
                for dst, src in ((wk_c, "L0_xattn_Wk"), (wq_c, "L0_xattn_Wq"), (wv_c, "L0_xattn_Wv")):
                    sp.dma_start(dst[:, k, :], A[src].rearrange("m h d -> m (h d)")[rows, :]).then_inc(p0["w_early"], 16)
            sp.dma_start(ctx_in, A["ctx_1024"].rearrange("b k m -> (b k) m").rearrange("(t p) m -> p t m", p=P)).then_inc(p0["w_early"], 16)
            for dst, src in ((bq, "L0_xattn_bq"), (bk, "L0_xattn_bk"), (bv, "L0_xattn_bv")):
                sp.dma_start(dst[:, :], A[src].rearrange("h d -> (h d)").rearrange("(a p) -> p a", p=P),
                             allow_slow_non_contiguous=True).then_inc(p0["w_early"], 16)
            sp.dma_start(wo_c[:, :, :], A["L0_xattn_Wo"].rearrange("h d m -> (h d) m").rearrange("(a p) m -> p a m", p=P)).then_inc(p0["w_late"], 16)
            for dst, src in ((wq, "L0_ffn_wq"), (wk, "L0_ffn_wk"), (wo, "L0_ffn_wo"), (w1, "L0_ffn_w1"), (w3, "L0_ffn_w3"), (w2, "L0_ffn_w2")):
                sp.dma_start(dst[:, :, :], A[src].rearrange("(k p) n -> p k n", p=P)).then_inc(p0["w_late"], 16)
            sp.dma_start(wv[:, :, 0:D], A["L0_ffn_wv"].rearrange("(k p) n -> p k n", p=P)).then_inc(p0["w_late"], 16)
            sp.dma_start(wv[:, :, D:D + E], A["L0_ffn_router_w"].rearrange("(k p) n -> p k n", p=P)).then_inc(p0["w_late"], 16)
            for dst, src in ((bo_bc, "L0_xattn_bo"), (aw_bc, "L0_ffn_attn_norm_w"), (fw_bc, "L0_ffn_ff_norm_w"), (mw_bc, "L0_ffn_moe_norm_w")):
                sp.dma_start(dst[:, :], A[src].partition_broadcast(P)).then_inc(p0["w_late"], 16)
            for i in range(2 * PAIRS):
                sp.wait_ge(p0["kv_sb"], i + 1)
                dst = (kt_d, vt_d)[i % 2]
                sp.dma_start(dst[i // 2, :, :], kv_st[:, i % 4, :]).then_inc(kv_out[i % 4], 16)
            for i in range(4):
                sp.wait_ge(kv_out[i], 16 * 2 * PAIRS // 4)
            sp.wait_ge(p0["const"], 9)
            with sp.Fori(0, B, 1) as b:
                before(sp, b, "vw_ps")
                for dst, src in ((k_bd, kt_d), (v_bd, vt_d)):
                    for i in range(2):
                        half = slice(i * CHD, (i + 1) * CHD)
                        done(sp.dma_start(dst[half, :, i * CK:(i + 1) * CK],
                                          src.rearrange("a p n -> p a n")[half, :, bass.ds(b * CK, CK)]), "kv_in", 16)
                before(sp, b, "out")
                done(sp.dma_start(x1[:, :, :], x_v[bass.ds(b, 1), :, :, :].rearrange("a p t d -> p (a t) d")), "x_in", 16)
                for a in range(4):
                    for i, name in enumerate(("part1", "part2", "part3")):
                        need(sp, b, name, a + 1)
                        done(sp.dma_start(parts_d[i, a // 2, a % 2, :, :], parts[i][:, a, :]), ("q_out", "k_out")[a // 2], 16)
                before(sp, b, "fd_ps")
                for which, part_of, rep, out_name, name in ((0, Q_PART, q_rep, "q_out", "rep_q"), (1, K_PART, k_rep, "k_out", "rep_k")):
                    need(sp, b, out_name, per[out_name])
                    for j in range(NREP):
                        src = parts_d[part_of[j], which, :, :, :].rearrange("a (h d) n -> d (a h) n", d=HD)
                        done(sp.dma_start(rep[j * HD:(j + 1) * HD, :, :], src), name, 16)
                need(sp, b, "mT_sb", 1)
                for r in range(MROWS):
                    done(sp.dma_start(q_rep[KREP + r:KREP + r + 1, :, :], mT[r * H:(r + 1) * H, :]), "m_row", 16)
                need(sp, b, "y", T)
                done(sp.dma_start(y_v[bass.ds(b, 1), :, :, :].rearrange("a p t d -> p (a t) d"), x1[:, :, :]), "out", 16)
            sp.wait_ge(sems["out"], AHEAD["out"] + 16 * B)

        @block.gpsimd
        def _(pool):
            for name, n in AHEAD.items():
                pool.sem_inc(sems[name], n)
            nc.gpsimd.memset(ident[:, :], 0.0).then_inc(p0["ident"], 1)
            nc.gpsimd.memset(ident_b[:, :], 0.0).then_inc(p0["ident"], 1)
            nc.gpsimd.memset(mask_qk[:, :], 0.0).then_inc(p0["ident"], 1)
            nc.gpsimd.memset(mask_kq[:, :], 0.0).then_inc(p0["ident"], 1)
            pool.wait_ge(p0["ident"], 4)
            for m in (ident, ident_b):
                nc.gpsimd.affine_select(out=m[:, :], in_=m[:, :], compare_op=ALU.not_equal, fill=1.0, base=0,
                                        pattern=[[-1, P]], channel_multiplier=1).then_inc(p0["ident"], 1)
            nc.gpsimd.affine_select(out=mask_qk[:, :], in_=mask_qk[:, :], compare_op=ALU.is_ge, fill=MASKED, base=0,
                                    pattern=[[-1, P]], channel_multiplier=1).then_inc(p0["ident"], 1)
            nc.gpsimd.affine_select(out=mask_kq[:, :], in_=mask_kq[:, :], compare_op=ALU.is_ge, fill=MASKED, base=0,
                                    pattern=[[1, P]], channel_multiplier=-1).then_inc(p0["ident"], 1)
            nc.gpsimd.memset(neg_half[:, :], -0.5).then_inc(p0["const"], 1)
            nc.gpsimd.memset(eps[:, 0, :], EPS).then_inc(p0["const"], 1)
            nc.gpsimd.memset(eps[:, 1, :], D * EPS).then_inc(p0["const"], 1)
            nc.gpsimd.memset(nparts[:, :, :], 0.0).then_inc(p0["const"], 1)
            nc.gpsimd.memset(k_bd[:, :, :], 0.0).then_inc(p0["const"], 1)
            nc.gpsimd.memset(v_bd[:, :, :], 0.0).then_inc(p0["const"], 1)
            nc.gpsimd.memset(v_aug[:, :, :, :], 0.0).then_inc(p0["const"], 1)
            pool.wait_ge(p0["const"], 7)
            nc.gpsimd.memset(v_aug[:, :, :, HD:HD + 1], 1.0).then_inc(p0["const"], 1)
            pool.wait_ge(p0["const"], 8)
            nc.gpsimd.memset(k_rep[KREP:KREP + MROWS, :, :], 1.0).then_inc(p0["const"], 1)
            pool.wait_ge(p0["const"], 9)
            pool.wait_ge(p0["w_late"], 16 * 13)
            ntmp = [0]

            def inv_sqrt(dst, src, scale):
                n = src.shape[-1]
                ntmp[0] += 1
                done(nc.gpsimd.tensor_tensor(ve[:, ntmp[0], 0:n], src, eps[:, scale, 0:n], ALU.add), "pool_step")
                return ntmp[0]

            with pool.Fori(0, B, 1) as b:
                def rsqrt(dst, src, scale, name):
                    n = src.shape[-1]
                    k = inv_sqrt(dst, src, scale)
                    need(pool, b, "pool_step", k)
                    done(nc.gpsimd.tensor_tensor(dst, ve[:, k, 0:n], neg_half[:, 0:n], ALU.pow), name)

                need(pool, b, "mv1", 1)
                rsqrt(rs1[:, :], mv1[:, :, 1], 0, "rstd1")
                need(pool, b, "xn1", T)
                done(nc.gpsimd.tensor_tensor(x1[:, :, :], x1[:, :, :], bo_bc[:, :].unsqueeze(1).to_broadcast([P, T, D]), ALU.add), "xb")

                def crossed(t):
                    need(pool, b, "mv2", t + 1)
                    rsqrt(rs2[:, t:t + 1], mv2[:, t, 1:2], 0, "rstd2")

                for t in range(T):
                    need(pool, b, "sc_rec", t + 1)
                    v = s_sb[:, t % 2, :].rearrange("p (h k) -> p h k", h=CH)
                    done(nc.gpsimd.tensor_tensor(v, v, crec[:, t % 2, :].unsqueeze(2).to_broadcast([P, CH, CK]), ALU.mult), "sc_nrm")
                    if t >= 1:
                        crossed(t - 1)
                crossed(T - 1)
                for a in range(4):
                    need(pool, b, "part2", a + 1)
                    done(nc.gpsimd.tensor_tensor(parts[2][:, a, :], rest[:, a % 2, :], parts[1][:, a, :], ALU.subtract), "part3")
                for t in range(T):
                    need(pool, b, "wo_sq", t + 1)
                    rsqrt(ri[:, 0, t:t + 1], ss[:, 0, t:t + 1], 1, "wo_ri")
                    need(pool, b, "wo_n", t + 1)
                    done(nc.gpsimd.tensor_tensor(xn[:, t, :], xn[:, t, :], o_tok[:, t, :], ALU.add), "h")
                need(pool, b, "mo_sq", 1)
                rsqrt(ri[:, 1, :], ss[:, 1, :], 1, "mo_ri")
                for t in range(T):
                    need(pool, b, "mo_y", t + 1)
                    need(pool, b, "h", t + 1)
                    ntmp[0] += 1
                    done(nc.gpsimd.tensor_tensor(x1[:, t, :], x1[:, t, :], xn[:, t, :], ALU.add), "pool_step")
                    need(pool, b, "pool_step", ntmp[0])
                    ntmp[0] += 1
                    done(nc.gpsimd.tensor_tensor(x1[:, t, :], x1[:, t, :], acc[:, t, :], ALU.add), "pool_step")
                    xk = ntmp[0]
                    need(pool, b, "fd_sq", t + 1)
                    rsqrt(ri[:, 2, t:t + 1], ss[:, 2, t:t + 1], 1, "fd_ri")
                    need(pool, b, "fd_n", t + 1)
                    need(pool, b, "pool_step", xk)
                    done(nc.gpsimd.tensor_tensor(x1[:, t, :], x1[:, t, :], o_tok[:, t, :], ALU.add), "y")

        @block.tensor
        def _(pe):
            mm, tr = nc.tensor.matmul, nc.tensor.transpose
            pe.wait_ge(p0["ident"], 8)
            pe.wait_ge(p0["w_early"], 16 * 10)
            blocks = [(ctx_in[:, t, k * P:(k + 1) * P]) for k in range(KD) for t in range(4)]
            blocks += [(wq_c[:, k, a * P:(a + 1) * P]) for k in range(KD) for a in range(PAIRS)]
            for i, src in enumerate(blocks):
                last = tr(bank(i // 4, P, i % 4 * P), src, ident[:, :])
                if i % 4 == 3:
                    last.then_inc(p0["tr_ps"], 1)
            pe.wait_ge(p0["tr_sb"], 6)
            for i in range(2 * PAIRS):
                if i >= 2:
                    pe.wait_ge(p0["kv_sb"], i - 1)
                w = (wk_c, wv_c)[i % 2]
                for k in range(KD):
                    last = mm(bank(6 + i % 2), w[:, k, (i // 2) * P:(i // 2 + 1) * P], ctxT[:, k, :], start=(k == 0), stop=(k == KD - 1))
                last.then_inc(p0["kv_ps"], 1)
            pe.wait_ge(p0["w_late"], 16 * 13)
            pe.wait_ge(p0["const"], 12)
            pe.wait_ge(p0["kv_sb"], 16)
            with pe.Fori(0, B, 1) as b:
                def turn(src, dst_bank, waits, name):
                    for t2 in range(2):
                        if t2 == 0 or True:
                            for w, c in waits(t2):
                                need(pe, b, w, c)
                        for k in range(KD):
                            for t in (2 * t2, 2 * t2 + 1):
                                last = tr(bank(dst_bank[t2], P, (k * 2 + t % 2) * P), src[:, t, k * P:(k + 1) * P], ident[:, :])
                        done(last, name)

                before(pe, b, "fd_n")
                turn(xn, (4, 7), lambda t2: [("xn1", 2 * t2 + 2)], "xT1")
                need(pe, b, "kv_in", 64)
                for i in range(4):
                    k, half = i // 2, i % 2
                    for a in range(4):
                        pa = half * 4 + a
                        last = mm(bank(i, P, a * P), wqT[:, pa, k * P:(k + 1) * P], k_bd[:, pa, :], start=True, stop=True)
                    done(last, "m_ps")
                pe.wait_ge(p0["bq"], b + 1)
                for i in range(2):
                    for a in range(4):
                        pa = i * 4 + a
                        last = mm(bank(5 + i, P, a * P), bq_bc[:, pa, :], k_bd[:, pa, :], start=True, stop=True)
                    done(last, "bqk_ps")
                for i in range(4):
                    need(pe, b, ("m_act", "m_dve")[i % 2], i // 2 + 1)
                    for a in range(2):
                        last = mm(bank(i, D, a * D), v_bd[:, 2 * i + a, :], wo_c[:, 2 * i + a, :], start=True, stop=True)
                    done(last, "vw_ps")

                def cross_scores(t):
                    for half in range(2):
                        i = t % 2 * 2 + half
                        if t < 2:
                            need(pe, b, ("vw_act", "vw_dve")[i % 2], i // 2 + 1)
                        else:
                            need(pe, b, "sc_add", t - 1)
                        for k in range(KD):
                            last = mm(bank(i), xnT[:, k, t * P:(t + 1) * P], m_sb[:, k, half * 512:(half + 1) * 512], start=(k == 0), stop=(k == KD - 1))
                    done(last, "sc_ps")

                def cross_values(t):
                    need(pe, b, "sc_nrm", t + 1)
                    for half in range(2):
                        if t == 0:
                            need(pe, b, "bqk_sb", 2)
                        else:
                            need(pe, b, "pT_sb", 2 * t)
                        for a in range(4):
                            last = tr(bank(5 + half, P, a * P), s_sb[:, t % 2, (half * 4 + a) * P:(half * 4 + a + 1) * P], ident[:, :])
                        done(last, "pT_ps")
                    if t < 2:
                        need(pe, b, "xnT", 2)
                    else:
                        need(pe, b, "x1", t - 1)
                    need(pe, b, "pT_sb", 2 * t + 2)
                    for a in range(PAIRS):
                        last = mm(bank((4, 7)[t % 2], D), pT[:, t % 2, a * P:(a + 1) * P], vw[:, a, :], start=(a == 0), stop=(a == PAIRS - 1))
                    done(last, "pv_ps")

                need(pe, b, "xnT", 2)
                need(pe, b, "m_act", 2)
                need(pe, b, "m_dve", 2)
                need(pe, b, "vw_act", 2)
                need(pe, b, "vw_dve", 2)
                cross_scores(0)
                cross_scores(1)
                for t in range(T):
                    cross_values(t)
                    if t + 2 < T:
                        cross_scores(t + 2)
                turn(xn, (5, 6), lambda t2: [("xn2", 2 * t2 + 2), ("pT_sb", 2 * T)], "xT2")
                need(pe, b, "xn2T", 2)
                need(pe, b, "sc_add", T)
                for a in range(4):
                    w = (wq, wk)[a // 2]
                    for k in range(KD):
                        last = mm(bank(a), w[:, k, a % 2 * P:(a % 2 + 1) * P], xn2T[:, k, :], start=(k == 0), stop=(k == KD - 1))
                    done(last, "qk_ps")
                for t in range(T):
                    if t >= 2:
                        need(pe, b, "v_sb", t - 1)
                        need(pe, b, "lg", t - 1)
                    for k in range(KD):
                        last = mm(bank(5 + t % 2, D + E), xn2T[:, k, t * P:(t + 1) * P], wv[:, k, :], start=(k == 0), stop=(k == KD - 1))
                    done(last, "v_ps")
                need(pe, b, "rest1", 4)
                need(pe, b, "part1", 4)
                need(pe, b, "v_sb", T)
                need(pe, b, "lg", T)
                need(pe, b, "x1", T)
                nmax = 0
                for step in STEPS:
                    if step[0] == "max":
                        hp = step[1]
                        if hp == 0:
                            need(pe, b, "rep_q", per["rep_q"])
                            need(pe, b, "rep_k", per["rep_k"])
                        for t in range(T):
                            if nmax >= 2:
                                need(pe, b, "a_max", nmax - 1)
                            n = (t + 1) * P
                            for i in range(2):
                                h, o = 2 * hp + i, nmax % 2 * 2 + i
                                mm(bank(o, n), q_rep[0:KREP, h, t * P:n], k_rep[0:KREP, h, 0:n], start=True, stop=False)
                                last = mm(bank(o, P, t * P), ident_b[:, :], mask_qk[:, :], start=False, stop=True)
                            done(last, "a_ps")
                            nmax += 1
                    elif step[0] == "shift":
                        need(pe, b, "m_part", 1)
                        psb = bank(4, 256).bitcast(BF16)
                        for t in range(T):
                            last = tr(psb[:, t * P:(t + 1) * P], nparts[:, t, :], ident_b[:, :])
                        done(last, "mT_ps")
                    elif step[0] == "score":
                        g, u = step[1:]
                        n = g * 5 + u
                        if n == 0:
                            need(pe, b, "m_row", per["m_row"])
                            need(pe, b, "a_max", 32)
                        if n >= 2:
                            need(pe, b, "b_exp", n - 1)
                        for j in range(4):
                            for kb, at, w in score_segments(j):
                                if at // 1024 != u:
                                    continue
                                o = n % 2 * 1024 + at % 1024
                                mm(ps[:, o:o + w], k_rep[0:KREP + MROWS, 4 * g + j, kb * P:(kb + 1) * P],
                                   q_rep[0:KREP + MROWS, 4 * g + j, kb * P:S], start=True, stop=False, skip_group_check=True)
                                last = mm(ps[:, o:o + P], ident_b[:, :], mask_kq[:, :], start=False, stop=True, skip_group_check=True)
                        done(last, "b_ps")
                    elif step[0] == "value":
                        g = step[1]
                        need(pe, b, "b_exp", 5 * g + 5)
                        if g == 0:
                            need(pe, b, "mT_sb", 1)
                        else:
                            need(pe, b, "o_nrm", g)
                        for kb in range(T):
                            for j in range(4):
                                at = [a for k, a, _ in score_segments(j) if k == kb][0]
                                w = S - kb * P
                                last = mm(ps[32 * j:32 * j + 32, 4 * 512 + kb * P:5 * 512], v_aug[:, kb, 4 * g + j, :],
                                          prob[:, g % 2, at:at + w], start=(kb == 0), stop=(kb == T - 1),
                                          skip_group_check=True, tile_position=(0, 32 * j))
                        done(last, "av_ps")
                    elif step[0] == "out_t":
                        g = step[1]
                        need(pe, b, "av_sb", g + 1)
                        for t in range(T):
                            last = tr(bank(4, P, t * P), av[:, t * P:(t + 1) * P], ident[:, :])
                        done(last, "avT_ps")
                    elif step[0] == "up":
                        e, m = step[1:]
                        n = e * EB + m
                        if m == 0:
                            pe.wait_ge(e_in[e % 2], b * (16 * 3 * E // 2) + 48 * (e // 2 + 1))
                        if n >= 1:
                            need(pe, b, "mu_g", n)
                        for i in range(2):
                            for k in range(KD):
                                last = mm(bank(5 + i), ew[:, e % 2, i, k, m * P:(m + 1) * P], xn2T[:, k, :], start=(k == 0), stop=(k == KD - 1))
                        done(last, "mu_ps")
                    elif step[0] == "down":
                        e, t2 = step[1:]
                        n = 2 * e + t2
                        need(pe, b, "mu_g", e * EB + EB)
                        if n >= 1:
                            need(pe, b, "md_acc", n)
                        for t in (2 * t2, 2 * t2 + 1):
                            for m in range(EB):
                                last = mm(bank(7, D, t % 2 * D), mg[:, e % 2, m, t * P:(t + 1) * P], ew[:, e % 2, 2, m, :], start=(m == 0), stop=(m == EB - 1))
                        done(last, "md_ps")
                need(pe, b, "b_exp", 20)
                turn(o_tok, (0, 1), lambda t2: [("o_nrm", G)], "oT_ps")
                for t in range(T):
                    need(pe, b, "oT_sb", 2 if t >= 2 else 1)
                    if t >= 2:
                        need(pe, b, "wo_n", t - 1)
                    for k in range(KD):
                        last = mm(bank(2 + t % 2, D), oT[:, k, t * P:(t + 1) * P], wo[:, k, :], start=(k == 0), stop=(k == KD - 1))
                    done(last, "wo_ps")
                turn(xn, (4, 7), lambda t2: [("h", 2 * t2 + 2), ("md_acc", 16)], "hT_ps")
                need(pe, b, "hT_sb", 2)
                need(pe, b, "mu_g", E * EB)
                need(pe, b, "wo_n", T)
                for m in range(FB):
                    base = (5, 0)[m % 2]
                    if m >= 2:
                        need(pe, b, "fu_g", m - 1)
                    for i, w in enumerate((w1, w3)):
                        for k in range(KD):
                            last = mm(bank(base + i), w[:, k, m * P:(m + 1) * P], hT[:, k, :], start=(k == 0), stop=(k == KD - 1))
                    done(last, "fu_ps")
                need(pe, b, "fu_g", FB)
                for t in range(T):
                    if t >= 2:
                        need(pe, b, "fd_n", t - 1)
                    for m in range(FB):
                        last = mm(bank(2 + t % 2, D), gT[:, m, t * P:(t + 1) * P], w2[:, m, :], start=(m == 0), stop=(m == FB - 1))
                    done(last, "fd_ps")

        @block.scalar
        def _(act):
            fn = nc.scalar.activation
            for i in range(6):
                act.wait_ge(p0["tr_ps"], i + 1)
                src = bank(i)
                if i < 2:
                    fn(ctxT[:, i, :], src, ACT.Copy).then_inc(p0["tr_sb"], 1)
                else:
                    k, a0 = (i - 2) // 2, (i - 2) % 2 * 4
                    fn(wqT[:, a0:a0 + 4, k * P:(k + 1) * P], src.rearrange("p (a n) -> p a n", a=4), ACT.Copy).then_inc(p0["tr_sb"], 1)
            for i in range(2 * PAIRS):
                act.wait_ge(p0["kv_ps"], i + 1)
                if i == 0:
                    act.wait_ge(p0["bk"], 1)
                if i >= 4:
                    act.wait_ge(kv_out[i % 4], 16 * (i // 4))
                if i % 2 == 0:
                    fn(kv_st[:, i % 4, :], bank(6 + i % 2), ACT.Identity, bias=bk[:, i // 2:i // 2 + 1], scale=CHD ** -0.5).then_inc(p0["kv_sb"], 1)
                else:
                    fn(kv_st[:, i % 4, :], bank(6 + i % 2), ACT.Identity, bias=bv[:, i // 2:i // 2 + 1]).then_inc(p0["kv_sb"], 1)
            act.wait_ge(p0["kv_sb"], 16)
            for i in range(4):
                act.wait_ge(kv_out[i], 16 * 2 * PAIRS // 4)
            with act.Fori(0, B, 1) as b:
                def spread(dst, banks, src_name, name):
                    for t2 in range(2):
                        need(act, b, src_name, t2 + 1)
                        done(fn(dst[:, :, t2 * 2 * P:(t2 + 1) * 2 * P], bank(banks[t2]).rearrange("p (k n) -> p k n", k=KD), ACT.Copy), name)

                def load_expert(e):
                    if e >= 2:
                        need(act, b, "md_ps", 2 * (e - 2) + 2)
                    elif e >= 0:
                        before(act, b, "md_ps")
                    for i, w in enumerate(("L0_ffn_ew1", "L0_ffn_ew3", "L0_ffn_ew2")):
                        act.dma_start(ew[:, e % 2, i, :, :], A[w][e, :, :].rearrange("(k p) n -> p k n", p=P)).then_inc(e_in[e % 2], 16)

                load_expert(0)
                load_expert(1)
                spread(xnT, (4, 7), "xT1", "xnT")
                for i in (0, 2):
                    need(act, b, "m_ps", i + 1)
                    if i == 0:
                        before(act, b, "av_ps")
                    k, half = i // 2, i % 2
                    done(fn(m_sb[:, k, 0:512], bank(i), ACT.Copy), "m_act")
                for i in range(2):
                    need(act, b, "bqk_ps", i + 1)
                    done(fn(bqk[:, i * 512:(i + 1) * 512], bank(5 + i), ACT.Copy), "bqk_sb")
                for i in (0, 2):
                    need(act, b, "vw_ps", i + 1)
                    done(fn(vw[:, 2 * i:2 * i + 2, :], bank(i).rearrange("p (a n) -> p a n", a=2), ACT.Copy), "vw_act")

                def cross_exp(t):
                    need(act, b, "sc_sub", t + 1)
                    done(fn(s_sb[:, t % 2, :], s_sb[:, t % 2, :], ACT.Exp), "sc_exp")

                cross_exp(0)
                for t in range(T):
                    if t + 1 < T:
                        cross_exp(t + 1)
                    for half in range(2):
                        need(act, b, "pT_ps", 2 * t + half + 1)
                        if t >= 2:
                            need(act, b, "pv_ps", t - 1)
                        done(fn(pT[:, t % 2, half * 512:(half + 1) * 512], bank(5 + half), ACT.Copy), "pT_sb")
                spread(xn2T, (5, 6), "xT2", "xn2T")
                for a in range(4):
                    need(act, b, "qk_ps", a + 1)
                    done(fn(parts[0][:, a, :], bank(a), ACT.Copy, scale=(HD ** -0.5 if a < 2 else 1.0)), "part1")
                    if a >= 1:
                        need(act, b, "rest1", a)
                        done(fn(parts[1][:, a - 1, :], rest[:, (a - 1) % 2, :], ACT.Copy), "part2")
                need(act, b, "rest1", 4)
                done(fn(parts[1][:, 3, :], rest[:, 1, :], ACT.Copy), "part2")
                for t in range(T):
                    need(act, b, "lg", t + 1)
                    done(fn(v_aug[:, t, :, 0:HD], bank(5 + t % 2, D).rearrange("p (h d) -> p h d", h=H), ACT.Copy), "v_sb")
                need(act, b, "gmax", 1)
                done(fn(g_b[:, :, :], g_a[:, :, :], ACT.Exp), "gexp")
                for step in STEPS:
                    if step[0] == "score":
                        g, u = step[1:]
                        n = g * 5 + u
                        need(act, b, "b_ps", n + 1)
                        if u == 0 and g >= 2:
                            need(act, b, "av_ps", g - 1)
                        done(fn(prob[:, g % 2, u * 1024:(u + 1) * 1024], ps[:, n % 2 * 1024:n % 2 * 1024 + 1024], ACT.Exp), "b_exp")
                    elif step[0] == "value":
                        g = step[1]
                        need(act, b, "av_ps", g + 1)
                        if g >= 1:
                            need(act, b, "avT_ps", g)
                        done(fn(av[:, :], bank(4), ACT.Copy), "av_sb")
                    elif step[0] == "up":
                        e, m = step[1:]
                        n = e * EB + m
                        need(act, b, "mu_ps", n + 1)
                        if n >= 2:
                            need(act, b, "mu_u", n - 1)
                        done(fn(th[:, n % 2, :], bank(5), ACT.Tanh, scale=0.5), "mu_th")
                    elif step[0] == "down":
                        e, t2 = step[1:]
                        if t2 == 1 and e + 2 < E:
                            load_expert(e + 2)
                spread(oT, (0, 1), "oT_ps", "oT_sb")
                need(act, b, "md_acc", 16)
                for t in range(T):
                    last = fn(squares[:, t, :], acc[:, t, :], ACT.Square, accum_out=ss[:, 1, t:t + 1])
                done(last, "mo_sq")
                need(act, b, "mo_sq", 1)
                for t in range(T):
                    need(act, b, "wo_ps", t + 1)
                    done(fn(squares[:, t, :], bank(2 + t % 2, D), ACT.Square, accum_out=ss[:, 0, t:t + 1]), "wo_sq")
                spread(hT, (4, 7), "hT_ps", "hT_sb")
                for m in range(FB):
                    need(act, b, "fu_ps", m + 1)
                    if m >= 2:
                        need(act, b, "fu_u", m - 1)
                    done(fn(th[:, m % 2, :], bank((5, 0)[m % 2]), ACT.Tanh, scale=0.5), "fu_th")
                need(act, b, "fu_u", FB)
                for t in range(T):
                    need(act, b, "fd_ps", t + 1)
                    done(fn(squares[:, t, :], bank(2 + t % 2, D), ACT.Square, accum_out=ss[:, 2, t:t + 1]), "fd_sq")

        @block.vector
        def _(dve):
            v = nc.vector
            dve.wait_ge(p0["w_early"], 16 * 10)
            v.tensor_scalar(bk[:, :], bk[:, :], CHD ** -0.5, None, ALU.mult).then_inc(p0["bk"], 1)
            dve.wait_ge(p0["w_late"], 16 * 13)
            dve.wait_ge(p0["const"], 9)
            for w in (aw_bc, fw_bc, mw_bc):
                v.tensor_scalar(w[:, :], w[:, :], float(D) ** 0.5, None, ALU.mult).then_inc(p0["const"], 1)
            dve.wait_ge(p0["const"], 12)
            for i in range(4):
                dve.wait_ge(kv_out[i], 16 * 2 * PAIRS // 4)
            with dve.Fori(0, B, 1) as b:
                before(dve, b, "av_ps")
                v.tensor_copy(bq_bc, bq[:, :].unsqueeze(2).to_broadcast([P, PAIRS, P])).then_inc(p0["bq"], 1)
                need(dve, b, "x_in", 16)
                for t in range(T):
                    last = v.bn_stats(st1[:, t, :], x1[:, t, :])
                done(last, "stats")
                need(dve, b, "stats", 1)
                carry_wait()
                for t in range(T):
                    last = v.bn_aggr(mv1[:, t, :], st1[:, t, :])
                done(last, "mv1")
                need(dve, b, "rstd1", 1)
                need(dve, b, "mv1", 1)
                before(dve, b, "y")
                for t in range(T):
                    done(v.tensor_scalar(xn[:, t, :], x1[:, t, :], mv1[:, t, 0:1], rs1[:, t:t + 1], ALU.subtract, ALU.mult), "xn1")
                for i in (1, 3):
                    need(dve, b, "m_ps", i + 1)
                    done(v.tensor_copy(m_sb[:, i // 2, 512:1024], bank(i)), "m_dve")
                for i in (1, 3):
                    need(dve, b, "vw_ps", i + 1)
                    done(v.tensor_copy(vw[:, 2 * i:2 * i + 2, :], bank(i).rearrange("p (a n) -> p a n", a=2)), "vw_dve")

                def cross_shift(t):
                    need(dve, b, "sc_ps", t + 1)
                    if t == 0:
                        need(dve, b, "bqk_sb", 2)
                    if t >= 2:
                        need(dve, b, "pT_ps", 2 * (t - 2) + 2)
                    s3 = s_sb[:, t % 2, :].rearrange("p (h k) -> p h k", h=CH)
                    done(v.tensor_tensor(s_sb[:, t % 2, :], ps[:, t % 2 * 1024:t % 2 * 1024 + 1024], bqk, ALU.add), "sc_add")
                    need(dve, b, "sc_add", t + 1)
                    done(v.tensor_reduce(cmax[:, t % 2, :], s3, AX.X, ALU.max), "sc_max")
                    need(dve, b, "sc_max", t + 1)
                    done(v.tensor_tensor(s3, s3, cmax[:, t % 2, :].unsqueeze(2).to_broadcast([P, CH, CK]), ALU.subtract), "sc_sub")

                def cross_sum(t):
                    need(dve, b, "sc_exp", t + 1)
                    if t >= 2:
                        need(dve, b, "sc_nrm", t - 1)
                    s3 = s_sb[:, t % 2, :].rearrange("p (h k) -> p h k", h=CH)
                    done(v.tensor_reduce(csum[:, t % 2, :], s3, AX.X, ALU.add), "sc_sum")
                    need(dve, b, "sc_sum", t + 1)
                    done(v.reciprocal(crec[:, t % 2, :], csum[:, t % 2, :]), "sc_rec")

                def crossed(t):
                    need(dve, b, "pv_ps", t + 1)
                    need(dve, b, "xb", 1)
                    done(v.tensor_tensor(x1[:, t, :], x1[:, t, :], bank((4, 7)[t % 2], D), ALU.add), "x1")
                    need(dve, b, "x1", t + 1)
                    done(v.bn_stats(st2[:, t, :], x1[:, t, :]), "stats")
                    need(dve, b, "stats", 2 + t)
                    carry_wait()
                    done(v.bn_aggr(mv2[:, t, :], st2[:, t, :]), "mv2")

                def normed(t):
                    need(dve, b, "rstd2", t + 1)
                    need(dve, b, "mv2", t + 1)
                    need(dve, b, "xT1", 2)
                    done(v.tensor_scalar(xn[:, t, :], x1[:, t, :], mv2[:, t, 0:1], rs2[:, t:t + 1], ALU.subtract, ALU.mult), "xn2")

                cross_shift(0)
                cross_shift(1)
                cross_sum(0)
                for t in range(T):
                    if t + 1 < T:
                        cross_sum(t + 1)
                    if t + 2 < T:
                        cross_shift(t + 2)
                    crossed(t)
                    if t >= 1:
                        normed(t - 1)
                normed(T - 1)
                for a in range(4):
                    need(dve, b, "part1", a + 1)
                    if a >= 2:
                        need(dve, b, "part3", a - 1)
                    done(v.scalar_tensor_tensor(rest[:, a % 2, :], bank(a), (HD ** -0.5 if a < 2 else 1.0), parts[0][:, a, :], ALU.mult, ALU.subtract), "rest1")
                for t in range(T):
                    need(dve, b, "v_ps", t + 1)
                    done(v.tensor_copy(lg[:, t, :], bank(5 + t % 2, E, D)), "lg")
                need(dve, b, "lg", T)
                c = [0]

                def link(ins):
                    c[0] += 1
                    done(ins, "dve_step")
                    need(dve, b, "dve_step", c[0])

                link(v.tensor_reduce(g1[:, :], lg[:, :, :], AX.X, ALU.max))
                done(v.tensor_tensor(g_a[:, :, :], lg[:, :, :], g1[:, :].unsqueeze(2).to_broadcast([P, T, E]), ALU.subtract), "gmax")
                need(dve, b, "gexp", 1)
                link(v.tensor_reduce(g1[:, :], g_b[:, :, :], AX.X, ALU.add))
                link(v.reciprocal(g2[:, :], g1[:, :]))
                link(v.tensor_tensor(g_a[:, :, :], g_b[:, :, :], g2[:, :].unsqueeze(2).to_broadcast([P, T, E]), ALU.mult))
                carry_wait()
                for t in range(T):
                    last = v.max(g_s[:, t, :], g_a[:, t, :])
                link(last)
                link(v.memset(g_s[:, :, 2:8], -1.0))
                carry_wait()
                for t in range(T):
                    last = v.match_replace(g_b[:, t, :], g_s[:, t, :], g_a[:, t, :], 2.0)
                link(last)
                link(v.tensor_scalar(g_b[:, :, :], g_b[:, :, :], 2.0, None, ALU.is_equal))
                done(v.tensor_tensor(gate[:, :, :], g_a[:, :, :], g_b[:, :, :], ALU.mult), "gate")
                need(dve, b, "gate", 1)
                nmax = 0
                for step in STEPS:
                    if step[0] == "max":
                        hp = step[1]
                        for t in range(T):
                            need(dve, b, "a_ps", nmax + 1)
                            o = nmax % 2 * 1024
                            done(v.tensor_reduce(nm[:, t, 2 * hp:2 * hp + 2], ps[:, o:o + 1024].rearrange("p (i n) -> p i n", i=2)[:, :, 0:(t + 1) * P],
                                                 AX.X, ALU.max, negate=True), "a_max")
                            nmax += 1
                    elif step[0] == "shift":
                        need(dve, b, "a_max", 32)
                        link(v.tensor_copy(npart[:, :, 0, :], nm[:, :, :]))
                        link(v.tensor_tensor(nr[:, :, :], nm[:, :, :], npart[:, :, 0, :], ALU.subtract))
                        link(v.tensor_copy(npart[:, :, 1, :], nr[:, :, :]))
                        done(v.tensor_tensor(npart[:, :, 2, :], nr[:, :, :], npart[:, :, 1, :], ALU.subtract), "m_part")
                        need(dve, b, "mT_ps", 1)
                        done(v.tensor_copy(mT[:, :], bank(4, 256).bitcast(BF16)[0:MROWS * H, :]), "mT_sb")
                    elif step[0] == "out_t":
                        g = step[1]
                        need(dve, b, "avT_ps", g + 1)
                        t4 = bank(4).rearrange("p (t j c) -> p t j c", t=T, j=4)
                        done(v.reciprocal(orec[:, :, :], t4[:, :, :, HD]), "o_rec")
                        need(dve, b, "o_rec", g + 1)
                        done(v.tensor_tensor(o_tok[:, :, g * 64:(g + 1) * 64].rearrange("p t (j d) -> p t j d", j=4), t4[:, :, :, 0:HD],
                                             orec[:, :, :].unsqueeze(3).to_broadcast([P, T, 4, HD]), ALU.mult), "o_nrm")
                    elif step[0] == "up":
                        e, m = step[1:]
                        n = e * EB + m
                        need(dve, b, "mu_th", n + 1)
                        done(v.scalar_tensor_tensor(uu[:, n % 2, :], th[:, n % 2, :], 1.0, bank(5), ALU.add, ALU.mult), "mu_u")
                        need(dve, b, "mu_u", n + 1)
                        if e >= 2 and m == 0:
                            need(dve, b, "md_ps", 2 * (e - 2) + 2)
                        done(v.scalar_tensor_tensor(mg[:, e % 2, m, :], uu[:, n % 2, :], 0.5, bank(6), ALU.mult, ALU.mult), "mu_g")
                    elif step[0] == "down":
                        e, t2 = step[1:]
                        n = 2 * e + t2
                        need(dve, b, "md_ps", n + 1)
                        if e >= 1:
                            need(dve, b, "md_acc", n - 1)
                        for t in (2 * t2, 2 * t2 + 1):
                            o = bank(7, D, t % 2 * D)
                            if e == 0:
                                last = v.tensor_scalar(acc[:, t, :], o, gate[:, t, e:e + 1], None, ALU.mult)
                            else:
                                last = v.scalar_tensor_tensor(acc[:, t, :], o, gate[:, t, e:e + 1], acc[:, t, :], ALU.mult, ALU.add)
                        done(last, "md_acc")
                for t in range(T):
                    need(dve, b, "wo_ri", t + 1)
                    need(dve, b, "oT_ps", 2)
                    done(v.scalar_tensor_tensor(o_tok[:, t, :], bank(2 + t % 2, D), ri[:, 0, t:t + 1], aw_bc[:, :], ALU.mult, ALU.mult), "wo_n")
                need(dve, b, "mo_ri", 1)
                for t in range(T):
                    done(v.scalar_tensor_tensor(acc[:, t, :], acc[:, t, :], ri[:, 1, t:t + 1], mw_bc[:, :], ALU.mult, ALU.mult), "mo_y")
                for m in range(FB):
                    base = (5, 0)[m % 2]
                    need(dve, b, "fu_th", m + 1)
                    done(v.scalar_tensor_tensor(uu[:, m % 2, :], th[:, m % 2, :], 1.0, bank(base), ALU.add, ALU.mult), "fu_u")
                    need(dve, b, "fu_u", m + 1)
                    done(v.scalar_tensor_tensor(gT[:, m, :], uu[:, m % 2, :], 0.5, bank(base + 1), ALU.mult, ALU.mult), "fu_g")
                for t in range(T):
                    need(dve, b, "fd_ri", t + 1)
                    need(dve, b, "h", t + 1)
                    done(v.scalar_tensor_tensor(o_tok[:, t, :], bank(2 + t % 2, D), ri[:, 2, t:t + 1], fw_bc[:, :], ALU.mult, ALU.mult), "fd_n")

        assert counted == per, [(n, counted.get(n), per[n]) for n in per if counted.get(n) != per[n]]


_INS = ['x', 'ctx_1024', 'L0_xattn_Wq', 'L0_xattn_bq', 'L0_xattn_Wk', 'L0_xattn_bk', 'L0_xattn_Wv', 'L0_xattn_bv',
        'L0_xattn_Wo', 'L0_xattn_bo', 'L0_ffn_wq', 'L0_ffn_wk', 'L0_ffn_wv', 'L0_ffn_wo', 'L0_ffn_w1', 'L0_ffn_w2',
        'L0_ffn_w3', 'L0_ffn_attn_norm_w', 'L0_ffn_ff_norm_w', 'L0_ffn_moe_norm_w', 'L0_ffn_router_w', 'L0_ffn_ew1',
        'L0_ffn_ew2', 'L0_ffn_ew3']


def kernel(**inputs):
    import numpy as np
    import concourse.bacc as bacc
    from concourse.bass_utils import run_bass_kernel_spmd

    nc = bacc.Bacc("TRN2", target_bir_lowering=False, num_devices=1, dynamic_dma_scratch_size=4096)
    arrays, args = {}, {}
    for name in _INS:
        a = np.ascontiguousarray(inputs[name])
        arrays[f"in_{name}"] = a
        args[name] = nc.dram_tensor(f"in_{name}", a.shape, mybir.dt.from_np(a.dtype), kind="ExternalInput").ap()
    out = nc.dram_tensor("out_x", (B, S, D), F32, kind="ExternalOutput").ap()
    xattn_ffn(nc, args, out)
    r = run_bass_kernel_spmd(nc, [arrays], core_ids=[0])
    return r.results[0]["out_x"]
```

```python
from contextlib import ExitStack

import concourse.bass as bass
from concourse import mybir

ALU = mybir.AluOpType
ACT = mybir.ActivationFunctionType
AX = mybir.AxisListType
F32 = mybir.dt.float32
BF16 = mybir.dt.bfloat16

P = 128
B, S, D = 8, 512, 256
T = S // P
KD = D // P
CH, CHD, CK = 16, 64, 64
PAIRS = CH // 2
H, HD = 16, 16
HB = P // HD
NREP = 6
KREP = NREP * HD
MROWS = 3
G = H // 4
FF = 1024
FB = FF // P
E, EH = 8, 256
EB = EH // P
EPS = 1e-5
REG = S * B + P
MT = 2 * S * B // P + E
EW = (2 * KD + EB) * D
MASKED = -1e30
Q_PART = (0, 0, 1, 1, 0, 2)
K_PART = (0, 1, 0, 1, 2, 0)

PER = dict(
    x_in=16, kv_in=64, stats=5, mv1=1, rstd1=1, xn1=1, xT1=2, xnT=2, bq=1,
    m_ps=4, m_act=2, m_dve=2, bqk_ps=2, bqk_sb=2, vw_ps=4, vw_sb=4,
    sc_ps=4, sc_add=4, sc_max=4, sc_sub=4, sc_exp=4, sc_sum=4, sc_rec=4, sc_nrm=4,
    pT_ps=8, pT_sb=8, pv_ps=4, xb=1, x1=4, mv2=4, rstd2=4, xn2=4, xT2=2, xn2T=2,
    qk_ps=4, part1=4, rest1=4, part2=4, part3=4, v_ps=4, v_sb=4, lg=4,
    q_out=96, k_out=96, rep_q=96, rep_k=96,
    gmax=1, gexp=1, mask=1, rank_ps=1, slot=1, slot_copy=1, scat=128, dve_step=33, pool_a=5,
    a_ps=32, a_max=32, m_part=2, mT_ps=2, mT_sb=2, m_row=96,
    b_ps=20, b_exp=20, av_ps=4, av_sb=4, avT_ps=4, o_rec=4, o_nrm=4,
    oT_ps=2, oT_sb=2, wo_ps=2, wo_sq=2, wo_ri=1, wo_n=2, h=1, yb=1, hT_ps=2, hT_sb=2,
    fu_ps=8, fu_th=8, fu_u=8, fu_g=8, fd_ps=8, fd_sq=1, fd_ri=1, fd_n=1, y=1, y_out=16, pool_f=2,
)
AHEAD = dict(fd_n=1, fd_ps=1, y=1, y_out=16)

STEPS = [
    ("x_norm",), ("x_turn",), ("f_out_t", G - 1), ("m_build",), ("bqk",), ("f_o_turn",),
    ("cs", 0), ("vw",), ("exp", 0), ("f_wo",), ("sum", 0), ("f_o_norm",), ("x_bias",), ("cs", 1), ("exp", 1), ("sum", 1),
    ("ct", 0), ("cs", 2), ("f_h_turn",), ("exp", 2), ("cv", 0), ("fu", 0), ("sum", 2), ("ct", 1), ("cs", 3), ("exp", 3),
    ("cv", 1), ("sum", 3), ("fu", 1), ("ct", 2), ("fd", 0), ("cv", 2), ("ct", 3), ("fd", 1), ("cv", 3), ("norm_3",),
    ("fu", 2), ("x2_turn",), ("qk",), ("v",), ("route",), ("fu", 3), ("fd", 2), ("slots",), ("fu", 4), ("fd", 3), ("fd", 4),
    ("max", 0), ("max", 1), ("fu", 5), ("max", 2), ("max", 3), ("shift_parts", 0), ("fd", 5), ("max", 4), ("shift", 0),
    ("fu", 6), ("max", 5), ("fd", 6), ("max", 6), ("fu", 7), ("max", 7), ("shift_parts", 1), ("fd", 7), ("f_end",),
]
for _g in range(G):
    STEPS += [("score", _g, 0), ("score", _g, 1)]
    STEPS += [("value", _g - 1)] if _g else [("shift", 1)]
    STEPS += [("score", _g, 2), ("score", _g, 3)]
    if _g:
        STEPS += [("out_t", _g - 1)]
    STEPS += [("score", _g, 4)]
STEPS += [("value", G - 1)]


def steps_of(attention, net):
    if attention:
        return [s for s in STEPS if net or s[0][0] != "f"]
    order = [("f_out_t", G - 1), ("f_o_turn",), ("f_wo",), ("f_o_norm",), ("f_h_turn",), ("fu", 0)]
    for m in range(FB):
        order += ([("fu", m + 1)] if m + 1 < FB else []) + [("fd", m)]
    return order + [("f_end",)]


def up_banks(b, m):
    return (0, 1) if b is None and m % 2 else (5, 6)


def score_segments(j):
    order = (0, 1, 3, 2) if j % 2 == 0 else (2, 0, 1, 3)
    at = j * 1280
    found = []
    for kb in order:
        n = S - kb * P
        found.append((kb, at, n))
        at += n
    return found


def xattn_ffn(nc, A, out):
    per = PER
    counted = {}
    with ExitStack() as ctx:
        def sb(name, shape, dt=F32):
            return ctx.enter_context(nc.sbuf_tensor(name, shape, dt))

        def sem(name):
            return ctx.enter_context(nc.semaphore(name))

        reps_free = sem("reps_free")

        sems = {n: sem(n) for n in per}
        kv_out = [sem(f"p0_kv_out{i}") for i in range(4)]
        p0 = {n: sem("p0_" + n) for n in ("w_early", "w_mid", "w_late", "norms", "ident", "const", "iota", "tr_ps", "tr_sb", "kv_ps", "kv_sb", "bk")}
        moe = {n: sem("moe_" + n) for n in ("table_step", "table", "ew_in", "zero", "xs_free", "xT_ps", "xT", "up_ps", "th", "u", "g", "gT_ps", "gT", "dn_ps", "eo")}
        xs_in = [sem(f"xs_in{i}") for i in range(4)]
        eo_out = [sem(f"eo_out{i}") for i in range(4)]
        fin = {n: sem("fin_" + n) for n in ("idx", "gates", "mix", "sum", "sq", "eps", "ri", "scaled", "y", "y_free")}
        got = [sem(f"got{i}") for i in range(2)]
        y_in = [sem(f"y_in{i}") for i in range(2)]
        o_out = [sem(f"o_out{i}") for i in range(2)]

        wo_c = sb("wo_c", [P, PAIRS, D])
        wqT = sb("wqT", [P, PAIRS, D])
        wq = sb("wq", [P, KD, D])
        wk = sb("wk", [P, KD, D])
        wv = sb("wv", [P, KD, D + E])
        wo = sb("wo", [P, KD, D])
        w1 = sb("w1", [P, KD, FF])
        w3 = sb("w3", [P, KD, FF])
        w2 = sb("w2", [P, FB, D])
        bq = sb("bq", [P, PAIRS])
        bk = sb("bk", [P, PAIRS])
        bv = sb("bv", [P, PAIRS])
        bo_bc = sb("bo_bc", [P, D])
        aw_bc = sb("aw_bc", [P, D])
        fw_bc = sb("fw_bc", [P, D])
        mw_bc = sb("mw_bc", [P, D])
        ident = sb("ident", [P, P])
        ident_b = sb("ident_b", [P, P], BF16)
        mask_qk = sb("mask_qk", [P, P], BF16)
        mask_kq = sb("mask_kq", [P, P], BF16)
        before_b = sb("before_b", [P, P], BF16)
        ones_b = sb("ones_b", [P, P], BF16)
        neg_half = sb("neg_half", [P, T])
        eps = sb("eps", [P, 2, T])
        spare = sb("spare", [P, 1])
        spare_p = sb("spare_p", [P, 1])
        e_less = sb("e_less", [P, E])
        e_row = sb("e_row", [P, E])
        tile_at = sb("tile_at", [P, S * B // P])
        tile_no = sb("tile_no", [P, MT])
        iotas = sb("iotas", [P, 2 * E + S * B // P + MT], mybir.dt.int32)
        zeros = sb("zeros", [P, D])

        k_bd = sb("k_bd", [P, PAIRS, P])
        v_bd = sb("v_bd", [P, PAIRS, P])
        room = sb("room", [P, 2 * 5120 + 2 * H * S // 2])
        big = room[:, 0:2 * 5120]
        q_rep = room[:, 10240:10240 + 4096].bitcast(BF16).rearrange("p (h n) -> p h n", h=H)
        k_rep = room[:, 14336:14336 + 4096].bitcast(BF16).rearrange("p (h n) -> p h n", h=H)

        def part(a, n):
            return room[:, a:a + n]

        m_sb = part(0, 2048).rearrange("p (k n) -> p k n", k=KD)
        vw = part(2048, 2048).rearrange("p (a n) -> p a n", a=PAIRS)
        bqk = part(4096, 1024)
        s_sb = part(5120, 2048).rearrange("p (i n) -> p i n", i=2)
        pT = part(7168, 2048).rearrange("p (i n) -> p i n", i=2)
        bq_bc = part(9216, 1024).rearrange("p (a n) -> p a n", a=PAIRS)
        prob = big.rearrange("p (i n) -> p i n", i=2)
        wq_c = part(0, 2048).rearrange("p (k n) -> p k n", k=KD)
        wk_c = part(2048, 2048).rearrange("p (k n) -> p k n", k=KD)
        wv_c = part(4096, 2048).rearrange("p (k n) -> p k n", k=KD)
        ctx_in = part(6144, 1024).rearrange("p (t n) -> p t n", t=4)
        ctxT = part(7168, 1024).rearrange("p (k n) -> p k n", k=KD)
        kv_st = part(8192, 2048).rearrange("p (i n) -> p i n", i=4)
        ew = part(0, E * EW)
        base2 = E * EW
        xs = part(base2, 4 * D).rearrange("p (i n) -> p i n", i=4)
        xsT = part(base2 + 1024, 2 * D).rearrange("p (i n) -> p i n", i=2)
        e_th = part(base2 + 1536, 2 * D).rearrange("p (i n) -> p i n", i=2)
        e_uu = part(base2 + 2048, 2 * D).rearrange("p (i n) -> p i n", i=2)
        e_g = part(base2 + 2560, 2 * D).rearrange("p (i n) -> p i n", i=2)
        e_gT = part(base2 + 3072, 2 * D).rearrange("p (i n) -> p i n", i=2)
        eo = part(base2 + 3584, 4 * D).rearrange("p (i n) -> p i n", i=4)

        xin = sb("xin", [P, T, D])
        xh = sb("xh", [P, T, D])
        x1 = sb("x1", [P, T, D])
        xn = sb("xn", [P, T, D])
        yb = sb("yb", [P, T, D])
        xnT = sb("xnT", [P, KD, S])
        xn2T = sb("xn2T", [P, KD, S])
        hT = sb("hT", [P, KD, S])
        o_tok = sb("o_tok", [P, T, D])
        oT = sb("oT", [P, KD, S])
        parts = [xnT[:, :, :].rearrange("p k n -> p (k n)").bitcast(BF16).rearrange("p (a n) -> p a n", a=4),
                 o_tok[:, :, :].rearrange("p t n -> p (t n)").bitcast(BF16).rearrange("p (a n) -> p a n", a=4),
                 oT[:, :, :].rearrange("p k n -> p (k n)").bitcast(BF16).rearrange("p (a n) -> p a n", a=4)]
        rest = sb("rest", [P, 2, S])
        v_aug = sb("v_aug", [P, T, H, 32])
        gT = sb("gT", [P, 2, S])
        th = sb("th", [P, 2, S])
        uu = sb("uu", [P, 2, S])
        squares = th[:, :, :].rearrange("p i n -> p (i n)").rearrange("p (t d) -> p t d", t=T)
        scaled = uu[:, :, :].rearrange("p i n -> p (i n)").rearrange("p (t d) -> p t d", t=T)
        av = sb("av", [P, S])
        st1 = sb("st1", [P, T, 6])
        st2 = sb("st2", [P, T, 6])
        mv1 = sb("mv1", [P, T, 2])
        mv2 = sb("mv2", [P, T, 2])
        rs1 = sb("rs1", [P, T])
        rs2 = sb("rs2", [P, T])
        ve_a = sb("ve_a", [P, 5, T])
        ve_f = sb("ve_f", [P, 2, T])
        cmax = sb("cmax", [P, 2, CH])
        csum = sb("csum", [P, 2, CH])
        crec = sb("crec", [P, 2, CH])
        small = sb("small", [P, 8, T, E])
        lg, g_a, g_b, g_c, mask1, mask2, mask, pos = (small[:, i, :, :] for i in range(8))
        g1 = sb("g1", [P, 8, T])
        maskb = sb("maskb", [P, T, E], BF16)
        ahead = sb("ahead", [P, T + 1, E])
        idx_f = sb("idx_f", [P, T, 2])
        idx_u = sb("idx_u", [P, T * 2], mybir.dt.uint32)
        idx_all = sb("idx_all", [P, B * T * 2])
        idx_u_all = sb("idx_u_all", [P, B * T * 2], mybir.dt.uint32)
        gate_b = sb("gate_b", [P, T, 2])
        gate_all = sb("gate_all", [P, B * T * 2])
        nm = sb("nm", [P, T, H])
        nr = sb("nr", [P, T, H])
        nparts = sb("nparts", [P, T, P], BF16)
        npart = nparts[:, :, 0:MROWS * H].rearrange("p t (r h) -> p t r h", r=MROWS)
        mT = sb("mT", [MROWS * H, 2, S], BF16)
        orec = sb("orec", [P, T, 4])
        ss = sb("ss", [P, 2, T])
        ri = sb("ri", [P, 2, T])
        n_tiles = sb("n_tiles", [P, E])
        first = sb("first", [P, E + 1])
        cmp_j = sb("cmp_j", [P, E, S * B // P])
        table = sb("table", [P, 2, MT], mybir.dt.uint32)
        shift = sb("shift", [P, E])
        idx_step = sb("idx_step", [P, B * T * 2])
        idx_now = sb("idx_now", [P, B * T * 2])
        zero_row = sb("zero_row", [P, E], mybir.dt.uint32)
        t_a = sb("t_a", [P, 4, MT])
        begun = sb("begun", [P, MT, E])
        pair = room[:, 0:2 * T * 2 * D].rearrange("p (i t k d) -> p i t k d", i=2, t=T, k=2)
        mixed = room[:, 4096:4096 + 2 * T * D].rearrange("p (i t d) -> p i t d", i=2, t=T)
        y_sb = room[:, 6144:6144 + 2 * T * D].rearrange("p (i t d) -> p i t d", i=2, t=T)
        squares_e = room[:, 8192:8192 + 2 * T * D].rearrange("p (i t d) -> p i t d", i=2, t=T)
        idx_two = sb("idx_two", [P, 2, T * 2], mybir.dt.uint32)
        gate_now = sb("gate_now", [P, 2, T * 2])
        ss_e = sb("ss_e", [P, 2, T])
        se_e = sb("se_e", [P, 2, T])
        ri_e = sb("ri_e", [P, 2, T])

        ps = ctx.enter_context(nc.psum_tensor("ps", [P, 8 * 512], F32))

        def bank(i, n=512, at=0):
            return ps[:, i * 512 + at:i * 512 + at + n]

        def internal(name, shape, dt=F32):
            return nc.dram_tensor(name, shape, dt, kind="Internal").ap()

        kt_d = internal("kt_d", (PAIRS, P, B * CK))
        vt_d = internal("vt_d", (PAIRS, P, B * CK))
        parts_d = internal("parts_d", (3, 2, KD, P, S), BF16)
        y_d = internal("y_d", (B, P, T, D))
        xs_d = internal("xs_d", (E * REG, D))
        eo_d = internal("eo_d", (MT * P, D))

        def done(ins, name, n=1):
            counted[name] = counted.get(name, 0) + n
            return ins.then_inc(sems[name], n)

        def need(eng, b, name, k):
            eng.wait_ge(sems[name], b * per[name] + k + AHEAD.get(name, 0))

        def before(eng, b, name):
            if not (isinstance(b, int) and b == 0):
                eng.wait_ge(sems[name], b * per[name] + AHEAD.get(name, 0))

        def carry_wait():
            nc.vector.memset(spare[:, :], 0.0)

        def in_batches(eng, walk, before_last=lambda: None):
            walk(0, None)
            with eng.Fori(1, B, 1) as b:
                walk(b, b - 1)
            before_last()
            walk(None, B - 1)

        def walked(b, c):
            return steps_of(b is not None, c is not None)

        def in_tiles(eng, walk, peeled=1):
            for q in range(peeled):
                walk(q, q == 0, False)
            with eng.Fori(peeled, MT // 4 - 1, 1) as q:
                walk(q, False, False)
            walk(MT // 4 - 1, False, True)

        x_v = A["x"].rearrange("b (t p) d -> b p t d", p=P)
        o_v = out.rearrange("b (t p) d -> b p t d", p=P)

        def at_batch(v, b):
            return v[b:b + 1, :, :, :].rearrange("a p t d -> p (a t) d") if isinstance(b, int) else v[bass.ds(b, 1), :, :, :].rearrange("a p t d -> p (a t) d")

        def span(b, n):
            return slice(b * n, (b + 1) * n) if isinstance(b, int) else bass.ds(b * n, n)

        block = ctx.enter_context(nc.Block())

        @block.sync
        def _(sp):
            def load_x(b):
                before(sp, b, "xb")
                before(sp, b, "xn1")
                done(sp.dma_start(xin[:, :, :], at_batch(x_v, b)), "x_in", 16)

            for k in range(KD):
                rows = slice(k * P, (k + 1) * P)
                for dst, src in ((wk_c, "L0_xattn_Wk"), (wq_c, "L0_xattn_Wq"), (wv_c, "L0_xattn_Wv")):
                    sp.dma_start(dst[:, k, :], A[src].rearrange("m h d -> m (h d)")[rows, :]).then_inc(p0["w_early"], 16)
            sp.dma_start(ctx_in, A["ctx_1024"].rearrange("b k m -> (b k) m").rearrange("(t p) m -> p t m", p=P)).then_inc(p0["w_early"], 16)
            for dst, src in ((bq, "L0_xattn_bq"), (bk, "L0_xattn_bk"), (bv, "L0_xattn_bv")):
                sp.dma_start(dst[:, :], A[src].rearrange("h d -> (h d)").rearrange("(a p) -> p a", p=P),
                             allow_slow_non_contiguous=True).then_inc(p0["w_early"], 16)
            sp.dma_start(wo_c[:, :, :], A["L0_xattn_Wo"].rearrange("h d m -> (h d) m").rearrange("(a p) m -> p a m", p=P)).then_inc(p0["w_mid"], 16)
            sp.dma_start(bo_bc[:, :], A["L0_xattn_bo"].partition_broadcast(P)).then_inc(p0["w_mid"], 16)
            load_x(0)
            for dst, src in ((wq, "L0_ffn_wq"), (wk, "L0_ffn_wk")):
                sp.dma_start(dst[:, :, :], A[src].rearrange("(k p) n -> p k n", p=P)).then_inc(p0["w_late"], 16)
            sp.dma_start(wv[:, :, 0:D], A["L0_ffn_wv"].rearrange("(k p) n -> p k n", p=P)).then_inc(p0["w_late"], 16)
            sp.dma_start(wv[:, :, D:D + E], A["L0_ffn_router_w"].rearrange("(k p) n -> p k n", p=P)).then_inc(p0["w_late"], 16)
            for dst, src in ((wo, "L0_ffn_wo"), (w1, "L0_ffn_w1"), (w3, "L0_ffn_w3"), (w2, "L0_ffn_w2")):
                sp.dma_start(dst[:, :, :], A[src].rearrange("(k p) n -> p k n", p=P)).then_inc(p0["w_late"], 16)
            for dst, src in ((aw_bc, "L0_ffn_attn_norm_w"), (fw_bc, "L0_ffn_ff_norm_w"), (mw_bc, "L0_ffn_moe_norm_w")):
                sp.dma_start(dst[:, :], A[src].partition_broadcast(P)).then_inc(p0["w_late"], 16)
            for i in range(2 * PAIRS):
                sp.wait_ge(p0["kv_sb"], i + 1)
                sp.dma_start((kt_d, vt_d)[i % 2][i // 2, :, :], kv_st[:, i % 4, :]).then_inc(kv_out[i % 4], 16)
            for i in range(4):
                sp.wait_ge(kv_out[i], 16 * 2 * PAIRS // 4)
            sp.wait_ge(p0["const"], 9)

            def batch(b, c):
                if b is not None:
                    if c is not None:
                        before(sp, b, "rep_k")
                        sp.sem_inc(reps_free, 1)
                    before(sp, b, "vw_ps")
                    for dst, src in ((k_bd, kt_d), (v_bd, vt_d)):
                        for i in range(2):
                            half = slice(i * CHD, (i + 1) * CHD)
                            done(sp.dma_start(dst[half, :, i * CK:(i + 1) * CK],
                                              src.rearrange("a p n -> p a n")[half, :, span(b, CK)]), "kv_in", 16)
                    if c is not None:
                        load_x(b)
                    for a in range(4):
                        for i, name in enumerate(("part1", "part2", "part3")):
                            need(sp, b, name, a + 1)
                            done(sp.dma_start(parts_d[i, a // 2, a % 2, :, :], parts[i][:, a, :]), ("q_out", "k_out")[a // 2], 16)
                    if c is not None:
                        before(sp, b, "b_ps")
                        sp.sem_inc(reps_free, 1)
                    for which, part_of, rep, out_name, name in ((0, Q_PART, q_rep, "q_out", "rep_q"), (1, K_PART, k_rep, "k_out", "rep_k")):
                        need(sp, b, out_name, per[out_name])
                        for j in range(NREP):
                            src = parts_d[part_of[j], which, :, :, :].rearrange("a (h d) n -> d (a h) n", d=HD)
                            done(sp.dma_start(rep[j * HD:(j + 1) * HD, :, :], src), name, 16)
                    for i in range(2):
                        need(sp, b, "mT_sb", i + 1)
                        for r in range(MROWS):
                            heads = slice(i * H // 2, (i + 1) * H // 2)
                            done(sp.dma_start(q_rep[KREP + r:KREP + r + 1, heads, :], mT[r * H + i * H // 2:r * H + (i + 1) * H // 2, i, :]), "m_row", 16)
                if c is not None:
                    need(sp, c, "y", 1)
                    done(sp.dma_start(at_batch(y_d, c), yb[:, :, :]), "y_out", 16)

            def tiles(q, is_first, is_last):
                for i in range(4):
                    row = sp.value_load(table[0:1, 1, span(q * 4 + i, 1)], min_val=0, max_val=E * REG - P)
                    if not is_first:
                        sp.wait_ge(moe["xT_ps"], q * 4 + i - 3)
                        sp.sem_inc(moe["xs_free"], 1)
                    sp.dma_start(xs[:, i, :], xs_d[bass.ds(row, P), :]).then_inc(xs_in[i], 16)

            def experts_first():
                sp.wait_ge(sems["av_ps"], B * per["av_ps"])
                sp.wait_ge(sems["b_ps"], B * per["b_ps"])
                for e in range(E):
                    up = ew[:, e * EW:e * EW + 2 * KD * D].rearrange("p (k i n) -> p k i n", k=KD, i=2)
                    down = ew[:, e * EW + 2 * KD * D:(e + 1) * EW].rearrange("p (m n) -> p m n", m=EB)
                    for dst, w in ((up[:, :, 0, :], "L0_ffn_ew1"), (up[:, :, 1, :], "L0_ffn_ew3"), (down, "L0_ffn_ew2")):
                        sp.dma_start(dst, A[w][e, :, :].rearrange("(k p) n -> p k n", p=P)).then_inc(moe["ew_in"], 16)
                sp.wait_ge(moe["table"], 2)
                for e in range(E):
                    row = sp.value_load(zero_row[0:1, e:e + 1], min_val=0, max_val=E * REG - P)
                    sp.dma_start(xs_d[bass.ds(row, P), :], zeros[:, :]).then_inc(moe["zero"], 16)
                sp.wait_ge(moe["zero"], 16 * E)
                sp.wait_ge(sems["scat"], B * per["scat"])
                tiles(0, True, False)

            in_batches(sp, batch, experts_first)
            with sp.Fori(1, MT // 4, 1) as q:
                tiles(q, False, False)
            sp.wait_ge(moe["dn_ps"], MT)
            sp.wait_ge(sems["y_out"], B * per["y_out"] + AHEAD["y_out"])
            for i in range(2):
                sp.dma_start(y_sb[:, i, :, :], at_batch(y_d, i)).then_inc(y_in[i], 16)
            with sp.Fori(0, B // 2 - 1, 1) as q:
                for i in range(2):
                    sp.wait_ge(fin["y"], q * 2 + i + 1)
                    sp.sem_inc(fin["y_free"], 1)
                    sp.dma_start(at_batch(o_v, q * 2 + i), y_sb[:, i, :, :]).then_inc(o_out[i], 16)
                for i in range(2):
                    sp.wait_ge(o_out[i], q * 16 + 16)
                    sp.sem_inc(fin["y_free"], 1)
                    sp.dma_start(y_sb[:, i, :, :], at_batch(y_d, q * 2 + i + 2)).then_inc(y_in[i], 16)
            for i in range(2):
                sp.wait_ge(fin["y"], B - 1 + i)
                sp.dma_start(at_batch(o_v, B - 2 + i), y_sb[:, i, :, :]).then_inc(o_out[i], 16)
            for i in range(2):
                sp.wait_ge(o_out[i], 16 * (B // 2))

        @block.gpsimd
        def _(pool):
            g = nc.gpsimd
            for name, n in AHEAD.items():
                pool.sem_inc(sems[name], n)
            for i, m in enumerate((ident, ident_b)):
                g.memset(m[:, :], 0.0).then_inc(p0["ident"], 1)
                pool.wait_ge(p0["ident"], 2 * i + 1)
                g.affine_select(out=m[:, :], in_=m[:, :], compare_op=ALU.not_equal, fill=1.0, base=0,
                                pattern=[[-1, P]], channel_multiplier=1).then_inc(p0["ident"], 1)
            for m, x in ((mask_qk, 0.0), (mask_kq, 0.0), (before_b, 1.0)):
                g.memset(m[:, :], x).then_inc(p0["ident"], 1)
            pool.wait_ge(p0["ident"], 7)
            g.affine_select(out=mask_qk[:, :], in_=mask_qk[:, :], compare_op=ALU.is_ge, fill=MASKED, base=0,
                            pattern=[[-1, P]], channel_multiplier=1).then_inc(p0["ident"], 1)
            g.affine_select(out=mask_kq[:, :], in_=mask_kq[:, :], compare_op=ALU.is_ge, fill=MASKED, base=0,
                            pattern=[[1, P]], channel_multiplier=-1).then_inc(p0["ident"], 1)
            g.affine_select(out=before_b[:, :], in_=before_b[:, :], compare_op=ALU.is_gt, fill=0.0, base=0,
                            pattern=[[1, P]], channel_multiplier=-1).then_inc(p0["ident"], 1)
            g.memset(neg_half[:, :], -0.5).then_inc(p0["const"], 1)
            g.memset(eps[:, 0, :], EPS).then_inc(p0["const"], 1)
            g.memset(eps[:, 1, :], D * EPS).then_inc(p0["const"], 1)
            g.memset(nparts[:, :, :], 0.0).then_inc(p0["const"], 1)
            g.memset(k_bd[:, :, :], 0.0).then_inc(p0["const"], 1)
            g.memset(v_bd[:, :, :], 0.0).then_inc(p0["const"], 1)
            g.memset(v_aug[:, :, :, :], 0.0).then_inc(p0["const"], 1)
            pool.wait_ge(p0["const"], 7)
            g.memset(v_aug[:, :, :, HD:HD + 1], 1.0).then_inc(p0["const"], 1)
            pool.wait_ge(p0["const"], 8)
            g.memset(k_rep[KREP:KREP + MROWS, :, :], 1.0).then_inc(p0["const"], 1)
            pool.wait_ge(p0["const"], 9)
            g.memset(ones_b[:, :], 1.0).then_inc(p0["iota"], 1)
            g.memset(zeros[:, :], 0.0).then_inc(p0["iota"], 1)
            g.memset(ahead[:, 0, :], 0.0).then_inc(p0["iota"], 1)
            at = 0
            for n, step, start in ((E, 1, -E), (E, 4, 0), (S * B // P, P, 0), (MT, 1, 0)):
                g.iota(iotas[:, at:at + n], pattern=[[step, n]], base=start, channel_multiplier=0).then_inc(p0["iota"], 1)
                at += n
            pool.wait_ge(p0["w_mid"], 16 * 2)

            def carry_wait():
                g.tensor_tensor(spare_p[:, :], neg_half[:, 0:1], neg_half[:, 0:1], ALU.mult)

            def batch(b, c):
                steps = {"pool_a": 0, "pool_f": 0}

                def rsqrt(n, dst, src, over, name, count, ve):
                    k, w = steps[count], src.shape[-1]
                    steps[count] += 1
                    done(g.tensor_tensor(ve[:, k, 0:w], src, eps[:, over, 0:w], ALU.add), count)
                    need(pool, n, count, k + 1)
                    done(g.tensor_tensor(dst, ve[:, k, 0:w], neg_half[:, 0:w], ALU.pow), name)

                def crossed(t):
                    need(pool, b, "mv2", t + 1)
                    rsqrt(b, rs2[:, t:t + 1], mv2[:, t, 1:2], 0, "rstd2", "pool_a", ve_a)

                for step in walked(b, c):
                    if step[0] == "x_norm":
                        need(pool, b, "mv1", 1)
                        rsqrt(b, rs1[:, :], mv1[:, :, 1], 0, "rstd1", "pool_a", ve_a)
                    elif step[0] == "f_wo":
                        for i in range(2):
                            need(pool, c, "wo_sq", i + 1)
                        rsqrt(c, ri[:, 0, :], ss[:, 0, :], 1, "wo_ri", "pool_f", ve_f)
                    elif step[0] == "f_o_norm":
                        need(pool, c, "wo_n", 2)
                        need(pool, c, "scat", per["scat"])
                        done(g.tensor_tensor(xn[:, :, :], xn[:, :, :], o_tok[:, :, :], ALU.add), "h")
                        need(pool, c, "h", 1)
                        before(pool, c, "y_out")
                        done(g.tensor_tensor(yb[:, :, :], x1[:, :, :], xn[:, :, :], ALU.add), "yb")
                    elif step[0] == "x_bias":
                        if c is not None:
                            need(pool, c, "yb", 1)
                        need(pool, b, "x_in", 16)
                        done(g.tensor_tensor(x1[:, :, :], xin[:, :, :], bo_bc[:, :].unsqueeze(1).to_broadcast([P, T, D]), ALU.add), "xb")
                    elif step[0] == "sum":
                        t = step[1]
                        need(pool, b, "sc_rec", t + 1)
                        v = s_sb[:, t % 2, :].rearrange("p (h k) -> p h k", h=CH)
                        done(g.tensor_tensor(v, v, crec[:, t % 2, :].unsqueeze(2).to_broadcast([P, CH, CK]), ALU.mult), "sc_nrm")
                    elif step[0] == "cv":
                        crossed(step[1])
                    elif step[0] == "qk":
                        for a in range(4):
                            need(pool, b, "part2", a + 1)
                            done(g.tensor_tensor(parts[2][:, a, :], rest[:, a % 2, :], parts[1][:, a, :], ALU.subtract), "part3")
                    elif step[0] == "slots":
                        need(pool, b, "slot", 1)
                        carry_wait()
                        for t in range(T):
                            for k in range(2):
                                done(g.indirect_dma_start(xs_d, bass.IndirectOffsetOnAxis(idx_u[:, 2 * t + k:2 * t + k + 1], 0),
                                                          xn[:, t, :], None), "scat", 16)
                    elif step[0] == "f_end":
                        need(pool, c, "fd_sq", 1)
                        rsqrt(c, ri[:, 1, :], ss[:, 1, :], 1, "fd_ri", "pool_f", ve_f)
                        need(pool, c, "fd_n", 1)
                        need(pool, c, "yb", 1)
                        done(g.tensor_tensor(yb[:, :, :], yb[:, :, :], scaled, ALU.add), "y")

            in_batches(pool, batch)

            def tiles(q, is_first, is_last):
                for i in range(4):
                    pool.wait_ge(moe["eo"], q * 4 + i + 1)
                    g.dma_start(eo_d[span(q * 4 + i, P), :], eo[:, i, :]).then_inc(eo_out[i], 16)

            in_tiles(pool, tiles)
            for i in range(4):
                pool.wait_ge(eo_out[i], 16 * (MT // 4))

            def gather(n, i, first_time):
                if not first_time:
                    pool.wait_ge(fin["mix"], n - 1)
                g.tensor_copy(idx_two[:, i, :], idx_u_all[:, span(n, 2 * T)]).then_inc(fin["idx"], 1)
                pool.wait_ge(fin["idx"], n + 1)
                carry_wait()
                for t in range(T):
                    for k in range(2):
                        g.indirect_dma_start(pair[:, i, t, k, :], None, eo_d,
                                             bass.IndirectOffsetOnAxis(idx_two[:, i, 2 * t + k:2 * t + k + 1], 0)).then_inc(got[i], 16)

            def inverse(n, i):
                pool.wait_ge(fin["sq"], n + 1)
                g.tensor_tensor(se_e[:, i, :], ss_e[:, i, :], eps[:, 1, :], ALU.add).then_inc(fin["eps"], 1)
                pool.wait_ge(fin["eps"], n + 1)
                g.tensor_tensor(ri_e[:, i, :], se_e[:, i, :], neg_half[:, :], ALU.pow).then_inc(fin["ri"], 1)

            pool.wait_ge(moe["table"], 3)
            gather(0, 0, True)
            gather(1, 1, True)
            with pool.Fori(1, B // 2, 1) as q:
                for i in range(2):
                    inverse(q * 2 + i - 2, i)
                    gather(q * 2 + i, i, False)
            for i in range(2):
                inverse(B - 2 + i, i)

        @block.tensor
        def _(pe):
            mm, tr = nc.tensor.matmul, nc.tensor.transpose
            pe.wait_ge(p0["ident"], 2)
            pe.wait_ge(p0["w_early"], 16 * 10)
            blocks = [(ctx_in[:, t, k * P:(k + 1) * P]) for k in range(KD) for t in range(4)]
            blocks += [(wq_c[:, k, a * P:(a + 1) * P]) for k in range(KD) for a in range(PAIRS)]
            for i, src in enumerate(blocks):
                last = tr(bank(i // 4, P, i % 4 * P), src, ident[:, :])
                if i % 4 == 3:
                    last.then_inc(p0["tr_ps"], 1)
            pe.wait_ge(p0["tr_sb"], 6)
            for i in range(2 * PAIRS):
                if i >= 2:
                    pe.wait_ge(p0["kv_sb"], i - 1)
                w = (wk_c, wv_c)[i % 2]
                for k in range(KD):
                    last = mm(bank(6 + i % 2), w[:, k, (i // 2) * P:(i // 2 + 1) * P], ctxT[:, k, :], start=(k == 0), stop=(k == KD - 1))
                last.then_inc(p0["kv_ps"], 1)
            pe.wait_ge(p0["w_mid"], 16 * 2)
            pe.wait_ge(p0["ident"], 10)
            pe.wait_ge(p0["const"], 9)
            pe.wait_ge(p0["iota"], 3)
            pe.wait_ge(p0["kv_sb"], 16)

            def batch(b, c):
                def turn(n, src, banks, waits, name):
                    for t2 in range(2):
                        for w, count in waits(t2):
                            need(pe, n, w, count)
                        for k in range(KD):
                            for t in (2 * t2, 2 * t2 + 1):
                                last = tr(bank(banks[t2], P, (k * 2 + t % 2) * P), src[:, t, k * P:(k + 1) * P], ident[:, :])
                        done(last, name)

                def out_t(n, grp):
                    need(pe, n, "av_sb", grp + 1)
                    if grp:
                        need(pe, n, "o_nrm", grp)
                    else:
                        need(pe, n, "mT_sb", 2)
                    for t in range(T):
                        last = tr(bank(6, P, t * P), av[:, t * P:(t + 1) * P], ident[:, :])
                    done(last, "avT_ps")

                nmax = 0
                for step in walked(b, c):
                    kind = step[0]
                    if kind == "x_turn":
                        if c is not None:
                            need(pe, c, "b_exp", per["b_exp"])
                        turn(b, xh, (2, 3), lambda t2: [("xn1", 1)], "xT1")
                    elif kind == "m_build":
                        need(pe, b, "kv_in", 64)
                        for i in range(4):
                            k, half = i // 2, i % 2
                            if i == 2:
                                need(pe, b, "xnT", 2)
                            for a in range(4):
                                pa = half * 4 + a
                                last = mm(bank(i, P, a * P), wqT[:, pa, k * P:(k + 1) * P], k_bd[:, pa, :], start=True, stop=True)
                            done(last, "m_ps")
                    elif kind == "bqk":
                        need(pe, b, "bq", 1)
                        for i in range(2):
                            need(pe, b, ("m_act", "m_dve")[i], 1)
                            for a in range(4):
                                pa = i * 4 + a
                                last = mm(bank(i, P, a * P), bq_bc[:, pa, :], k_bd[:, pa, :], start=True, stop=True)
                            done(last, "bqk_ps")
                    elif kind == "vw":
                        for i in range(4):
                            if i < 2:
                                need(pe, b, ("m_act", "m_dve")[i], 2)
                            else:
                                need(pe, b, "vw_sb", i - 1)
                            for a in range(2):
                                last = mm(bank(2 + i % 2, D, a * D), v_bd[:, 2 * i + a, :], wo_c[:, 2 * i + a, :], start=True, stop=True)
                            done(last, "vw_ps")
                    elif kind == "cs":
                        t = step[1]
                        if t == 0:
                            need(pe, b, "m_act", 2)
                            need(pe, b, "m_dve", 2)
                            need(pe, b, "bqk_sb", 2)
                        else:
                            need(pe, b, "sc_add", t)
                        for half in range(2):
                            for k in range(KD):
                                last = mm(bank(half), xnT[:, k, t * P:(t + 1) * P], m_sb[:, k, half * 512:(half + 1) * 512], start=(k == 0), stop=(k == KD - 1))
                        done(last, "sc_ps")
                    elif kind == "ct":
                        t = step[1]
                        need(pe, b, "sc_nrm", t + 1)
                        if t == 0:
                            need(pe, b, "vw_sb", 4)
                        for half in range(2):
                            if half and t:
                                need(pe, b, "x1", t)
                            for a in range(4):
                                last = tr(bank(2 + half, P, a * P), s_sb[:, t % 2, (half * 4 + a) * P:(half * 4 + a + 1) * P], ident[:, :])
                            done(last, "pT_ps")
                    elif kind == "cv":
                        t = step[1]
                        need(pe, b, "pT_sb", 2 * t + 2)
                        for a in range(PAIRS):
                            last = mm(bank(3, D), pT[:, t % 2, a * P:(a + 1) * P], vw[:, a, :], start=(a == 0), stop=(a == PAIRS - 1))
                        done(last, "pv_ps")
                    elif kind == "x2_turn":
                        turn(b, xn, (2, 3), lambda t2: [("xn2", 2 * t2 + 2), ("x1", T)], "xT2")
                    elif kind == "qk":
                        if c is None:
                            pe.wait_ge(p0["w_late"], 16 * 11)
                        need(pe, b, "xn2T", 2)
                        for a in range(4):
                            w = (wq, wk)[a // 2]
                            for k in range(KD):
                                last = mm(bank(a), w[:, k, a % 2 * P:(a % 2 + 1) * P], xn2T[:, k, :], start=(k == 0), stop=(k == KD - 1))
                            done(last, "qk_ps")
                    elif kind == "v":
                        for t in range(T):
                            need(pe, b, "rest1", t + 1)
                            for k in range(KD):
                                last = mm(bank(t, D + E), xn2T[:, k, t * P:(t + 1) * P], wv[:, k, :], start=(k == 0), stop=(k == KD - 1))
                            done(last, "v_ps")
                    elif kind == "slots":
                        need(pe, b, "mask", 1)
                        need(pe, b, "v_sb", T)
                        mb = maskb[:, :, :].rearrange("p t e -> p (t e)")
                        mm(bank(0, T * E), before_b[:, :], mb, start=True, stop=True)
                        done(mm(bank(0, T * E, T * E), ones_b[:, :], mb, start=True, stop=True), "rank_ps")
                    elif kind == "max":
                        hp = step[1]
                        if hp == 0:
                            need(pe, b, "slot", 1)
                            need(pe, b, "rep_q", per["rep_q"])
                            need(pe, b, "rep_k", per["rep_k"])
                        for t in range(T):
                            if nmax >= 2:
                                need(pe, b, "a_max", nmax - 1)
                            if nmax == 20:
                                need(pe, b, "mT_sb", 1)
                            n = (t + 1) * P
                            for i in range(2):
                                h, o = 2 * hp + i, nmax % 2 * 2 + i
                                mm(bank(o, n), q_rep[0:KREP, h, t * P:n], k_rep[0:KREP, h, 0:n], start=True, stop=False)
                                last = mm(bank(o, P, t * P), ident_b[:, :], mask_qk[:, :], start=False, stop=True)
                            done(last, "a_ps")
                            nmax += 1
                    elif kind == "shift":
                        half = step[1]
                        need(pe, b, "m_part", half + 1)
                        if half == 0:
                            need(pe, b, "a_max", nmax - 1)
                        elif c is not None:
                            need(pe, c, "fu_g", FB)
                        psb = bank(6 * half, 256).bitcast(BF16)
                        for t in range(T):
                            last = tr(psb[:, t * P:(t + 1) * P], nparts[:, t, :], ident_b[:, :])
                        done(last, "mT_ps")
                    elif kind == "score":
                        grp, u = step[1:]
                        n = grp * 5 + u
                        if n < 2:
                            need(pe, b, "a_max", per["a_max"] - 1 + n)
                        if n in (0, 10):
                            need(pe, b, "m_row", per["m_row"] // (1 if n else 2))
                        if n >= 2:
                            need(pe, b, "b_exp", n - 1)
                        for j in range(4):
                            for kb, at, w in score_segments(j):
                                if at // 1024 != u:
                                    continue
                                o = n % 2 * 1024 + at % 1024
                                mm(ps[:, o:o + w], k_rep[0:KREP + MROWS, 4 * grp + j, kb * P:(kb + 1) * P],
                                   q_rep[0:KREP + MROWS, 4 * grp + j, kb * P:S], start=True, stop=False, skip_group_check=True)
                                last = mm(ps[:, o:o + P], ident_b[:, :], mask_kq[:, :], start=False, stop=True, skip_group_check=True)
                        done(last, "b_ps")
                    elif kind == "value":
                        grp = step[1]
                        need(pe, b, "b_exp", 5 * grp + 5)
                        if grp:
                            need(pe, b, "av_sb", grp)
                        elif c is not None:
                            need(pe, c, "fu_g", FB)
                        for kb in range(T):
                            for j in range(4):
                                at = [a for k, a, _ in score_segments(j) if k == kb][0]
                                w = S - kb * P
                                last = mm(ps[32 * j:32 * j + 32, 5 * 512 + kb * P:6 * 512], v_aug[:, kb, 4 * grp + j, :],
                                          prob[:, grp % 2, at:at + w], start=(kb == 0), stop=(kb == T - 1),
                                          skip_group_check=True, tile_position=(0, 32 * j))
                        done(last, "av_ps")
                    elif kind == "out_t":
                        out_t(b, step[1])
                    elif kind == "f_out_t":
                        out_t(c, step[1])
                    elif kind == "f_o_turn":
                        before(pe, c, "fd_n")
                        turn(c, o_tok, (4, 7), lambda t2: [("o_nrm", G)], "oT_ps")
                    elif kind == "f_wo":
                        need(pe, c, "oT_sb", 2)
                        for t in range(T):
                            for k in range(KD):
                                last = mm(bank((4, 7)[t // 2], D, t % 2 * D), oT[:, k, t * P:(t + 1) * P], wo[:, k, :], start=(k == 0), stop=(k == KD - 1))
                            if t % 2:
                                done(last, "wo_ps")
                    elif kind == "f_h_turn":
                        turn(c, xn, (4, 7), lambda t2: [("h", 1)], "hT_ps")
                    elif kind == "fu":
                        m = step[1]
                        if m == 0:
                            need(pe, c, "hT_sb", 2)
                        elif b is not None or m >= 2:
                            need(pe, c, "fu_g", m if b is not None else m - 1)
                        for i, w in enumerate((w1, w3)):
                            for k in range(KD):
                                last = mm(bank(up_banks(b, m)[i]), w[:, k, m * P:(m + 1) * P], hT[:, k, :], start=(k == 0), stop=(k == KD - 1))
                        done(last, "fu_ps")
                    elif kind == "fd":
                        m = step[1]
                        need(pe, c, "fu_g", m + 1)
                        for t in range(T):
                            last = mm(bank((4, 7)[t // 2], D, t % 2 * D), gT[:, m % 2, t * P:(t + 1) * P], w2[:, m, :],
                                      start=(m == 0 and t % 2 == 0), stop=(m == FB - 1), skip_group_check=True)
                        done(last, "fd_ps")

            in_batches(pe, batch)
            pe.wait_ge(sems["b_exp"], B * per["b_exp"])

            pe.wait_ge(moe["table"], 2)
            pe.wait_ge(moe["ew_in"], 16 * 3 * E)

            def tiles(q, is_first, is_last):
                def turn_x(t, i):
                    pe.wait_ge(xs_in[i % 4], (q + i // 4) * 16 + 16)
                    if not (is_first and i < 2):
                        pe.wait_ge(moe["xT"], t - 1)
                    for k in range(KD):
                        last = tr(bank(i % 2, P, k * P), xs[:, i % 4, k * P:(k + 1) * P], ident[:, :])
                    last.then_inc(moe["xT_ps"], 1)

                def up(t, i):
                    at = pe.value_load(table[0:1, 0, span(t, 1)], min_val=0, max_val=(E - 1) * EW)
                    pe.wait_ge(moe["xT"], t + 1)
                    if not (is_first and i < 2):
                        pe.wait_ge(moe["g"], t - 1)
                    for k in range(KD):
                        last = mm(bank(2 + i % 2), xsT[:, i % 2, k * P:(k + 1) * P], ew[:, bass.ds(at + k * 2 * D, 2 * D)], start=(k == 0), stop=(k == KD - 1))
                    last.then_inc(moe["up_ps"], 1)

                def turn_g(t, i):
                    pe.wait_ge(moe["g"], t + 1)
                    if not (is_first and i < 2):
                        pe.wait_ge(moe["gT"], t - 1)
                    for k in range(EB):
                        last = tr(bank(4 + i % 2, P, k * P), e_g[:, i % 2, k * P:(k + 1) * P], ident[:, :])
                    last.then_inc(moe["gT_ps"], 1)

                def down(t, i):
                    at = pe.value_load(table[0:1, 0, span(t, 1)], min_val=0, max_val=(E - 1) * EW)
                    pe.wait_ge(moe["gT"], t + 1)
                    if not (is_first and i < 2):
                        pe.wait_ge(moe["eo"], t - 1)
                    for m in range(EB):
                        last = mm(bank(6 + i % 2, D), e_gT[:, i % 2, m * P:(m + 1) * P], ew[:, bass.ds(at + KD * 2 * D + m * D, D)], start=(m == 0), stop=(m == EB - 1))
                    last.then_inc(moe["dn_ps"], 1)

                if is_first:
                    turn_x(0, 0)
                for i in range(4):
                    t = q * 4 + i
                    up(t, i)
                    if is_first and i == 1:
                        pe.wait_ge(sems["fd_n"], B + AHEAD["fd_n"])
                    if not (is_first and i == 0):
                        turn_g(t - 1, (i - 1) % 4 + (0 if i else 8))
                    if not (is_last and i == 3):
                        turn_x(t + 1, i + 1)
                    if not (is_first and i < 2):
                        down(t - 2, (i - 2) % 4 + (0 if i > 1 else 8))
                if is_last:
                    turn_g(t, 3)
                    down(t - 1, 2)
                    down(t, 3)

            in_tiles(pe, tiles)

        @block.scalar
        def _(act):
            fn = nc.scalar.activation
            for i in range(6):
                act.wait_ge(p0["tr_ps"], i + 1)
                src = bank(i)
                if i < 2:
                    fn(ctxT[:, i, :], src, ACT.Copy).then_inc(p0["tr_sb"], 1)
                else:
                    k, a0 = (i - 2) // 2, (i - 2) % 2 * 4
                    fn(wqT[:, a0:a0 + 4, k * P:(k + 1) * P], src.rearrange("p (a n) -> p a n", a=4), ACT.Copy).then_inc(p0["tr_sb"], 1)
            for i in range(2 * PAIRS):
                act.wait_ge(p0["kv_ps"], i + 1)
                if i == 0:
                    act.wait_ge(p0["bk"], 1)
                if i >= 4:
                    act.wait_ge(kv_out[i % 4], 16 * (i // 4))
                if i % 2 == 0:
                    fn(kv_st[:, i % 4, :], bank(6 + i % 2), ACT.Identity, bias=bk[:, i // 2:i // 2 + 1], scale=CHD ** -0.5).then_inc(p0["kv_sb"], 1)
                else:
                    fn(kv_st[:, i % 4, :], bank(6 + i % 2), ACT.Identity, bias=bv[:, i // 2:i // 2 + 1]).then_inc(p0["kv_sb"], 1)
            act.wait_ge(p0["kv_sb"], 16)
            for i in range(4):
                act.wait_ge(kv_out[i], 16 * 2 * PAIRS // 4)

            def batch(b, c):
                def spread(n, dst, banks, src_name, name):
                    for t2 in range(2):
                        need(act, n, src_name, t2 + 1)
                        done(fn(dst[:, :, t2 * 2 * P:(t2 + 1) * 2 * P], bank(banks[t2]).rearrange("p (k n) -> p k n", k=KD), ACT.Copy), name)

                for step in walked(b, c):
                    kind = step[0]
                    if kind == "x_turn":
                        spread(b, xnT, (2, 3), "xT1", "xnT")
                    elif kind == "m_build":
                        for i in (0, 2):
                            need(act, b, "m_ps", i + 1)
                            done(fn(m_sb[:, i // 2, 0:512], bank(i), ACT.Copy), "m_act")
                    elif kind == "bqk":
                        for i in range(2):
                            need(act, b, "bqk_ps", i + 1)
                            done(fn(bqk[:, i * 512:(i + 1) * 512], bank(i), ACT.Copy), "bqk_sb")
                    elif kind == "vw":
                        for i in range(4):
                            need(act, b, "vw_ps", i + 1)
                            done(fn(vw[:, 2 * i:2 * i + 2, :], bank(2 + i % 2).rearrange("p (a n) -> p a n", a=2), ACT.Copy), "vw_sb")
                    elif kind == "exp":
                        t = step[1]
                        need(act, b, "sc_sub", t + 1)
                        done(fn(s_sb[:, t % 2, :], s_sb[:, t % 2, :], ACT.Exp), "sc_exp")
                    elif kind == "ct":
                        t = step[1]
                        for half in range(2):
                            need(act, b, "pT_ps", 2 * t + half + 1)
                            if t >= 2:
                                need(act, b, "pv_ps", t - 1)
                            done(fn(pT[:, t % 2, half * 512:(half + 1) * 512], bank(2 + half), ACT.Copy), "pT_sb")
                    elif kind == "x2_turn":
                        spread(b, xn2T, (2, 3), "xT2", "xn2T")
                    elif kind == "qk":
                        before(act, b, "k_out")
                        for a in range(4):
                            need(act, b, "qk_ps", a + 1)
                            done(fn(parts[0][:, a, :], bank(a), ACT.Copy, scale=(HD ** -0.5 if a < 2 else 1.0)), "part1")
                            if a >= 1:
                                need(act, b, "rest1", a)
                                done(fn(parts[1][:, a - 1, :], rest[:, (a - 1) % 2, :], ACT.Copy), "part2")
                        need(act, b, "rest1", 4)
                        done(fn(parts[1][:, 3, :], rest[:, 1, :], ACT.Copy), "part2")
                    elif kind == "v":
                        for t in range(T):
                            need(act, b, "lg", t + 1)
                            done(fn(v_aug[:, t, :, 0:HD], bank(t, D).rearrange("p (h d) -> p h d", h=H), ACT.Copy), "v_sb")
                    elif kind == "route":
                        need(act, b, "gmax", 1)
                        done(fn(g_b, g_a, ACT.Exp), "gexp")
                    elif kind == "score":
                        grp, u = step[1:]
                        n = grp * 5 + u
                        need(act, b, "b_ps", n + 1)
                        if u == 0 and grp >= 2:
                            need(act, b, "av_ps", grp - 1)
                        done(fn(prob[:, grp % 2, u * 1024:(u + 1) * 1024], ps[:, n % 2 * 1024:n % 2 * 1024 + 1024], ACT.Exp), "b_exp")
                    elif kind == "value":
                        grp = step[1]
                        need(act, b, "av_ps", grp + 1)
                        if grp:
                            need(act, b, "avT_ps", grp)
                        done(fn(av[:, :], bank(5), ACT.Copy), "av_sb")
                    elif kind == "f_o_turn":
                        spread(c, oT, (4, 7), "oT_ps", "oT_sb")
                    elif kind == "f_wo":
                        for i in range(2):
                            need(act, c, "wo_ps", i + 1)
                            for t in (2 * i, 2 * i + 1):
                                last = fn(squares[:, t, :], bank((4, 7)[i], D, t % 2 * D), ACT.Square, accum_out=ss[:, 0, t:t + 1])
                            done(last, "wo_sq")
                    elif kind == "f_h_turn":
                        spread(c, hT, (4, 7), "hT_ps", "hT_sb")
                    elif kind == "fu":
                        m = step[1]
                        need(act, c, "fu_ps", m + 1)
                        if m >= 2:
                            need(act, c, "fu_u", m - 1)
                        done(fn(th[:, m % 2, :], bank(up_banks(b, m)[0]), ACT.Tanh, scale=0.5), "fu_th")
                    elif kind == "f_end":
                        need(act, c, "fd_ps", FB)
                        need(act, c, "fu_u", FB)
                        for t in range(T):
                            last = fn(squares[:, t, :], bank((4, 7)[t // 2], D, t % 2 * D), ACT.Square, accum_out=ss[:, 1, t:t + 1])
                        done(last, "fd_sq")

            in_batches(act, batch)

            def tiles(q, is_first, is_last):
                def x_out(t, i):
                    act.wait_ge(moe["xT_ps"], t + 1)
                    if not (is_first and i < 2):
                        act.wait_ge(moe["up_ps"], t - 1)
                    fn(xsT[:, i % 2, :], bank(i % 2, D), ACT.Copy).then_inc(moe["xT"], 1)

                def eo_copy(t, i, sent):
                    act.wait_ge(moe["dn_ps"], t + 1)
                    if sent is not None:
                        act.wait_ge(eo_out[i], sent * 16)
                    fn(eo[:, i, :], bank(6 + i % 2, D), ACT.Copy).then_inc(moe["eo"], 1)

                if is_first:
                    x_out(0, 0)
                for i in range(4):
                    t = q * 4 + i
                    act.wait_ge(moe["up_ps"], t + 1)
                    if not (is_first and i < 2):
                        act.wait_ge(moe["u"], t - 1)
                    fn(e_th[:, i % 2, :], bank(2 + i % 2, D), ACT.Tanh, scale=0.5).then_inc(moe["th"], 1)
                    if not (is_last and i == 3):
                        x_out(t + 1, i + 1)
                    if i >= 2:
                        eo_copy(t - 2, i - 2, None if is_first else q)
                    elif not is_first:
                        eo_copy(t - 2, i + 2, None if isinstance(q, int) and q == 1 else q - 1)
                if is_last:
                    eo_copy(t - 1, 2, q)
                    eo_copy(t, 3, q)

            in_tiles(act, tiles, 2)

            def square(n, i):
                act.wait_ge(fin["mix"], n + 1)
                for t in range(T):
                    last = fn(squares_e[:, i, t, :], mixed[:, i, t, :], ACT.Square, accum_out=ss_e[:, i, t:t + 1])
                last.then_inc(fin["sq"], 1)

            with act.Fori(0, B // 2, 1) as q:
                for i in range(2):
                    square(q * 2 + i, i)

        @block.vector
        def _(dve):
            v = nc.vector
            dve.wait_ge(p0["w_early"], 16 * 10)
            v.tensor_scalar(bk[:, :], bk[:, :], CHD ** -0.5, None, ALU.mult).then_inc(p0["bk"], 1)
            dve.wait_ge(p0["const"], 9)
            dve.wait_ge(p0["iota"], 7)
            at = 0
            for dst, n, scale in ((e_less, E, 1.0), (e_row, E, REG / 4), (tile_at, S * B // P, 1.0), (tile_no, MT, 1.0)):
                v.tensor_scalar(dst[:, :], iotas[:, at:at + n], scale, None, ALU.mult).then_inc(p0["const"], 1)
                at += n
            dve.wait_ge(p0["const"], 13)
            for i in range(4):
                dve.wait_ge(kv_out[i], 16 * 2 * PAIRS // 4)

            n_link = [0]

            def chain(ins):
                n_link[0] += 1
                ins.then_inc(moe["table_step"], 1)
                dve.wait_ge(moe["table_step"], n_link[0])

            def make_table():
                dve.wait_ge(sems["slot"], B)
                counts = ahead[:, 0, :]
                v.tensor_tensor(n_tiles[:, :], counts, e_row[:, :], ALU.add).then_inc(moe["table_step"], 1)
                n_link[0] += 1
                dve.wait_ge(moe["table_step"], n_link[0])
                v.tensor_copy(zero_row[:, :], n_tiles[:, :]).then_inc(moe["table"], 1)
                dve.wait_ge(moe["table"], 1)
                chain(v.tensor_tensor(cmp_j[:, :, :], counts.unsqueeze(2).to_broadcast([P, E, S * B // P]),
                                      tile_at[:, :].unsqueeze(1).to_broadcast([P, E, S * B // P]), ALU.is_gt))
                chain(v.tensor_reduce(n_tiles[:, :], cmp_j[:, :, :], AX.X, ALU.add))
                chain(v.memset(first[:, 0:1], 0.0))
                for e in range(E):
                    chain(v.tensor_tensor(first[:, e + 1:e + 2], first[:, e:e + 1], n_tiles[:, e:e + 1], ALU.add))
                total = first[:, E:E + 1]
                tile_c, expert, start, row = (t_a[:, i, :] for i in range(4))
                chain(v.tensor_scalar(start, tile_no[:, :], 1.0, total, ALU.add, ALU.min))
                chain(v.tensor_scalar(tile_c, start, -1.0, None, ALU.add))
                by_expert = [P, MT, E]
                starts = first[:, 0:E].unsqueeze(1).to_broadcast(by_expert)
                chain(v.tensor_tensor(begun[:, :, :], tile_c.unsqueeze(2).to_broadcast(by_expert), starts, ALU.is_ge))
                chain(v.tensor_reduce(expert, begun[:, :, :], AX.X, ALU.add))
                chain(v.tensor_tensor(begun[:, :, :], begun[:, :, :], starts, ALU.mult))
                chain(v.tensor_reduce(start, begun[:, :, :], AX.X, ALU.max))
                chain(v.tensor_scalar(expert, expert, -1.0, None, ALU.add))
                chain(v.tensor_tensor(row, tile_c, start, ALU.subtract))
                chain(v.tensor_scalar(row, row, float(P), None, ALU.mult))
                chain(v.scalar_tensor_tensor(row, expert, float(REG), row, ALU.mult, ALU.add))
                chain(v.tensor_scalar(table[:, 0, :], expert, float(EW), None, ALU.mult))
                v.tensor_copy(table[:, 1, :], row).then_inc(moe["table"], 1)

            def shift_indices():
                chain(v.tensor_scalar(shift[:, :], n_tiles[:, :], float(P), -float(REG), ALU.mult, ALU.add))
                chain(v.tensor_copy(idx_now[:, :], idx_all[:, :]))
                for e in range(1, E):
                    chain(v.tensor_scalar(idx_step[:, :], idx_all[:, :], float(e * REG), shift[:, e - 1:e], ALU.is_ge, ALU.mult))
                    chain(v.tensor_tensor(idx_now[:, :], idx_now[:, :], idx_step[:, :], ALU.add))
                v.tensor_copy(idx_u_all[:, :], idx_now[:, :]).then_inc(moe["table"], 1)

            def batch(b, c):
                links = [0]

                def link(ins):
                    links[0] += 1
                    done(ins, "dve_step")
                    need(dve, b, "dve_step", links[0])

                def per_tile(x):
                    return x.unsqueeze(2).to_broadcast([P, T, E])

                def per_expert(x):
                    return x.unsqueeze(1).to_broadcast([P, T, E])

                def out_t(n, grp):
                    need(dve, n, "avT_ps", grp + 1)
                    t4 = bank(6).rearrange("p (t j c) -> p t j c", t=T, j=4)
                    done(v.reciprocal(orec[:, :, :], t4[:, :, :, HD]), "o_rec")
                    need(dve, n, "o_rec", grp + 1)
                    done(v.tensor_tensor(o_tok[:, :, grp * 64:(grp + 1) * 64].rearrange("p t (j d) -> p t j d", j=4), t4[:, :, :, 0:HD],
                                         orec[:, :, :].unsqueeze(3).to_broadcast([P, T, 4, HD]), ALU.mult), "o_nrm")

                def normed(t):
                    need(dve, b, "rstd2", t + 1)
                    if t == 0 and c is not None:
                        need(dve, c, "hT_ps", 2)
                        need(dve, c, "yb", 1)
                    done(v.tensor_scalar(xn[:, t, :], x1[:, t, :], mv2[:, t, 0:1], rs2[:, t:t + 1], ALU.subtract, ALU.mult), "xn2")

                nmax = 0
                for step in walked(b, c):
                    kind = step[0]
                    if kind == "x_norm":
                        need(dve, b, "x_in", 16)
                        for t in range(T):
                            last = v.bn_stats(st1[:, t, :], xin[:, t, :])
                        done(last, "stats")
                        need(dve, b, "stats", 1)
                        carry_wait()
                        for t in range(T):
                            last = v.bn_aggr(mv1[:, t, :], st1[:, t, :])
                        done(last, "mv1")
                        need(dve, b, "rstd1", 1)
                        for t in range(T):
                            last = v.tensor_scalar(xh[:, t, :], xin[:, t, :], mv1[:, t, 0:1], rs1[:, t:t + 1], ALU.subtract, ALU.mult)
                        done(last, "xn1")
                    elif kind == "x_turn":
                        if c is not None:
                            need(dve, c, "av_ps", G)
                        done(v.tensor_copy(bq_bc, bq[:, :].unsqueeze(2).to_broadcast([P, PAIRS, P])), "bq")
                    elif kind == "m_build":
                        for i in (1, 3):
                            need(dve, b, "m_ps", i + 1)
                            done(v.tensor_copy(m_sb[:, i // 2, 512:1024], bank(i)), "m_dve")
                    elif kind == "cs":
                        t = step[1]
                        need(dve, b, "sc_ps", t + 1)
                        if t == 0:
                            need(dve, b, "bqk_sb", 2)
                        if t >= 2:
                            need(dve, b, "pT_ps", 2 * (t - 2) + 2)
                        s3 = s_sb[:, t % 2, :].rearrange("p (h k) -> p h k", h=CH)
                        done(v.tensor_tensor(s_sb[:, t % 2, :], ps[:, 0:1024], bqk, ALU.add), "sc_add")
                        need(dve, b, "sc_add", t + 1)
                        done(v.tensor_reduce(cmax[:, t % 2, :], s3, AX.X, ALU.max), "sc_max")
                        need(dve, b, "sc_max", t + 1)
                        done(v.tensor_tensor(s3, s3, cmax[:, t % 2, :].unsqueeze(2).to_broadcast([P, CH, CK]), ALU.subtract), "sc_sub")
                    elif kind == "sum":
                        t = step[1]
                        need(dve, b, "sc_exp", t + 1)
                        if t >= 2:
                            need(dve, b, "sc_nrm", t - 1)
                        s3 = s_sb[:, t % 2, :].rearrange("p (h k) -> p h k", h=CH)
                        done(v.tensor_reduce(csum[:, t % 2, :], s3, AX.X, ALU.add), "sc_sum")
                        need(dve, b, "sc_sum", t + 1)
                        done(v.reciprocal(crec[:, t % 2, :], csum[:, t % 2, :]), "sc_rec")
                    elif kind == "cv":
                        t = step[1]
                        need(dve, b, "pv_ps", t + 1)
                        need(dve, b, "xb", 1)
                        done(v.tensor_tensor(x1[:, t, :], x1[:, t, :], bank(3, D), ALU.add), "x1")
                        need(dve, b, "x1", t + 1)
                        done(v.bn_stats(st2[:, t, :], x1[:, t, :]), "stats")
                        need(dve, b, "stats", 2 + t)
                        carry_wait()
                        done(v.bn_aggr(mv2[:, t, :], st2[:, t, :]), "mv2")
                        if t >= 1:
                            normed(t - 1)
                    elif kind == "norm_3":
                        normed(T - 1)
                    elif kind == "qk":
                        if c is None:
                            dve.wait_ge(p0["w_late"], 16 * 11)
                            for w in (aw_bc, fw_bc, mw_bc):
                                v.tensor_scalar(w[:, :], w[:, :], float(D) ** 0.5, None, ALU.mult).then_inc(p0["norms"], 1)
                            dve.wait_ge(p0["norms"], 3)
                        for a in range(4):
                            need(dve, b, "part1", a + 1)
                            if a >= 2:
                                need(dve, b, "part3", a - 1)
                            done(v.scalar_tensor_tensor(rest[:, a % 2, :], bank(a), (HD ** -0.5 if a < 2 else 1.0), parts[0][:, a, :], ALU.mult, ALU.subtract), "rest1")
                    elif kind == "v":
                        for t in range(T):
                            need(dve, b, "v_ps", t + 1)
                            last = done(v.tensor_copy(lg[:, t, :], bank(t, E, D)), "lg")
                    elif kind == "route":
                        need(dve, b, "lg", T)
                        link(v.tensor_reduce(g1[:, 0, :], lg, AX.X, ALU.max))
                        done(v.tensor_tensor(g_a, lg, per_tile(g1[:, 0, :]), ALU.subtract), "gmax")
                        need(dve, b, "gexp", 1)
                        link(v.tensor_reduce(g1[:, 1, :], g_b, AX.X, ALU.add))
                        link(v.reciprocal(g1[:, 2, :], g1[:, 1, :]))
                        link(v.tensor_tensor(g_a, g_b, per_tile(g1[:, 2, :]), ALU.mult))
                        for k, (probs, one) in enumerate(((g_a, mask1), (g_b, mask2))):
                            link(v.tensor_reduce(gate_b[:, :, k], probs, AX.X, ALU.max))
                            link(v.tensor_tensor(g_c, probs, per_tile(gate_b[:, :, k]), ALU.is_equal))
                            link(v.tensor_tensor(g_c, g_c, per_expert(e_less[:, :]), ALU.mult))
                            link(v.tensor_reduce(g1[:, 3 + k, :], g_c, AX.X, ALU.min))
                            link(v.tensor_tensor(one, per_expert(e_less[:, :]), per_tile(g1[:, 3 + k, :]), ALU.is_equal))
                            if k == 0:
                                link(v.scalar_tensor_tensor(g_b, mask1, -2.0, g_a, ALU.mult, ALU.add))
                        done(v.tensor_tensor(maskb[:, :, :], mask1, mask2, ALU.add), "mask")
                        done(v.tensor_copy(gate_all[:, span(b, 2 * T)], gate_b[:, :, :].rearrange("p t k -> p (t k)")), "slot_copy")
                    elif kind == "slots":
                        need(dve, b, "rank_ps", 1)
                        count = bank(0, T * E, T * E).rearrange("p (t e) -> p t e", t=T)
                        for t in range(T):
                            link(v.tensor_tensor(ahead[:, t + 1, :], ahead[:, t, :], count[:, t, :], ALU.add))
                        link(v.tensor_tensor(pos, ahead[:, 0:T, :], bank(0, T * E).rearrange("p (t e) -> p t e", t=T), ALU.add))
                        link(v.tensor_tensor(pos, pos, per_expert(e_row[:, :]), ALU.add))
                        for k, one in enumerate((mask1, mask2)):
                            link(v.tensor_tensor(g_c, pos, one, ALU.mult))
                            link(v.tensor_reduce(idx_f[:, :, k], g_c, AX.X, ALU.add))
                        before(dve, b, "scat")
                        link(v.tensor_copy(idx_u[:, :], idx_f[:, :, :].rearrange("p t k -> p (t k)")))
                        link(v.tensor_copy(ahead[:, 0, :], ahead[:, T, :]))
                        done(v.tensor_copy(idx_all[:, span(b, 2 * T)], idx_f[:, :, :].rearrange("p t k -> p (t k)")), "slot")
                    elif kind == "max":
                        hp = step[1]
                        for t in range(T):
                            need(dve, b, "a_ps", nmax + 1)
                            o = nmax % 2 * 1024
                            done(v.tensor_reduce(nm[:, t, 2 * hp:2 * hp + 2], ps[:, o:o + 1024].rearrange("p (i n) -> p i n", i=2)[:, :, 0:(t + 1) * P],
                                                 AX.X, ALU.max, negate=True), "a_max")
                            nmax += 1
                    elif kind == "shift_parts":
                        half = step[1]
                        heads = slice(half * H // 2, (half + 1) * H // 2)
                        need(dve, b, "a_max", 16 * (half + 1))
                        if half:
                            need(dve, b, "mT_ps", 1)
                        link(v.tensor_copy(npart[:, :, 0, heads], nm[:, :, heads]))
                        link(v.tensor_tensor(nr[:, :, heads], nm[:, :, heads], npart[:, :, 0, heads], ALU.subtract))
                        link(v.tensor_copy(npart[:, :, 1, heads], nr[:, :, heads]))
                        done(v.tensor_tensor(npart[:, :, 2, heads], nr[:, :, heads], npart[:, :, 1, heads], ALU.subtract), "m_part")
                    elif kind == "shift":
                        half = step[1]
                        need(dve, b, "mT_ps", half + 1)
                        done(v.tensor_copy(mT[:, half, :], bank(6 * half, 256).bitcast(BF16)[0:MROWS * H, :]), "mT_sb")
                    elif kind == "out_t":
                        out_t(b, step[1])
                    elif kind == "f_out_t":
                        out_t(c, step[1])
                    elif kind == "f_h_turn":
                        if b is None:
                            shift_indices()
                    elif kind == "f_o_norm":
                        need(dve, c, "wo_ri", 1)
                        need(dve, c, "oT_ps", 2)
                        for i in range(2):
                            for t in (2 * i, 2 * i + 1):
                                last = v.scalar_tensor_tensor(o_tok[:, t, :], bank((4, 7)[i], D, t % 2 * D), ri[:, 0, t:t + 1], aw_bc[:, :], ALU.mult, ALU.mult)
                            done(last, "wo_n")
                    elif kind == "fu":
                        m = step[1]
                        need(dve, c, "fu_th", m + 1)
                        if m == 0:
                            before(dve, c, "y")
                        done(v.scalar_tensor_tensor(uu[:, m % 2, :], th[:, m % 2, :], 1.0, bank(up_banks(b, m)[0]), ALU.add, ALU.mult), "fu_u")
                        need(dve, c, "fu_u", m + 1)
                        if m >= 2:
                            need(dve, c, "fd_ps", m - 1)
                        else:
                            before(dve, c, "fd_ps")
                        done(v.scalar_tensor_tensor(gT[:, m % 2, :], uu[:, m % 2, :], 0.5, bank(up_banks(b, m)[1]), ALU.mult, ALU.mult), "fu_g")
                    elif kind == "f_end":
                        need(dve, c, "fd_ri", 1)
                        for t in range(T):
                            last = v.scalar_tensor_tensor(scaled[:, t, :], bank((4, 7)[t // 2], D, t % 2 * D), ri[:, 1, t:t + 1], fw_bc[:, :], ALU.mult, ALU.mult)
                        done(last, "fd_n")

            in_batches(dve, batch, make_table)

            def tiles(q, is_first, is_last):
                def g_out(t, i):
                    dve.wait_ge(moe["gT_ps"], t + 1)
                    if not (is_first and i < 2):
                        dve.wait_ge(moe["dn_ps"], t - 1)
                    v.tensor_copy(e_gT[:, i % 2, :], bank(4 + i % 2, D)).then_inc(moe["gT"], 1)

                for i in range(4):
                    t = q * 4 + i
                    if not (is_first and i == 0):
                        g_out(t - 1, (i - 1) % 4 + (0 if i else 8))
                    dve.wait_ge(moe["th"], t + 1)
                    v.scalar_tensor_tensor(e_uu[:, i % 2, :], e_th[:, i % 2, :], 1.0, bank(2 + i % 2, D), ALU.add, ALU.mult).then_inc(moe["u"], 1)
                    dve.wait_ge(moe["u"], t + 1)
                    if not (is_first and i < 2):
                        dve.wait_ge(moe["gT_ps"], t - 1)
                    v.scalar_tensor_tensor(e_g[:, i % 2, :], e_uu[:, i % 2, :], 0.5, bank(2 + i % 2, D, D), ALU.mult, ALU.mult).then_inc(moe["g"], 1)
                if is_last:
                    g_out(t, 3)

            in_tiles(dve, tiles)
            dve.wait_ge(moe["dn_ps"], MT)

            with dve.Fori(0, B // 2, 1) as q:
                for i in range(2):
                    n = q * 2 + i
                    v.tensor_copy(gate_now[:, i, :], gate_all[:, span(n, 2 * T)]).then_inc(fin["gates"], 1)
                    dve.wait_ge(fin["gates"], n + 1)
                    dve.wait_ge(got[i], q * 128 + 128)
                    for t in range(T):
                        last = v.tensor_scalar(mixed[:, i, t, :], pair[:, i, t, 0, :], gate_now[:, i, 2 * t:2 * t + 1], None, ALU.mult)
                    last.then_inc(fin["sum"], 1)
                    dve.wait_ge(fin["sum"], n + 1)
                    for t in range(T):
                        last = v.scalar_tensor_tensor(mixed[:, i, t, :], pair[:, i, t, 1, :], gate_now[:, i, 2 * t + 1:2 * t + 2], mixed[:, i, t, :], ALU.mult, ALU.add)
                    last.then_inc(fin["mix"], 1)
                for i in range(2):
                    n = q * 2 + i
                    dve.wait_ge(fin["ri"], n + 1)
                    for t in range(T):
                        last = v.scalar_tensor_tensor(mixed[:, i, t, :], mixed[:, i, t, :], ri_e[:, i, t:t + 1], mw_bc[:, :], ALU.mult, ALU.mult)
                    last.then_inc(fin["scaled"], 1)
                    dve.wait_ge(fin["scaled"], n + 1)
                    dve.wait_ge(y_in[i], q * 16 + 16)
                    v.tensor_tensor(y_sb[:, i, :, :], y_sb[:, i, :, :], mixed[:, i, :, :], ALU.add).then_inc(fin["y"], 1)

        assert counted == {n: 2 * x for n, x in per.items()}, [(n, counted.get(n), 2 * per[n]) for n in per if counted.get(n) != 2 * per[n]]


_INS = ['x', 'ctx_1024', 'L0_xattn_Wq', 'L0_xattn_bq', 'L0_xattn_Wk', 'L0_xattn_bk', 'L0_xattn_Wv', 'L0_xattn_bv',
        'L0_xattn_Wo', 'L0_xattn_bo', 'L0_ffn_wq', 'L0_ffn_wk', 'L0_ffn_wv', 'L0_ffn_wo', 'L0_ffn_w1', 'L0_ffn_w2',
        'L0_ffn_w3', 'L0_ffn_attn_norm_w', 'L0_ffn_ff_norm_w', 'L0_ffn_moe_norm_w', 'L0_ffn_router_w', 'L0_ffn_ew1',
        'L0_ffn_ew2', 'L0_ffn_ew3']


def kernel(**inputs):
    import numpy as np
    import concourse.bacc as bacc
    from concourse.bass_utils import run_bass_kernel_spmd

    nc = bacc.Bacc("TRN2", target_bir_lowering=False, num_devices=1, dynamic_dma_scratch_size=8192)
    arrays, args = {}, {}
    for name in _INS:
        a = np.ascontiguousarray(inputs[name])
        arrays[f"in_{name}"] = a
        args[name] = nc.dram_tensor(f"in_{name}", a.shape, mybir.dt.from_np(a.dtype), kind="ExternalInput").ap()
    out = nc.dram_tensor("out_x", (B, S, D), F32, kind="ExternalOutput").ap()
    xattn_ffn(nc, args, out)
    r = run_bass_kernel_spmd(nc, [arrays], core_ids=[0])
    return r.results[0]["out_x"]
```

```python
from contextlib import ExitStack

import concourse.bass as bass
from concourse import mybir

ALU = mybir.AluOpType
ACT = mybir.ActivationFunctionType
AX = mybir.AxisListType
F32 = mybir.dt.float32
F32R = mybir.dt.float32r
BF16 = mybir.dt.bfloat16

P = 128
B, S, D = 8, 512, 256
T = S // P
KD = D // P
CH, CHD, CK = 16, 64, 64
PAIRS = CH // 2
H, HD = 16, 16
NREP = 6
KREP = NREP * HD
MROWS = 3
G = H // 4
FF = 1024
FB = FF // P
E, EH = 8, 256
EB = EH // P
EPS = 1e-5
REG = S * B + P
MT = 2 * S * B // P + E
EW = (2 * KD + EB) * D
MASKED = -1e30
Q_PART = (0, 0, 1, 1, 0, 2)
K_PART = (0, 1, 0, 1, 2, 0)

PER = dict(
    x_in=16, kv_in=64, stats=5, mv1=1, rstd1=1, xn1=1, xT1=2, xnT=2, bq=1,
    m_ps=4, m_act=2, m_dve=2, bqk_ps=2, bqk_sb=2, vw_ps=4, vw_sb=4,
    sc_ps=4, sc_add=4, sc_max=4, sc_sub=4, sc_exp=4, sc_sum=4, sc_rec=4, sc_nrm=4,
    pT_ps=8, pT_sb=8, pv_ps=4, xb=1, x1=4, mv2=4, rstd2=4, xn2=4, xT2=2, xn2T=2,
    qk_ps=4, part1=4, rest1=4, part2=4, part3=4, v_ps=4, v_sb=4, lg=4,
    q_out=96, k_out=96, rep_q=96, rep_k=96,
    gmax=1, gexp=1, mask=1, rank_ps=1, slot=1, slot_copy=1, scat=256, dve_step=36, pool_a=5,
    a_ps=44, a_max=44, m_part=3, mT_ps=3, mT_sb=3, m_row=144,
    b_ps=20, b_exp=20, av_ps=4, av_sb=4, avT_ps=4, o_rec=4, o_nrm=4,
    oT_ps=2, oT_sb=2, wo_ps=2, wo_sq=2, wo_ri=1, wo_n=2, h=1, yb=1, hT_ps=2, hT_sb=2, hT_lo=2,
    fu_ps=8, fu_th=8, fu_u=8, fu_g=8, fd_ps=8, fd_sq=1, fd_ri=1, fd_n=1, y=1, y_out=16, pool_f=2,
)
AHEAD = dict(fd_n=1, fd_ps=1, y=1, y_out=16)


def maxima(hp):
    return [("max", hp, t) for t in range(T)]


STEPS = [
    ("x_norm",), ("x_turn",), ("f_out_t", G - 1), ("m_build",), ("bqk",), ("f_o_turn",),
    ("cs", 0), ("vw",), ("exp", 0), ("f_wo",), ("sum", 0), ("f_o_norm",), ("x_bias",), ("cs", 1), ("exp", 1), ("sum", 1),
    ("ct", 0), ("f_h_turn",), ("cs", 2), ("exp", 2), ("cv", 0), ("fu", 0), ("sum", 2), ("ct", 1), ("cs", 3), ("exp", 3),
    ("cv", 1), ("sum", 3), ("fu", 1), ("ct", 2), ("fd", 0), ("cv", 2), ("ct", 3), ("fd", 1), ("cv", 3), ("norm_3",),
    ("fu", 2), ("x2_turn",), ("qk",), ("v",), ("route",), ("fu", 3), ("fd", 2), ("slots",), ("fu", 4), ("fd", 3),
    *maxima(0), ("fu", 5), ("fd", 4), *maxima(1), ("fu", 6), ("fd", 5), *maxima(2),
    ("fu", 7), ("fd", 6), *maxima(3), ("shift_parts", 0), ("fd", 7), ("shift", 0),
    *maxima(4)[:2], ("f_end",), *maxima(4)[2:], ("f_scale",),
]
_late = [s for hp in (5, 6, 7) for s in (maxima(hp)[:2], maxima(hp)[2:3], maxima(hp)[3:])]
for _g in range(G):
    for _u in range(5):
        STEPS += [("score", _g, _u)]
        if _g and _u == 1:
            STEPS += [("value", _g - 1)]
        if _g and _u == 3:
            STEPS += [("out_t", _g - 1)]
        if _late:
            STEPS += _late.pop(0)
            STEPS += {6: [("shift_parts", 1)], 0: [("shift_parts", 2)]}.get(len(_late), [])
        STEPS += {(0, 4): [("shift", 1)], (2, 0): [("shift", 2)]}.get((_g, _u), [])
STEPS += [("value", G - 1)]


def steps_of(attention, net):
    if attention:
        return [s for s in STEPS if net or s[0][0] != "f"]
    order = [("f_out_t", G - 1), ("f_o_turn",), ("f_wo",), ("f_o_norm",), ("f_h_turn",), ("fu", 0)]
    for m in range(FB):
        order += ([("fu", m + 1)] if m + 1 < FB else []) + [("fd", m)]
    return order + [("f_end",), ("f_scale",)]


EARLY = 5 * T


SHIFTS = ((0, 8), (8, 12), (12, 16))


def up_banks(b, m):
    return (0, 1) if b is None and m % 2 else (4, 5)


def score_segments(j):
    order = (0, 1, 3, 2) if j % 2 == 0 else (2, 0, 1, 3)
    at = j * 1280
    found = []
    for kb in order:
        n = S - kb * P
        found.append((kb, at, n))
        at += n
    return found


def xattn_ffn(nc, A, out):
    per = PER
    counted = {}
    with ExitStack() as ctx:
        def sb(name, shape, dt=F32):
            return ctx.enter_context(nc.sbuf_tensor(name, shape, dt))

        def sem(name):
            return ctx.enter_context(nc.semaphore(name))

        reps_free = sem("reps_free")

        sems = {n: sem(n) for n in per}
        kv_out = [sem(f"p0_kv_out{i}") for i in range(4)]
        p0 = {n: sem("p0_" + n) for n in ("w_first", "bias_ps", "w_early", "w_mid", "w_late", "norms", "split_hi", "split", "ident", "const", "iota", "tr_ps", "tr_sb", "kv_ps", "kv_sb", "bk")}
        moe = {n: sem("moe_" + n) for n in ("table_step", "table", "ids_off", "ids", "ew_in", "zero", "xs_free", "xT_ps", "xT", "up_ps", "th", "u", "g", "gT_ps", "gT", "dn_ps", "eo")}
        xs_in = [sem(f"xs_in{i}") for i in range(4)]
        ids_in = [sem(f"ids_in{i}") for i in range(4)]
        eo_out = [sem(f"eo_out{i}") for i in range(4)]
        fin = {n: sem("fin_" + n) for n in ("pair_free", "gates", "mix", "sum", "sq", "eps", "ri", "scaled", "y", "y_free")}
        got = [sem(f"got{i}") for i in range(2)]
        y_in = [sem(f"y_in{i}") for i in range(2)]
        o_out = [sem(f"o_out{i}") for i in range(2)]

        wo_c = sb("wo_c", [P, PAIRS, D])
        wqT = sb("wqT", [P, PAIRS, D])
        wq = sb("wq", [P, KD, D])
        wk = sb("wk", [P, KD, D])
        wv = sb("wv", [P, KD, D + E])
        wo = sb("wo", [P, KD, D])
        w1 = sb("w1", [P, 2, KD, FF], F32R)
        w3 = sb("w3", [P, 2, KD, FF], F32R)
        w2 = sb("w2", [P, FB, D])
        bq = sb("bq", [P, PAIRS])
        bk = sb("bk", [P, PAIRS])
        bv = sb("bv", [P, PAIRS])
        bo_bc = sb("bo_bc", [P, D])
        aw_bc = sb("aw_bc", [P, D])
        fw_bc = sb("fw_bc", [P, D])
        mw_bc = sb("mw_bc", [P, D])
        ident = sb("ident", [P, P])
        ident_b = sb("ident_b", [P, P], BF16)
        mask_qk = sb("mask_qk", [P, P], BF16)
        mask_kq = sb("mask_kq", [P, P], BF16)
        before_b = sb("before_b", [P, P], BF16)
        ones_b = sb("ones_b", [P, P], BF16)
        neg_half = sb("neg_half", [P, T])
        eps = sb("eps", [P, 2, T])
        spare = sb("spare", [P, 1])
        spare_p = sb("spare_p", [P, 1])
        e_less = sb("e_less", [P, E])
        e_row = sb("e_row", [P, E])
        tile_at = sb("tile_at", [P, S * B // P])
        tile_no = sb("tile_no", [P, MT])
        iotas = sb("iotas", [P, 3 * E + 1 + S * B // P + MT + 2 * B * T], mybir.dt.int32)
        pad_ids = sb("pad_ids", [P, E + 1], mybir.dt.uint32)
        ids_all = sb("ids_all", [P, 2 * B * T], mybir.dt.uint32)
        zeros = sb("zeros", [P, D])

        k_bd = sb("k_bd", [P, PAIRS, P])
        v_bd = sb("v_bd", [P, PAIRS, P])
        room = sb("room", [P, 2 * 5120 + 2 * H * S // 2])
        big = room[:, 0:2 * 5120]
        q_rep = room[:, 10240:10240 + 4096].bitcast(BF16).rearrange("p (h n) -> p h n", h=H)
        k_rep = room[:, 14336:14336 + 4096].bitcast(BF16).rearrange("p (h n) -> p h n", h=H)

        def part(a, n):
            return room[:, a:a + n]

        m_sb = part(0, 2048).rearrange("p (k n) -> p k n", k=KD)
        vw = part(2048, 2048).rearrange("p (a n) -> p a n", a=PAIRS)
        bqk = part(4096, 1024)
        s_sb = part(5120, 2048).rearrange("p (i n) -> p i n", i=2)
        pT = part(7168, 2048).rearrange("p (i n) -> p i n", i=2)
        bq_bc = part(9216, 1024).rearrange("p (a n) -> p a n", a=PAIRS)
        prob = big.rearrange("p (i n) -> p i n", i=2)
        wq_c = part(0, 2048).rearrange("p (k n) -> p k n", k=KD)
        wk_c = part(2048, 2048).rearrange("p (k n) -> p k n", k=KD)
        wv_c = part(4096, 2048).rearrange("p (k n) -> p k n", k=KD)
        ctx_in = part(6144, 1024).rearrange("p (t n) -> p t n", t=4)
        ctxT = part(7168, 1024).rearrange("p (k n) -> p k n", k=KD)
        bias_in = part(8192 + 3 * 512, P)[0:3 * PAIRS, :]
        kv_st = part(8192, 2048).rearrange("p (i n) -> p i n", i=4)
        ew = part(0, E * EW)
        base2 = E * EW
        xs = part(base2, 4 * D).rearrange("p (i n) -> p i n", i=4)
        xsT = part(base2 + 1024, 2 * D).rearrange("p (i n) -> p i n", i=2)
        e_th = part(base2 + 1536, 2 * D).rearrange("p (i n) -> p i n", i=2)
        e_uu = part(base2 + 2048, 2 * D).rearrange("p (i n) -> p i n", i=2)
        e_g = part(base2 + 2560, 2 * D).rearrange("p (i n) -> p i n", i=2)
        e_gT = part(base2 + 3072, 2 * D).rearrange("p (i n) -> p i n", i=2)
        eo = part(base2 + 3584, 4 * D).rearrange("p (i n) -> p i n", i=4)

        xin = sb("xin", [P, T, D])
        x1 = sb("x1", [P, T, D])
        xn = sb("xn", [P, T, D])
        yb = sb("yb", [P, T, D])
        xnT = sb("xnT", [P, KD, S])
        xn2T = sb("xn2T", [P, KD, S])
        hT = sb("hT", [P, 2, KD, S], F32R)
        o_tok = sb("o_tok", [P, T, D])
        oT = sb("oT", [P, KD, S])
        parts = [xnT[:, :, :].rearrange("p k n -> p (k n)").bitcast(BF16).rearrange("p (a n) -> p a n", a=4),
                 o_tok[:, :, :].rearrange("p t n -> p (t n)").bitcast(BF16).rearrange("p (a n) -> p a n", a=4),
                 oT[:, :, :].rearrange("p k n -> p (k n)").bitcast(BF16).rearrange("p (a n) -> p a n", a=4)]
        rest = xin[:, :, :].rearrange("p t d -> p (t d)").rearrange("p (i n) -> p i n", i=2)
        v_aug = sb("v_aug", [P, T * H * (HD + 1) + 16])
        v_heads = v_aug[:, 0:T * H * (HD + 1)].rearrange("p (t h n) -> p t h n", t=T, h=H)
        gT = sb("gT", [P, 2, S])
        xh = gT[:, :, :].rearrange("p i n -> p (i n)").rearrange("p (t d) -> p t d", t=T)
        th = sb("th", [P, 2, S])
        squares = th[:, :, :].rearrange("p i n -> p (i n)").rearrange("p (t d) -> p t d", t=T)
        scaled = gT[:, :, :].rearrange("p i n -> p (i n)").rearrange("p (t d) -> p t d", t=T)
        av = th[:, 0, :]
        st1 = sb("st1", [P, T, 6])
        st2 = sb("st2", [P, T, 6])
        mv1 = sb("mv1", [P, T, 2])
        mv2 = sb("mv2", [P, T, 2])
        rs1 = sb("rs1", [P, T])
        rs2 = sb("rs2", [P, T])
        ve_a = sb("ve_a", [P, 5, T])
        ve_f = sb("ve_f", [P, 2, T])
        w13_in = [part(10240, KD * FF).rearrange("p (k n) -> p k n", k=KD), part(10240 + KD * FF, KD * FF).rearrange("p (k n) -> p k n", k=KD)]
        cmax = sb("cmax", [P, 2, CH])
        csum = sb("csum", [P, 2, CH])
        crec = sb("crec", [P, 2, CH])
        small = sb("small", [P, 8, T, E])
        lg, g_a, g_b, g_c, mask1, mask2, mask, pos = (small[:, i, :, :] for i in range(8))
        g1 = sb("g1", [P, 8, T])
        maskb = sb("maskb", [P, T, E], BF16)
        ahead = sb("ahead", [P, T + 1, E])
        idx_f = sb("idx_f", [P, T, 2])
        idx_u = sb("idx_u", [P, T * 2], mybir.dt.uint32)
        ids_now = sb("ids_now", [P, T * 2], mybir.dt.uint32)
        ids_in_sb = sb("ids_in_sb", [P, 4], mybir.dt.uint32)
        ids_off = sb("ids_off", [P, 4], mybir.dt.uint32)
        ids_u = sb("ids_u", [P, 4], mybir.dt.uint32)
        spare_off = sb("spare_off", [P, MT], mybir.dt.uint32)
        gate_b = sb("gate_b", [P, T, 2])
        gate_all = sb("gate_all", [P, B * T * 2])
        nm = sb("nm", [P, T, H])
        nr = sb("nr", [P, T, H])
        nparts = sb("nparts", [P, T, P], BF16)
        npart = nparts[:, :, 0:MROWS * H].rearrange("p t (r h) -> p t r h", r=MROWS)
        mT = sb("mT", [MROWS * H, 3, S], BF16)
        orec = sb("orec", [P, T, 4])
        ss = sb("ss", [P, 2, T])
        ri = sb("ri", [P, 2, T])
        n_tiles = sb("n_tiles", [P, E])
        first = sb("first", [P, E + 1])
        cmp_j = sb("cmp_j", [P, E, S * B // P])
        table = sb("table", [P, 2, MT], mybir.dt.uint32)
        zero_row = sb("zero_row", [P, E], mybir.dt.uint32)
        t_a = sb("t_a", [P, 4, MT])
        begun = rest[:, :, :].rearrange("p i n -> p (i n)")[:, 0:MT * E].rearrange("p (j e) -> p j e", e=E)
        pair = room[:, 0:2 * T * 2 * D].rearrange("p (i t k d) -> p i t k d", i=2, t=T, k=2)
        mixed = room[:, 4096:4096 + 2 * T * D].rearrange("p (i t d) -> p i t d", i=2, t=T)
        y_sb = room[:, 6144:6144 + 2 * T * D].rearrange("p (i t d) -> p i t d", i=2, t=T)
        squares_e = room[:, 8192:8192 + 2 * T * D].rearrange("p (i t d) -> p i t d", i=2, t=T)
        gate_now = sb("gate_now", [P, 2, T * 2])
        ss_e = sb("ss_e", [P, 2, T])
        se_e = sb("se_e", [P, 2, T])
        ri_e = sb("ri_e", [P, 2, T])

        ps = ctx.enter_context(nc.psum_tensor("ps", [P, 8 * 512], F32))

        def bank(i, n=512, at=0):
            return ps[:, i * 512 + at:i * 512 + at + n]

        def internal(name, shape, dt=F32):
            return nc.dram_tensor(name, shape, dt, kind="Internal").ap()

        kt_d = internal("kt_d", (PAIRS, P, B * CK))
        vt_d = internal("vt_d", (PAIRS, P, B * CK))
        parts_d = internal("parts_d", (3, 2, KD, P, S), BF16)
        y_d = internal("y_d", (B, P, T, D))
        xs_d = internal("xs_d", (E * REG + P, D))
        ids_d = internal("ids_d", (E * REG + P, 1), mybir.dt.uint32)
        pair_d = internal("pair_d", (2 * B * S + (E + 1 + MT) * P, D))

        def done(ins, name, n=1):
            counted[name] = counted.get(name, 0) + n
            return ins.then_inc(sems[name], n)

        def need(eng, b, name, k):
            eng.wait_ge(sems[name], b * per[name] + k + AHEAD.get(name, 0))

        def before(eng, b, name):
            if not (isinstance(b, int) and b == 0):
                eng.wait_ge(sems[name], b * per[name] + AHEAD.get(name, 0))

        def carry_wait():
            nc.vector.memset(spare[:, :], 0.0)

        def in_batches(eng, walk, before_last=lambda: None):
            walk(0, None)
            with eng.Fori(1, B, 1) as b:
                walk(b, b - 1)
            before_last()
            walk(None, B - 1)

        def walked(b, c):
            return steps_of(b is not None, c is not None)

        def in_tiles(eng, walk, peeled=1):
            for q in range(peeled):
                walk(q, q == 0, False)
            with eng.Fori(peeled, MT // 4 - 1, 1) as q:
                walk(q, False, False)
            walk(MT // 4 - 1, False, True)

        x_v = A["x"].rearrange("b (t p) d -> b p t d", p=P)
        o_v = out.rearrange("b (t p) d -> b p t d", p=P)

        def at_batch(v, b):
            return v[b:b + 1, :, :, :].rearrange("a p t d -> p (a t) d") if isinstance(b, int) else v[bass.ds(b, 1), :, :, :].rearrange("a p t d -> p (a t) d")

        def span(b, n):
            return slice(b * n, (b + 1) * n) if isinstance(b, int) else bass.ds(b * n, n)

        block = ctx.enter_context(nc.Block())

        @block.sync
        def _(sp):
            def load_x(b):
                before(sp, b, "xb")
                before(sp, b, "xn1")
                done(sp.dma_start(xin[:, :, :], at_batch(x_v, b)), "x_in", 16)

            for i, src in enumerate(("L0_xattn_bq", "L0_xattn_bk", "L0_xattn_bv")):
                sp.dma_start(bias_in[i * PAIRS:(i + 1) * PAIRS, :], A[src].rearrange("h d -> (h d)").rearrange("(a p) -> a p", p=P)).then_inc(p0["w_first"], 16)
            sp.dma_start(ctx_in, A["ctx_1024"].rearrange("b k m -> (b k) m").rearrange("(t p) m -> p t m", p=P)).then_inc(p0["w_first"], 16)
            for dst, src, name in ((wq_c, "L0_xattn_Wq", "w_first"), (wk_c, "L0_xattn_Wk", "w_early"), (wv_c, "L0_xattn_Wv", "w_early")):
                for k in range(KD):
                    sp.dma_start(dst[:, k, :], A[src].rearrange("m h d -> m (h d)")[k * P:(k + 1) * P, :]).then_inc(p0[name], 16)
            sp.dma_start(wo_c[:, :, :], A["L0_xattn_Wo"].rearrange("h d m -> (h d) m").rearrange("(a p) m -> p a m", p=P)).then_inc(p0["w_mid"], 16)
            sp.dma_start(bo_bc[:, :], A["L0_xattn_bo"].partition_broadcast(P)).then_inc(p0["w_mid"], 16)
            load_x(0)
            for i in range(2 * PAIRS):
                sp.wait_ge(p0["kv_sb"], i + 1)
                sp.dma_start((kt_d, vt_d)[i % 2][i // 2, :, :], kv_st[:, i % 4, :]).then_inc(kv_out[i % 4], 16)
            for i in range(4):
                sp.wait_ge(kv_out[i], 16 * 2 * PAIRS // 4)
            sp.wait_ge(p0["const"], 9)

            def load_late_weights():
                for dst, src in ((wq, "L0_ffn_wq"), (wk, "L0_ffn_wk")):
                    sp.dma_start(dst[:, :, :], A[src].rearrange("(k p) n -> p k n", p=P)).then_inc(p0["w_late"], 16)
                sp.dma_start(wv[:, :, 0:D], A["L0_ffn_wv"].rearrange("(k p) n -> p k n", p=P)).then_inc(p0["w_late"], 16)
                sp.dma_start(wv[:, :, D:D + E], A["L0_ffn_router_w"].rearrange("(k p) n -> p k n", p=P)).then_inc(p0["w_late"], 16)
                for dst, src in ((wo, "L0_ffn_wo"), (w13_in[0], "L0_ffn_w1"), (w13_in[1], "L0_ffn_w3"), (w2, "L0_ffn_w2")):
                    sp.dma_start(dst[:, :, :], A[src].rearrange("(k p) n -> p k n", p=P)).then_inc(p0["w_late"], 16)
                for dst, src in ((aw_bc, "L0_ffn_attn_norm_w"), (fw_bc, "L0_ffn_ff_norm_w"), (mw_bc, "L0_ffn_moe_norm_w")):
                    sp.dma_start(dst[:, :], A[src].partition_broadcast(P)).then_inc(p0["w_late"], 16)

            def batch(b, c):
                if b is not None:
                    if c is not None:
                        before(sp, b, "rep_k")
                        sp.sem_inc(reps_free, 1)
                    before(sp, b, "vw_ps")
                    for dst, src in ((k_bd, kt_d), (v_bd, vt_d)):
                        for i in range(2):
                            half = slice(i * CHD, (i + 1) * CHD)
                            done(sp.dma_start(dst[half, :, i * CK:(i + 1) * CK],
                                              src.rearrange("a p n -> p a n")[half, :, span(b, CK)]), "kv_in", 16)
                    if c is not None:
                        load_x(b)
                    else:
                        load_late_weights()
                    for a in range(4):
                        for i, name in enumerate(("part1", "part2", "part3")):
                            need(sp, b, name, a + 1)
                            done(sp.dma_start(parts_d[i, a // 2, a % 2, :, :], parts[i][:, a, :]), ("q_out", "k_out")[a // 2], 16)
                    if c is not None:
                        before(sp, b, "b_ps")
                        sp.sem_inc(reps_free, 1)
                    for which, part_of, rep, out_name, name in ((0, Q_PART, q_rep, "q_out", "rep_q"), (1, K_PART, k_rep, "k_out", "rep_k")):
                        if c is None:
                            sp.wait_ge(p0["split"], 2)
                        need(sp, b, out_name, per[out_name])
                        for j in range(NREP):
                            src = parts_d[part_of[j], which, :, :, :].rearrange("a (h d) n -> d (a h) n", d=HD)
                            done(sp.dma_start(rep[j * HD:(j + 1) * HD, :, :], src), name, 16)
                    for i, (first_head, end_head) in enumerate(SHIFTS):
                        need(sp, b, "mT_sb", i + 1)
                        for r in range(MROWS):
                            done(sp.dma_start(q_rep[KREP + r:KREP + r + 1, first_head:end_head, :], mT[r * H + first_head:r * H + end_head, i, :]), "m_row", 16)
                if c is not None:
                    need(sp, c, "y", 1)
                    done(sp.dma_start(at_batch(y_d, c), yb[:, :, :]), "y_out", 16)

            def tiles(q, is_first, is_last):
                for i in range(4):
                    row = sp.value_load(table[0:1, 1, span(q * 4 + i, 1)], min_val=0, max_val=E * REG)
                    if not is_first:
                        sp.wait_ge(moe["xT_ps"], q * 4 + i - 3)
                        sp.sem_inc(moe["xs_free"], 1)
                    sp.dma_start(xs[:, i, :], xs_d[bass.ds(row, P), :]).then_inc(xs_in[i], 16)

            def experts_first():
                sp.wait_ge(sems["av_ps"], B * per["av_ps"])
                sp.wait_ge(sems["b_ps"], B * per["b_ps"])
                for e in range(E):
                    up = ew[:, e * EW:e * EW + 2 * KD * D].rearrange("p (k i n) -> p k i n", k=KD, i=2)
                    down = ew[:, e * EW + 2 * KD * D:(e + 1) * EW].rearrange("p (m n) -> p m n", m=EB)
                    for dst, w in ((up[:, :, 0, :], "L0_ffn_ew1"), (up[:, :, 1, :], "L0_ffn_ew3"), (down, "L0_ffn_ew2")):
                        sp.dma_start(dst, A[w][e, :, :].rearrange("(k p) n -> p k n", p=P)).then_inc(moe["ew_in"], 16)
                sp.wait_ge(moe["table"], 2)
                for e in range(E):
                    row = sp.value_load(zero_row[0:1, e:e + 1], min_val=0, max_val=E * REG - P)
                    sp.dma_start(xs_d[bass.ds(row, P), :], zeros[:, :]).then_inc(moe["zero"], 16)
                    sp.dma_start(ids_d[bass.ds(row, P), :], pad_ids[:, e:e + 1]).then_inc(moe["zero"], 16)
                sp.dma_start(xs_d[E * REG:, :], zeros[:, :]).then_inc(moe["zero"], 16)
                sp.dma_start(ids_d[E * REG:, :], pad_ids[:, E:E + 1]).then_inc(moe["zero"], 16)
                sp.wait_ge(moe["zero"], 16 * 2 * (E + 1))
                sp.wait_ge(sems["scat"], B * per["scat"])
                tiles(0, True, False)

            in_batches(sp, batch, experts_first)
            with sp.Fori(1, MT // 4, 1) as q:
                tiles(q, False, False)
            sp.wait_ge(moe["dn_ps"], MT)
            sp.wait_ge(sems["y_out"], B * per["y_out"] + AHEAD["y_out"])
            for i in range(4):
                sp.wait_ge(eo_out[i], 16 * (MT // 4))
            pairs_v = pair_d[0:2 * B * S, :].rearrange("(b t p k) d -> b p t (k d)", b=B, t=T, k=2)

            def load_pair(n, i):
                sp.dma_start(pair[:, i, :, :, :].rearrange("p t k d -> p t (k d)"), at_batch(pairs_v, n)).then_inc(got[i], 16)

            for i in range(2):
                load_pair(i, i)
            for i in range(2):
                sp.dma_start(y_sb[:, i, :, :], at_batch(y_d, i)).then_inc(y_in[i], 16)
            with sp.Fori(0, B // 2 - 1, 1) as q:
                for i in range(2):
                    sp.wait_ge(fin["mix"], q * 2 + i + 1)
                    sp.sem_inc(fin["pair_free"], 1)
                    load_pair(q * 2 + i + 2, i)
                for i in range(2):
                    sp.wait_ge(fin["y"], q * 2 + i + 1)
                    sp.sem_inc(fin["y_free"], 1)
                    sp.dma_start(at_batch(o_v, q * 2 + i), y_sb[:, i, :, :]).then_inc(o_out[i], 16)
                for i in range(2):
                    sp.wait_ge(o_out[i], q * 16 + 16)
                    sp.sem_inc(fin["y_free"], 1)
                    sp.dma_start(y_sb[:, i, :, :], at_batch(y_d, q * 2 + i + 2)).then_inc(y_in[i], 16)
            for i in range(2):
                sp.wait_ge(fin["y"], B - 1 + i)
                sp.dma_start(at_batch(o_v, B - 2 + i), y_sb[:, i, :, :]).then_inc(o_out[i], 16)
            for i in range(2):
                sp.wait_ge(o_out[i], 16 * (B // 2))

        @block.gpsimd
        def _(pool):
            g = nc.gpsimd
            for name, n in AHEAD.items():
                pool.sem_inc(sems[name], n)
            for i, m in enumerate((ident, ident_b)):
                g.memset(m[:, :], 0.0).then_inc(p0["ident"], 1)
                pool.wait_ge(p0["ident"], 2 * i + 1)
                g.affine_select(out=m[:, :], in_=m[:, :], compare_op=ALU.not_equal, fill=1.0, base=0,
                                pattern=[[-1, P]], channel_multiplier=1).then_inc(p0["ident"], 1)
            for m, x in ((mask_qk, 0.0), (mask_kq, 0.0), (before_b, 1.0)):
                g.memset(m[:, :], x).then_inc(p0["ident"], 1)
            pool.wait_ge(p0["ident"], 7)
            g.affine_select(out=mask_qk[:, :], in_=mask_qk[:, :], compare_op=ALU.is_ge, fill=MASKED, base=0,
                            pattern=[[-1, P]], channel_multiplier=1).then_inc(p0["ident"], 1)
            g.affine_select(out=mask_kq[:, :], in_=mask_kq[:, :], compare_op=ALU.is_ge, fill=MASKED, base=0,
                            pattern=[[1, P]], channel_multiplier=-1).then_inc(p0["ident"], 1)
            g.affine_select(out=before_b[:, :], in_=before_b[:, :], compare_op=ALU.is_gt, fill=0.0, base=0,
                            pattern=[[1, P]], channel_multiplier=-1).then_inc(p0["ident"], 1)
            g.memset(neg_half[:, :], -0.5).then_inc(p0["const"], 1)
            g.memset(eps[:, 0, :], EPS).then_inc(p0["const"], 1)
            g.memset(eps[:, 1, :], D * EPS).then_inc(p0["const"], 1)
            g.memset(nparts[:, :, :], 0.0).then_inc(p0["const"], 1)
            g.memset(k_bd[:, :, :], 0.0).then_inc(p0["const"], 1)
            g.memset(v_bd[:, :, :], 0.0).then_inc(p0["const"], 1)
            g.memset(v_aug[:, :], 0.0).then_inc(p0["const"], 1)
            pool.wait_ge(p0["const"], 7)
            g.memset(v_heads[:, :, :, HD:HD + 1], 1.0).then_inc(p0["const"], 1)
            pool.wait_ge(p0["const"], 8)
            g.memset(k_rep[KREP:KREP + MROWS, :, :], 1.0).then_inc(p0["const"], 1)
            pool.wait_ge(p0["const"], 9)
            g.memset(ones_b[:, :], 1.0).then_inc(p0["iota"], 1)
            g.memset(zeros[:, :], 0.0).then_inc(p0["iota"], 1)
            g.memset(ahead[:, 0, :], 0.0).then_inc(p0["iota"], 1)
            at = 0
            for n, pattern, start, by_row in ((E, [[1, E]], -E, 0), (E, [[4, E]], 0, 0), (S * B // P, [[P, S * B // P]], 0, 0), (MT, [[1, MT]], 0, 0),
                                              (E + 1, [[P, E + 1]], 2 * B * S, 1), (2 * B * T, [[2 * P, B * T], [1, 2]], 0, 2)):
                g.iota(iotas[:, at:at + n], pattern=pattern, base=start, channel_multiplier=by_row).then_inc(p0["iota"], 1)
                at += n
            pool.wait_ge(p0["w_mid"], 16 * 2)

            def carry_wait():
                g.tensor_tensor(spare_p[:, :], neg_half[:, 0:1], neg_half[:, 0:1], ALU.mult)

            def batch(b, c):
                steps = {"pool_a": 0, "pool_f": 0}

                def rsqrt(n, dst, src, over, name, count, ve):
                    k, w = steps[count], src.shape[-1]
                    steps[count] += 1
                    done(g.tensor_tensor(ve[:, k, 0:w], src, eps[:, over, 0:w], ALU.add), count)
                    need(pool, n, count, k + 1)
                    done(g.tensor_tensor(dst, ve[:, k, 0:w], neg_half[:, 0:w], ALU.pow), name)

                def crossed(t):
                    need(pool, b, "mv2", t + 1)
                    rsqrt(b, rs2[:, t:t + 1], mv2[:, t, 1:2], 0, "rstd2", "pool_a", ve_a)

                for step in walked(b, c):
                    if step[0] == "x_norm":
                        need(pool, b, "mv1", 1)
                        rsqrt(b, rs1[:, :], mv1[:, :, 1], 0, "rstd1", "pool_a", ve_a)
                    elif step[0] == "f_wo":
                        for i in range(2):
                            need(pool, c, "wo_sq", i + 1)
                        rsqrt(c, ri[:, 0, :], ss[:, 0, :], 1, "wo_ri", "pool_f", ve_f)
                    elif step[0] == "f_o_norm":
                        need(pool, c, "wo_n", 2)
                        need(pool, c, "scat", per["scat"])
                        done(g.tensor_tensor(xn[:, :, :], xn[:, :, :], o_tok[:, :, :], ALU.add), "h")
                        need(pool, c, "h", 1)
                        before(pool, c, "y_out")
                        done(g.tensor_tensor(yb[:, :, :], x1[:, :, :], xn[:, :, :], ALU.add), "yb")
                    elif step[0] == "x_bias":
                        if c is not None:
                            need(pool, c, "yb", 1)
                        need(pool, b, "x_in", 16)
                        done(g.tensor_tensor(x1[:, :, :], xin[:, :, :], bo_bc[:, :].unsqueeze(1).to_broadcast([P, T, D]), ALU.add), "xb")
                    elif step[0] == "sum":
                        t = step[1]
                        need(pool, b, "sc_rec", t + 1)
                        v = s_sb[:, t % 2, :].rearrange("p (h k) -> p h k", h=CH)
                        done(g.tensor_tensor(v, v, crec[:, t % 2, :].unsqueeze(2).to_broadcast([P, CH, CK]), ALU.mult), "sc_nrm")
                    elif step[0] == "cv":
                        crossed(step[1])
                    elif step[0] == "qk":
                        for a in range(4):
                            need(pool, b, "part2", a + 1)
                            done(g.tensor_tensor(parts[2][:, a, :], rest[:, a % 2, :], parts[1][:, a, :], ALU.subtract), "part3")
                    elif step[0] == "slots":
                        need(pool, b, "slot", 1)
                        carry_wait()
                        for t in range(T):
                            for k in range(2):
                                done(g.indirect_dma_start(xs_d, bass.IndirectOffsetOnAxis(idx_u[:, 2 * t + k:2 * t + k + 1], 0),
                                                          xn[:, t, :], None), "scat", 16)
                                done(g.indirect_dma_start(ids_d, bass.IndirectOffsetOnAxis(idx_u[:, 2 * t + k:2 * t + k + 1], 0),
                                                          ids_now[:, 2 * t + k:2 * t + k + 1], None), "scat", 16)
                    elif step[0] == "f_end":
                        need(pool, c, "fd_sq", 1)
                        rsqrt(c, ri[:, 1, :], ss[:, 1, :], 1, "fd_ri", "pool_f", ve_f)
                        need(pool, c, "fd_n", 1)
                        need(pool, c, "yb", 1)
                        done(g.tensor_tensor(yb[:, :, :], yb[:, :, :], scaled, ALU.add), "y")

            in_batches(pool, batch)

            def tiles(q, is_first, is_last):
                for i in range(4):
                    t = q * 4 + i
                    g.tensor_copy(ids_off[:, i:i + 1], spare_off[:, span(t, 1)]).then_inc(moe["ids_off"], 1)
                    pool.wait_ge(moe["ids_off"], t + 1)
                    pool.wait_ge(ids_in[i], q * 16 + 16)
                    g.tensor_tensor(ids_u[:, i:i + 1], ids_in_sb[:, i:i + 1], ids_off[:, i:i + 1], ALU.add).then_inc(moe["ids"], 1)
                    pool.wait_ge(moe["ids"], t + 1)
                    pool.wait_ge(moe["eo"], t + 1)
                    carry_wait()
                    g.indirect_dma_start(pair_d, bass.IndirectOffsetOnAxis(ids_u[:, i:i + 1], 0), eo[:, i, :], None).then_inc(eo_out[i], 16)

            pool.wait_ge(moe["table"], 3)
            in_tiles(pool, tiles)
            for i in range(4):
                pool.wait_ge(eo_out[i], 16 * (MT // 4))

            with pool.Fori(0, B // 2, 1) as q:
                for i in range(2):
                    n = q * 2 + i
                    pool.wait_ge(fin["sq"], n + 1)
                    g.tensor_tensor(se_e[:, i, :], ss_e[:, i, :], eps[:, 1, :], ALU.add).then_inc(fin["eps"], 1)
                    pool.wait_ge(fin["eps"], n + 1)
                    g.tensor_tensor(ri_e[:, i, :], se_e[:, i, :], neg_half[:, :], ALU.pow).then_inc(fin["ri"], 1)

        @block.tensor
        def _(pe):
            mm, tr = nc.tensor.matmul, nc.tensor.transpose
            pe.wait_ge(p0["ident"], 2)
            pe.wait_ge(p0["w_first"], 16 * 6)
            tr(bank(7, 3 * PAIRS), bias_in[:, :], ident[0:3 * PAIRS, 0:3 * PAIRS]).then_inc(p0["bias_ps"], 1)
            blocks = [(ctx_in[:, t, k * P:(k + 1) * P]) for k in range(KD) for t in range(4)]
            blocks += [(wq_c[:, k, a * P:(a + 1) * P]) for k in range(KD) for a in range(PAIRS)]
            for i, src in enumerate(blocks):
                last = tr(bank(i // 4, P, i % 4 * P), src, ident[:, :])
                if i % 4 == 3:
                    last.then_inc(p0["tr_ps"], 1)
            pe.wait_ge(p0["tr_sb"], 6)
            pe.wait_ge(p0["w_early"], 16 * 4)
            pe.wait_ge(p0["bk"], 3)
            for i in range(2 * PAIRS):
                if i >= 2:
                    pe.wait_ge(p0["kv_sb"], i - 1)
                w = (wk_c, wv_c)[i % 2]
                for k in range(KD):
                    last = mm(bank(6 + i % 2), w[:, k, (i // 2) * P:(i // 2 + 1) * P], ctxT[:, k, :], start=(k == 0), stop=(k == KD - 1))
                last.then_inc(p0["kv_ps"], 1)
            pe.wait_ge(p0["w_mid"], 16 * 2)
            pe.wait_ge(p0["ident"], 10)
            pe.wait_ge(p0["const"], 9)
            pe.wait_ge(p0["iota"], 3)
            pe.wait_ge(p0["kv_sb"], 16)

            def v_at(kb, h):
                return (kb * H + h) * (HD + 1)

            def batch(b, c):
                def turn(n, src, banks, waits, name):
                    for t2 in range(2):
                        for w, count in waits(t2):
                            need(pe, n, w, count)
                        for k in range(KD):
                            for t in (2 * t2, 2 * t2 + 1):
                                last = tr(bank(banks[t2], P, (k * 2 + t % 2) * P), src[:, t, k * P:(k + 1) * P], ident[:, :])
                        done(last, name)

                def out_t(n, grp):
                    need(pe, n, "av_sb", grp + 1)
                    if grp:
                        need(pe, n, "o_nrm", grp)
                    if grp < 2:
                        need(pe, n, "mT_sb", grp + 2)
                    for t in range(T):
                        last = tr(bank(5, P, t * P), av[:, t * P:(t + 1) * P], ident[:, :])
                    done(last, "avT_ps")

                for step in walked(b, c):
                    kind = step[0]
                    if kind == "x_turn":
                        if c is not None:
                            need(pe, c, "b_exp", per["b_exp"])
                        turn(b, xh, (2, 3), lambda t2: [("xn1", 1)], "xT1")
                    elif kind == "m_build":
                        need(pe, b, "kv_in", 64)
                        for i in range(4):
                            k, half = i // 2, i % 2
                            if i == 2:
                                need(pe, b, "xnT", 2)
                            for a in range(4):
                                pa = half * 4 + a
                                last = mm(bank(i, P, a * P), wqT[:, pa, k * P:(k + 1) * P], k_bd[:, pa, :], start=True, stop=True)
                            done(last, "m_ps")
                    elif kind == "bqk":
                        need(pe, b, "bq", 1)
                        for i in range(2):
                            need(pe, b, ("m_act", "m_dve")[i], 1)
                            for a in range(4):
                                pa = i * 4 + a
                                last = mm(bank(i, P, a * P), bq_bc[:, pa, :], k_bd[:, pa, :], start=True, stop=True)
                            done(last, "bqk_ps")
                    elif kind == "vw":
                        for i in range(4):
                            if i < 2:
                                need(pe, b, ("m_act", "m_dve")[i], 2)
                            else:
                                need(pe, b, "vw_sb", i - 1)
                            for a in range(2):
                                last = mm(bank(2 + i % 2, D, a * D), v_bd[:, 2 * i + a, :], wo_c[:, 2 * i + a, :], start=True, stop=True)
                            done(last, "vw_ps")
                    elif kind == "cs":
                        t = step[1]
                        if t == 0:
                            need(pe, b, "m_act", 2)
                            need(pe, b, "m_dve", 2)
                            need(pe, b, "bqk_sb", 2)
                        else:
                            need(pe, b, "sc_add", t)
                        for half in range(2):
                            for k in range(KD):
                                last = mm(bank(half), xnT[:, k, t * P:(t + 1) * P], m_sb[:, k, half * 512:(half + 1) * 512], start=(k == 0), stop=(k == KD - 1))
                        done(last, "sc_ps")
                    elif kind == "ct":
                        t = step[1]
                        need(pe, b, "sc_nrm", t + 1)
                        if t == 0:
                            need(pe, b, "vw_sb", 4)
                        for half in range(2):
                            if half and t:
                                need(pe, b, "x1", t)
                            for a in range(4):
                                last = tr(bank(2 + half, P, a * P), s_sb[:, t % 2, (half * 4 + a) * P:(half * 4 + a + 1) * P], ident[:, :])
                            done(last, "pT_ps")
                    elif kind == "cv":
                        t = step[1]
                        need(pe, b, "pT_sb", 2 * t + 2)
                        for a in range(PAIRS):
                            last = mm(bank(3, D), pT[:, t % 2, a * P:(a + 1) * P], vw[:, a, :], start=(a == 0), stop=(a == PAIRS - 1))
                        done(last, "pv_ps")
                    elif kind == "x2_turn":
                        turn(b, xn, (2, 3), lambda t2: [("xn2", 2 * t2 + 2), ("x1", T)], "xT2")
                    elif kind == "qk":
                        if c is None:
                            pe.wait_ge(p0["w_late"], 16 * 11)
                        need(pe, b, "xn2T", 2)
                        for a in range(4):
                            w = (wq, wk)[a // 2]
                            for k in range(KD):
                                last = mm(bank(a), w[:, k, a % 2 * P:(a % 2 + 1) * P], xn2T[:, k, :], start=(k == 0), stop=(k == KD - 1))
                            done(last, "qk_ps")
                    elif kind == "v":
                        for t in range(T):
                            need(pe, b, "rest1", t + 1)
                            for k in range(KD):
                                last = mm(bank(t, D + E), xn2T[:, k, t * P:(t + 1) * P], wv[:, k, :], start=(k == 0), stop=(k == KD - 1))
                            done(last, "v_ps")
                    elif kind == "slots":
                        need(pe, b, "mask", 1)
                        need(pe, b, "v_sb", T)
                        mb = maskb[:, :, :].rearrange("p t e -> p (t e)")
                        mm(bank(0, T * E), before_b[:, :], mb, start=True, stop=True)
                        done(mm(bank(0, T * E, T * E), ones_b[:, :], mb, start=True, stop=True), "rank_ps")
                    elif kind == "max":
                        hp, t = step[1:]
                        nmax = hp * T + t
                        if nmax == 0:
                            need(pe, b, "slot", 1)
                            need(pe, b, "rep_q", per["rep_q"])
                            need(pe, b, "rep_k", per["rep_k"])
                        elif 2 <= nmax < EARLY:
                            need(pe, b, "a_max", nmax - 1)
                        if nmax == 16:
                            need(pe, b, "mT_sb", 1)
                        n = (t + 1) * P
                        for i in range(2):
                            h = 2 * hp + i
                            if nmax < EARLY:
                                o = nmax % 2 * 2 + i
                            else:
                                o = 6 + i
                                need(pe, b, "a_max", 2 * nmax - EARLY + i - (1 if nmax > EARLY else i))
                                if nmax == EARLY and c is not None:
                                    need(pe, c, "fd_n", 1)
                            mm(bank(o, n), q_rep[0:KREP, h, t * P:n], k_rep[0:KREP, h, 0:n], start=True, stop=False)
                            last = mm(bank(o, P, t * P), ident_b[:, :], mask_qk[:, :], start=False, stop=True)
                            if i or nmax >= EARLY:
                                done(last, "a_ps")
                    elif kind == "shift":
                        i = step[1]
                        need(pe, b, "m_part", i + 1)
                        if i == 1 and c is not None:
                            need(pe, c, "fu_g", FB)
                        elif i == 2:
                            need(pe, b, "o_nrm", 1)
                        psb = bank(5 if i else 0, 256).bitcast(BF16)
                        for t in range(T):
                            last = tr(psb[:, t * P:(t + 1) * P], nparts[:, t, :], ident_b[:, :])
                        done(last, "mT_ps")
                    elif kind == "score":
                        grp, u = step[1:]
                        n = grp * 5 + u
                        if n < 2:
                            need(pe, b, "a_max", EARLY - 1 + n)
                        if c is None and n == 0:
                            pe.wait_ge(p0["split"], 2)
                        if n in (0, 10, 15):
                            need(pe, b, "m_row", {0: 48, 10: 96, 15: 144}[n])
                        if n >= 2:
                            need(pe, b, "b_exp", n - 1)
                        for j in range(4):
                            for kb, at, w in score_segments(j):
                                if at // 1024 != u:
                                    continue
                                o = n % 2 * 1024 + at % 1024
                                mm(ps[:, o:o + w], k_rep[0:KREP + MROWS, 4 * grp + j, kb * P:(kb + 1) * P],
                                   q_rep[0:KREP + MROWS, 4 * grp + j, kb * P:S], start=True, stop=False, skip_group_check=True)
                                last = mm(ps[:, o:o + P], ident_b[:, :], mask_kq[:, :], start=False, stop=True, skip_group_check=True)
                        done(last, "b_ps")
                    elif kind == "value":
                        grp = step[1]
                        need(pe, b, "b_exp", 5 * grp + 5)
                        if grp:
                            need(pe, b, "av_sb", grp)
                        elif c is not None:
                            need(pe, c, "fu_g", FB)
                        for kb in range(T):
                            for j in range(4):
                                at = [a for k, a, _ in score_segments(j) if k == kb][0]
                                w = S - kb * P
                                last = mm(ps[32 * j:32 * j + 32, 4 * 512 + kb * P:5 * 512], v_aug[:, v_at(kb, 4 * grp + j):v_at(kb, 4 * grp + j) + 32],
                                          prob[:, grp % 2, at:at + w], start=(kb == 0), stop=(kb == T - 1),
                                          skip_group_check=True, tile_position=(0, 32 * j))
                        done(last, "av_ps")
                    elif kind == "out_t":
                        out_t(b, step[1])
                    elif kind == "f_out_t":
                        out_t(c, step[1])
                    elif kind == "f_o_turn":
                        before(pe, c, "fd_n")
                        turn(c, o_tok, (6, 7), lambda t2: [("o_nrm", G)], "oT_ps")
                    elif kind == "f_wo":
                        need(pe, c, "oT_sb", 2)
                        for t in range(T):
                            for k in range(KD):
                                last = mm(bank((6, 7)[t // 2], D, t % 2 * D), oT[:, k, t * P:(t + 1) * P], wo[:, k, :], start=(k == 0), stop=(k == KD - 1))
                            if t % 2:
                                done(last, "wo_ps")
                    elif kind == "f_h_turn":
                        turn(c, xn, (6, 7), lambda t2: [("h", 1)], "hT_ps")
                    elif kind == "fu":
                        m = step[1]
                        if m == 0:
                            need(pe, c, "hT_lo", 2)
                        elif b is not None or m >= 2:
                            need(pe, c, "fu_g", m if b is not None else m - 1)
                        for i, w in enumerate((w1, w3)):
                            terms = [(x, y, k) for x, y in ((0, 0), (0, 1), (1, 0)) for k in range(KD)]
                            for x, y, k in terms:
                                last = mm(bank(up_banks(b, m)[i]), w[:, x, k, m * P:(m + 1) * P], hT[:, y, k, :],
                                          start=((x, y, k) == terms[0]), stop=((x, y, k) == terms[-1]))
                        done(last, "fu_ps")
                    elif kind == "fd":
                        m = step[1]
                        need(pe, c, "fu_g", m + 1)
                        for t in range(T):
                            last = mm(bank((6, 7)[t // 2], D, t % 2 * D), gT[:, m % 2, t * P:(t + 1) * P], w2[:, m, :],
                                      start=(m == 0 and t % 2 == 0), stop=(m == FB - 1), skip_group_check=True)
                        done(last, "fd_ps")

            in_batches(pe, batch)
            pe.wait_ge(sems["b_exp"], B * per["b_exp"])

            pe.wait_ge(moe["table"], 2)
            pe.wait_ge(moe["ew_in"], 16 * 3 * E)

            def tiles(q, is_first, is_last):
                def turn_x(t, i):
                    pe.wait_ge(xs_in[i % 4], (q + i // 4) * 16 + 16)
                    if not (is_first and i < 2):
                        pe.wait_ge(moe["xT"], t - 1)
                    for k in range(KD):
                        last = tr(bank(i % 2, P, k * P), xs[:, i % 4, k * P:(k + 1) * P], ident[:, :])
                    last.then_inc(moe["xT_ps"], 1)

                def up(t, i):
                    at = pe.value_load(table[0:1, 0, span(t, 1)], min_val=0, max_val=(E - 1) * EW)
                    pe.wait_ge(moe["xT"], t + 1)
                    if not (is_first and i < 2):
                        pe.wait_ge(moe["g"], t - 1)
                    for k in range(KD):
                        last = mm(bank(2 + i % 2), xsT[:, i % 2, k * P:(k + 1) * P], ew[:, bass.ds(at + k * 2 * D, 2 * D)], start=(k == 0), stop=(k == KD - 1))
                    last.then_inc(moe["up_ps"], 1)

                def turn_g(t, i):
                    pe.wait_ge(moe["g"], t + 1)
                    if not (is_first and i < 2):
                        pe.wait_ge(moe["gT"], t - 1)
                    for k in range(EB):
                        last = tr(bank(4 + i % 2, P, k * P), e_g[:, i % 2, k * P:(k + 1) * P], ident[:, :])
                    last.then_inc(moe["gT_ps"], 1)

                def down(t, i):
                    at = pe.value_load(table[0:1, 0, span(t, 1)], min_val=0, max_val=(E - 1) * EW)
                    pe.wait_ge(moe["gT"], t + 1)
                    if not (is_first and i < 2):
                        pe.wait_ge(moe["eo"], t - 1)
                    for m in range(EB):
                        last = mm(bank(6 + i % 2, D), e_gT[:, i % 2, m * P:(m + 1) * P], ew[:, bass.ds(at + KD * 2 * D + m * D, D)], start=(m == 0), stop=(m == EB - 1))
                    last.then_inc(moe["dn_ps"], 1)

                if is_first:
                    turn_x(0, 0)
                for i in range(4):
                    t = q * 4 + i
                    up(t, i)
                    if is_first and i == 2:
                        pe.wait_ge(sems["fd_n"], B + AHEAD["fd_n"])
                    if not (is_first and i == 0):
                        turn_g(t - 1, (i - 1) % 4 + (0 if i else 8))
                    if not (is_last and i == 3):
                        turn_x(t + 1, i + 1)
                    if not (is_first and i < 2):
                        down(t - 2, (i - 2) % 4 + (0 if i > 1 else 8))
                if is_last:
                    turn_g(t, 3)
                    down(t - 1, 2)
                    down(t, 3)

            in_tiles(pe, tiles)

        @block.scalar
        def _(act):
            fn = nc.scalar.activation
            for i in range(6):
                act.wait_ge(p0["tr_ps"], i + 1)
                src = bank(i)
                if i < 2:
                    fn(ctxT[:, i, :], src, ACT.Copy).then_inc(p0["tr_sb"], 1)
                else:
                    k, a0 = (i - 2) // 2, (i - 2) % 2 * 4
                    fn(wqT[:, a0:a0 + 4, k * P:(k + 1) * P], src.rearrange("p (a n) -> p a n", a=4), ACT.Copy).then_inc(p0["tr_sb"], 1)
            for i in range(2 * PAIRS):
                act.wait_ge(p0["kv_ps"], i + 1)
                if i == 0:
                    act.wait_ge(p0["bk"], 3)
                if i >= 4:
                    act.wait_ge(kv_out[i % 4], 16 * (i // 4))
                if i % 2 == 0:
                    fn(kv_st[:, i % 4, :], bank(6 + i % 2), ACT.Identity, bias=bk[:, i // 2:i // 2 + 1], scale=CHD ** -0.5).then_inc(p0["kv_sb"], 1)
                else:
                    fn(kv_st[:, i % 4, :], bank(6 + i % 2), ACT.Identity, bias=bv[:, i // 2:i // 2 + 1]).then_inc(p0["kv_sb"], 1)
            act.wait_ge(p0["kv_sb"], 16)

            def batch(b, c):
                def spread(n, dst, banks, src_name, name):
                    for t2 in range(2):
                        need(act, n, src_name, t2 + 1)
                        done(fn(dst[:, :, t2 * 2 * P:(t2 + 1) * 2 * P], bank(banks[t2]).rearrange("p (k n) -> p k n", k=KD), ACT.Copy), name)

                for step in walked(b, c):
                    kind = step[0]
                    if kind == "x_turn":
                        spread(b, xnT, (2, 3), "xT1", "xnT")
                    elif kind == "m_build":
                        if c is None:
                            for i in range(4):
                                act.wait_ge(kv_out[i], 16 * 2 * PAIRS // 4)
                        for i in (0, 2):
                            need(act, b, "m_ps", i + 1)
                            done(fn(m_sb[:, i // 2, 0:512], bank(i), ACT.Copy), "m_act")
                    elif kind == "bqk":
                        for i in range(2):
                            need(act, b, "bqk_ps", i + 1)
                            done(fn(bqk[:, i * 512:(i + 1) * 512], bank(i), ACT.Copy), "bqk_sb")
                    elif kind == "vw":
                        for i in range(4):
                            need(act, b, "vw_ps", i + 1)
                            done(fn(vw[:, 2 * i:2 * i + 2, :], bank(2 + i % 2).rearrange("p (a n) -> p a n", a=2), ACT.Copy), "vw_sb")
                    elif kind == "exp":
                        t = step[1]
                        need(act, b, "sc_sub", t + 1)
                        done(fn(s_sb[:, t % 2, :], s_sb[:, t % 2, :], ACT.Exp), "sc_exp")
                    elif kind == "ct":
                        t = step[1]
                        for half in range(2):
                            need(act, b, "pT_ps", 2 * t + half + 1)
                            if t >= 2:
                                need(act, b, "pv_ps", t - 1)
                            done(fn(pT[:, t % 2, half * 512:(half + 1) * 512], bank(2 + half), ACT.Copy), "pT_sb")
                    elif kind == "x2_turn":
                        spread(b, xn2T, (2, 3), "xT2", "xn2T")
                    elif kind == "qk":
                        before(act, b, "k_out")
                        for a in range(4):
                            need(act, b, "qk_ps", a + 1)
                            done(fn(parts[0][:, a, :], bank(a), ACT.Copy, scale=(HD ** -0.5 if a < 2 else 1.0)), "part1")
                            if a >= 1:
                                need(act, b, "rest1", a)
                                done(fn(parts[1][:, a - 1, :], rest[:, (a - 1) % 2, :], ACT.Copy), "part2")
                        if c is None:
                            act.wait_ge(p0["w_late"], 16 * 11)
                            for w, src in zip((w1, w3), w13_in):
                                fn(w[:, 0, :, :], src, ACT.Copy).then_inc(p0["split_hi"], 1)
                        need(act, b, "rest1", 4)
                        done(fn(parts[1][:, 3, :], rest[:, 1, :], ACT.Copy), "part2")
                    elif kind == "v":
                        for t in range(T):
                            need(act, b, "lg", t + 1)
                            done(fn(v_heads[:, t, :, 0:HD], bank(t, D).rearrange("p (h d) -> p h d", h=H), ACT.Copy), "v_sb")
                    elif kind == "route":
                        need(act, b, "gmax", 1)
                        done(fn(g_b, g_a, ACT.Exp), "gexp")
                    elif kind == "score":
                        grp, u = step[1:]
                        n = grp * 5 + u
                        need(act, b, "b_ps", n + 1)
                        if u == 0 and grp >= 2:
                            need(act, b, "av_ps", grp - 1)
                        done(fn(prob[:, grp % 2, u * 1024:(u + 1) * 1024], ps[:, n % 2 * 1024:n % 2 * 1024 + 1024], ACT.Exp), "b_exp")
                    elif kind == "value":
                        grp = step[1]
                        need(act, b, "av_ps", grp + 1)
                        if grp:
                            need(act, b, "avT_ps", grp)
                        done(fn(av[:, :], bank(4), ACT.Copy), "av_sb")
                    elif kind == "f_o_turn":
                        spread(c, oT, (6, 7), "oT_ps", "oT_sb")
                    elif kind == "f_wo":
                        for i in range(2):
                            need(act, c, "wo_ps", i + 1)
                            for t in (2 * i, 2 * i + 1):
                                last = fn(squares[:, t, :], bank((6, 7)[i], D, t % 2 * D), ACT.Square, accum_out=ss[:, 0, t:t + 1])
                            done(last, "wo_sq")
                    elif kind == "f_h_turn":
                        spread(c, hT[:, 0, :, :], (6, 7), "hT_ps", "hT_sb")
                    elif kind == "fu":
                        m = step[1]
                        need(act, c, "fu_ps", m + 1)
                        if m >= 2:
                            need(act, c, "fu_g", m - 1)
                        done(fn(th[:, m % 2, :], bank(up_banks(b, m)[0]), ACT.Tanh, scale=0.5), "fu_th")
                    elif kind == "f_end":
                        need(act, c, "fd_ps", FB)
                        need(act, c, "fu_g", FB)
                        for t in range(T):
                            last = fn(squares[:, t, :], bank((6, 7)[t // 2], D, t % 2 * D), ACT.Square, accum_out=ss[:, 1, t:t + 1])
                        done(last, "fd_sq")

            in_batches(act, batch)

            def tiles(q, is_first, is_last):
                def x_out(t, i):
                    act.wait_ge(moe["xT_ps"], t + 1)
                    if not (is_first and i < 2):
                        act.wait_ge(moe["up_ps"], t - 1)
                    fn(xsT[:, i % 2, :], bank(i % 2, D), ACT.Copy).then_inc(moe["xT"], 1)

                def eo_copy(t, i, sent):
                    if sent is not None:
                        act.wait_ge(eo_out[i], sent * 16)
                    row = act.value_load(table[0:1, 1, span(t, 1)], min_val=0, max_val=E * REG)
                    act.dma_start(ids_in_sb[:, i:i + 1], ids_d[bass.ds(row, P), :]).then_inc(ids_in[i], 16)
                    act.wait_ge(moe["dn_ps"], t + 1)
                    fn(eo[:, i, :], bank(6 + i % 2, D), ACT.Copy).then_inc(moe["eo"], 1)

                if is_first:
                    x_out(0, 0)
                for i in range(4):
                    t = q * 4 + i
                    act.wait_ge(moe["up_ps"], t + 1)
                    if not (is_first and i < 2):
                        act.wait_ge(moe["u"], t - 1)
                    fn(e_th[:, i % 2, :], bank(2 + i % 2, D), ACT.Tanh, scale=0.5).then_inc(moe["th"], 1)
                    if not (is_last and i == 3):
                        x_out(t + 1, i + 1)
                    if i >= 2:
                        eo_copy(t - 2, i - 2, None if is_first else q)
                    elif not is_first:
                        eo_copy(t - 2, i + 2, None if isinstance(q, int) and q == 1 else q - 1)
                if is_last:
                    eo_copy(t - 1, 2, q)
                    eo_copy(t, 3, q)

            act.wait_ge(moe["zero"], 16 * 2 * (E + 1))
            act.wait_ge(sems["scat"], B * per["scat"])
            in_tiles(act, tiles, 2)

            def square(n, i):
                act.wait_ge(fin["mix"], n + 1)
                for t in range(T):
                    last = fn(squares_e[:, i, t, :], mixed[:, i, t, :], ACT.Square, accum_out=ss_e[:, i, t:t + 1])
                last.then_inc(fin["sq"], 1)

            with act.Fori(0, B // 2, 1) as q:
                for i in range(2):
                    square(q * 2 + i, i)

        @block.vector
        def _(dve):
            v = nc.vector
            dve.wait_ge(p0["bias_ps"], 1)
            for i, (dst, scale) in enumerate(((bq, 1.0), (bk, CHD ** -0.5), (bv, 1.0))):
                v.tensor_scalar(dst[:, :], bank(7, PAIRS, i * PAIRS), scale, None, ALU.mult).then_inc(p0["bk"], 1)
            dve.wait_ge(p0["bk"], 3)
            dve.wait_ge(p0["const"], 9)
            dve.wait_ge(p0["iota"], 9)
            at = 0
            for dst, n, scale in ((e_less, E, 1.0), (e_row, E, REG / 4), (tile_at, S * B // P, 1.0), (tile_no, MT, 1.0),
                                  (pad_ids, E + 1, 1.0), (ids_all, 2 * B * T, 1.0)):
                v.tensor_scalar(dst[:, :], iotas[:, at:at + n], scale, None, ALU.mult).then_inc(p0["const"], 1)
                at += n
            dve.wait_ge(p0["const"], 15)

            n_link = [0]

            def chain(ins):
                n_link[0] += 1
                ins.then_inc(moe["table_step"], 1)
                dve.wait_ge(moe["table_step"], n_link[0])

            def make_table():
                dve.wait_ge(sems["slot"], B)
                counts = ahead[:, 0, :]
                v.tensor_tensor(n_tiles[:, :], counts, e_row[:, :], ALU.add).then_inc(moe["table_step"], 1)
                n_link[0] += 1
                dve.wait_ge(moe["table_step"], n_link[0])
                v.tensor_copy(zero_row[:, :], n_tiles[:, :]).then_inc(moe["table"], 1)
                dve.wait_ge(moe["table"], 1)
                chain(v.tensor_tensor(cmp_j[:, :, :], counts.unsqueeze(2).to_broadcast([P, E, S * B // P]),
                                      tile_at[:, :].unsqueeze(1).to_broadcast([P, E, S * B // P]), ALU.is_gt))
                chain(v.tensor_reduce(n_tiles[:, :], cmp_j[:, :, :], AX.X, ALU.add))
                chain(v.memset(first[:, 0:1], 0.0))
                for e in range(E):
                    chain(v.tensor_tensor(first[:, e + 1:e + 2], first[:, e:e + 1], n_tiles[:, e:e + 1], ALU.add))
                total = first[:, E:E + 1]
                tile_c, expert, start, row = (t_a[:, i, :] for i in range(4))
                chain(v.tensor_scalar(start, tile_no[:, :], 1.0, total, ALU.add, ALU.min))
                chain(v.tensor_scalar(tile_c, start, -1.0, None, ALU.add))
                by_expert = [P, MT, E]
                starts = first[:, 0:E].unsqueeze(1).to_broadcast(by_expert)
                chain(v.tensor_tensor(begun[:, :, :], tile_c.unsqueeze(2).to_broadcast(by_expert), starts, ALU.is_ge))
                chain(v.tensor_reduce(expert, begun[:, :, :], AX.X, ALU.add))
                chain(v.tensor_tensor(begun[:, :, :], begun[:, :, :], starts, ALU.mult))
                chain(v.tensor_reduce(start, begun[:, :, :], AX.X, ALU.max))
                chain(v.tensor_scalar(expert, expert, -1.0, None, ALU.add))
                chain(v.tensor_tensor(row, tile_c, start, ALU.subtract))
                chain(v.tensor_scalar(row, row, float(P), None, ALU.mult))
                chain(v.scalar_tensor_tensor(row, expert, float(REG), row, ALU.mult, ALU.add))
                chain(v.tensor_scalar(table[:, 0, :], expert, float(EW), None, ALU.mult))
                chain(v.tensor_scalar(start, tile_no[:, :], total, None, ALU.is_lt))
                chain(v.tensor_scalar(row, row, -float(E * REG), None, ALU.add))
                chain(v.tensor_tensor(row, row, start, ALU.mult))
                v.tensor_scalar(table[:, 1, :], row, float(E * REG), None, ALU.add).then_inc(moe["table"], 1)
                chain(v.tensor_scalar(start, tile_no[:, :], total, None, ALU.is_ge))
                chain(v.tensor_tensor(start, start, tile_no[:, :], ALU.mult))
                v.tensor_scalar(spare_off[:, :], start, float(P), None, ALU.mult).then_inc(moe["table"], 1)

            def batch(b, c):
                links = [0]

                def link(ins):
                    links[0] += 1
                    done(ins, "dve_step")
                    need(dve, b, "dve_step", links[0])

                def per_tile(x):
                    return x.unsqueeze(2).to_broadcast([P, T, E])

                def per_expert(x):
                    return x.unsqueeze(1).to_broadcast([P, T, E])

                def out_t(n, grp):
                    need(dve, n, "avT_ps", grp + 1)
                    t4 = bank(5).rearrange("p (t j c) -> p t j c", t=T, j=4)
                    done(v.reciprocal(orec[:, :, :], t4[:, :, :, HD]), "o_rec")
                    need(dve, n, "o_rec", grp + 1)
                    done(v.tensor_tensor(o_tok[:, :, grp * 64:(grp + 1) * 64].rearrange("p t (j d) -> p t j d", j=4), t4[:, :, :, 0:HD],
                                         orec[:, :, :].unsqueeze(3).to_broadcast([P, T, 4, HD]), ALU.mult), "o_nrm")

                def normed(t):
                    need(dve, b, "rstd2", t + 1)
                    if t == 0 and c is not None:
                        need(dve, c, "hT_ps", 2)
                        need(dve, c, "yb", 1)
                    done(v.tensor_scalar(xn[:, t, :], x1[:, t, :], mv2[:, t, 0:1], rs2[:, t:t + 1], ALU.subtract, ALU.mult), "xn2")

                for step in walked(b, c):
                    kind = step[0]
                    if kind == "x_norm":
                        if c is not None:
                            before(dve, c, "y")
                        need(dve, b, "x_in", 16)
                        for t in range(T):
                            last = v.bn_stats(st1[:, t, :], xin[:, t, :])
                        done(last, "stats")
                        need(dve, b, "stats", 1)
                        carry_wait()
                        for t in range(T):
                            last = v.bn_aggr(mv1[:, t, :], st1[:, t, :])
                        done(last, "mv1")
                        need(dve, b, "rstd1", 1)
                        for t in range(T):
                            last = v.tensor_scalar(xh[:, t, :], xin[:, t, :], mv1[:, t, 0:1], rs1[:, t:t + 1], ALU.subtract, ALU.mult)
                        done(last, "xn1")
                    elif kind == "x_turn":
                        if c is not None:
                            need(dve, c, "av_ps", G)
                        else:
                            for i in range(4):
                                dve.wait_ge(kv_out[i], 16 * 2 * PAIRS // 4)
                        done(v.tensor_copy(bq_bc, bq[:, :].unsqueeze(2).to_broadcast([P, PAIRS, P])), "bq")
                    elif kind == "m_build":
                        for i in (1, 3):
                            need(dve, b, "m_ps", i + 1)
                            done(v.tensor_copy(m_sb[:, i // 2, 512:1024], bank(i)), "m_dve")
                    elif kind == "cs":
                        t = step[1]
                        need(dve, b, "sc_ps", t + 1)
                        if t == 0:
                            need(dve, b, "bqk_sb", 2)
                        if t >= 2:
                            need(dve, b, "pT_ps", 2 * (t - 2) + 2)
                        s3 = s_sb[:, t % 2, :].rearrange("p (h k) -> p h k", h=CH)
                        done(v.tensor_tensor(s_sb[:, t % 2, :], ps[:, 0:1024], bqk, ALU.add), "sc_add")
                        need(dve, b, "sc_add", t + 1)
                        done(v.tensor_reduce(cmax[:, t % 2, :], s3, AX.X, ALU.max), "sc_max")
                        need(dve, b, "sc_max", t + 1)
                        done(v.tensor_tensor(s3, s3, cmax[:, t % 2, :].unsqueeze(2).to_broadcast([P, CH, CK]), ALU.subtract), "sc_sub")
                    elif kind == "sum":
                        t = step[1]
                        need(dve, b, "sc_exp", t + 1)
                        if t >= 2:
                            need(dve, b, "sc_nrm", t - 1)
                        s3 = s_sb[:, t % 2, :].rearrange("p (h k) -> p h k", h=CH)
                        done(v.tensor_reduce(csum[:, t % 2, :], s3, AX.X, ALU.add), "sc_sum")
                        need(dve, b, "sc_sum", t + 1)
                        done(v.reciprocal(crec[:, t % 2, :], csum[:, t % 2, :]), "sc_rec")
                    elif kind == "cv":
                        t = step[1]
                        need(dve, b, "pv_ps", t + 1)
                        need(dve, b, "xb", 1)
                        done(v.tensor_tensor(x1[:, t, :], x1[:, t, :], bank(3, D), ALU.add), "x1")
                        need(dve, b, "x1", t + 1)
                        done(v.bn_stats(st2[:, t, :], x1[:, t, :]), "stats")
                        need(dve, b, "stats", 2 + t)
                        carry_wait()
                        done(v.bn_aggr(mv2[:, t, :], st2[:, t, :]), "mv2")
                        if t >= 1:
                            normed(t - 1)
                    elif kind == "norm_3":
                        normed(T - 1)
                    elif kind == "qk":
                        if c is None:
                            dve.wait_ge(p0["w_late"], 16 * 11)
                            for w in (aw_bc, fw_bc, mw_bc):
                                v.tensor_scalar(w[:, :], w[:, :], float(D) ** 0.5, None, ALU.mult).then_inc(p0["norms"], 1)
                            dve.wait_ge(p0["norms"], 3)
                        for a in range(4):
                            need(dve, b, "part1", a + 1)
                            if a >= 2:
                                need(dve, b, "part3", a - 1)
                            done(v.scalar_tensor_tensor(rest[:, a % 2, :], bank(a), (HD ** -0.5 if a < 2 else 1.0), parts[0][:, a, :], ALU.mult, ALU.subtract), "rest1")
                    elif kind == "v":
                        for t in range(T):
                            need(dve, b, "v_ps", t + 1)
                            done(v.tensor_copy(lg[:, t, :], bank(t, E, D)), "lg")
                        if c is None:
                            for i, (w, src) in enumerate(zip((w1, w3), w13_in)):
                                dve.wait_ge(p0["split_hi"], i + 1)
                                v.tensor_tensor(w[:, 1, :, :], src, w[:, 0, :, :].bitcast(F32), ALU.subtract).then_inc(p0["split"], 1)
                    elif kind == "route":
                        need(dve, b, "lg", T)
                        link(v.tensor_reduce(g1[:, 0, :], lg, AX.X, ALU.max))
                        done(v.tensor_tensor(g_a, lg, per_tile(g1[:, 0, :]), ALU.subtract), "gmax")
                        need(dve, b, "gexp", 1)
                        link(v.tensor_reduce(g1[:, 1, :], g_b, AX.X, ALU.add))
                        link(v.reciprocal(g1[:, 2, :], g1[:, 1, :]))
                        link(v.tensor_tensor(g_a, g_b, per_tile(g1[:, 2, :]), ALU.mult))
                        for k, (probs, one) in enumerate(((g_a, mask1), (g_b, mask2))):
                            link(v.tensor_reduce(gate_b[:, :, k], probs, AX.X, ALU.max))
                            link(v.tensor_tensor(g_c, probs, per_tile(gate_b[:, :, k]), ALU.is_equal))
                            link(v.tensor_tensor(g_c, g_c, per_expert(e_less[:, :]), ALU.mult))
                            link(v.tensor_reduce(g1[:, 3 + k, :], g_c, AX.X, ALU.min))
                            link(v.tensor_tensor(one, per_expert(e_less[:, :]), per_tile(g1[:, 3 + k, :]), ALU.is_equal))
                            if k == 0:
                                link(v.scalar_tensor_tensor(g_b, mask1, -2.0, g_a, ALU.mult, ALU.add))
                        done(v.tensor_tensor(maskb[:, :, :], mask1, mask2, ALU.add), "mask")
                        done(v.tensor_copy(gate_all[:, span(b, 2 * T)], gate_b[:, :, :].rearrange("p t k -> p (t k)")), "slot_copy")
                    elif kind == "slots":
                        need(dve, b, "rank_ps", 1)
                        count = bank(0, T * E, T * E).rearrange("p (t e) -> p t e", t=T)
                        for t in range(T):
                            link(v.tensor_tensor(ahead[:, t + 1, :], ahead[:, t, :], count[:, t, :], ALU.add))
                        link(v.tensor_tensor(pos, ahead[:, 0:T, :], bank(0, T * E).rearrange("p (t e) -> p t e", t=T), ALU.add))
                        link(v.tensor_tensor(pos, pos, per_expert(e_row[:, :]), ALU.add))
                        for k, one in enumerate((mask1, mask2)):
                            link(v.tensor_tensor(g_c, pos, one, ALU.mult))
                            link(v.tensor_reduce(idx_f[:, :, k], g_c, AX.X, ALU.add))
                        before(dve, b, "scat")
                        link(v.tensor_copy(idx_u[:, :], idx_f[:, :, :].rearrange("p t k -> p (t k)")))
                        link(v.tensor_copy(ahead[:, 0, :], ahead[:, T, :]))
                        done(v.tensor_copy(ids_now[:, :], ids_all[:, span(b, 2 * T)]), "slot")
                    elif kind == "max":
                        hp, t = step[1:]
                        nmax = hp * T + t
                        if nmax < EARLY:
                            need(dve, b, "a_ps", nmax + 1)
                            o = nmax % 2 * 1024
                            pair_ps = ps[:, o:o + 1024].rearrange("p (i n) -> p i n", i=2)[:, :, 0:(t + 1) * P]
                            done(v.tensor_reduce(nm[:, t, 2 * hp:2 * hp + 2], pair_ps, AX.X, ALU.max, negate=True), "a_max")
                        else:
                            for i in range(2):
                                need(dve, b, "a_ps", 2 * nmax - EARLY + i + 1)
                                done(v.tensor_reduce(nm[:, t, 2 * hp + i:2 * hp + i + 1], bank(6 + i, (t + 1) * P), AX.X, ALU.max, negate=True), "a_max")
                    elif kind == "shift_parts":
                        i = step[1]
                        heads = slice(*SHIFTS[i])
                        need(dve, b, "a_max", (16, EARLY + 8, per["a_max"])[i])
                        if i:
                            need(dve, b, "mT_ps", i)
                        link(v.tensor_copy(npart[:, :, 0, heads], nm[:, :, heads]))
                        link(v.tensor_tensor(nr[:, :, heads], nm[:, :, heads], npart[:, :, 0, heads], ALU.subtract))
                        link(v.tensor_copy(npart[:, :, 1, heads], nr[:, :, heads]))
                        done(v.tensor_tensor(npart[:, :, 2, heads], nr[:, :, heads], npart[:, :, 1, heads], ALU.subtract), "m_part")
                    elif kind == "shift":
                        i = step[1]
                        need(dve, b, "mT_ps", i + 1)
                        done(v.tensor_copy(mT[:, i, :], bank(5 if i else 0, 256).bitcast(BF16)[0:MROWS * H, :]), "mT_sb")
                    elif kind == "out_t":
                        out_t(b, step[1])
                    elif kind == "f_out_t":
                        out_t(c, step[1])
                    elif kind == "f_h_turn":
                        for t2 in range(2):
                            need(dve, c, "hT_sb", t2 + 1)
                            cols = slice(t2 * 2 * P, (t2 + 1) * 2 * P)
                            done(v.tensor_tensor(hT[:, 1, :, cols], bank(6 + t2).rearrange("p (k n) -> p k n", k=KD),
                                                 hT[:, 0, :, cols].bitcast(F32), ALU.subtract), "hT_lo")
                    elif kind == "f_o_norm":
                        need(dve, c, "wo_ri", 1)
                        need(dve, c, "oT_ps", 2)
                        for i in range(2):
                            for t in (2 * i, 2 * i + 1):
                                last = v.scalar_tensor_tensor(o_tok[:, t, :], bank((6, 7)[i], D, t % 2 * D), ri[:, 0, t:t + 1], aw_bc[:, :], ALU.mult, ALU.mult)
                            done(last, "wo_n")
                    elif kind == "fu":
                        m = step[1]
                        need(dve, c, "fu_th", m + 1)
                        if m == 0:
                            before(dve, c, "y")
                            if b is not None:
                                need(dve, b, "xT1", 2)
                        done(v.scalar_tensor_tensor(th[:, m % 2, :], th[:, m % 2, :], 1.0, bank(up_banks(b, m)[0]), ALU.add, ALU.mult), "fu_u")
                        need(dve, c, "fu_u", m + 1)
                        if m >= 2:
                            need(dve, c, "fd_ps", m - 1)
                        else:
                            before(dve, c, "fd_ps")
                        done(v.scalar_tensor_tensor(gT[:, m % 2, :], th[:, m % 2, :], 0.5, bank(up_banks(b, m)[1]), ALU.mult, ALU.mult), "fu_g")
                    elif kind == "f_scale":
                        need(dve, c, "fd_ri", 1)
                        for t in range(T):
                            last = v.scalar_tensor_tensor(scaled[:, t, :], bank((6, 7)[t // 2], D, t % 2 * D), ri[:, 1, t:t + 1], fw_bc[:, :], ALU.mult, ALU.mult)
                        done(last, "fd_n")

            in_batches(dve, batch, make_table)

            def tiles(q, is_first, is_last):
                def g_out(t, i):
                    dve.wait_ge(moe["gT_ps"], t + 1)
                    if not (is_first and i < 2):
                        dve.wait_ge(moe["dn_ps"], t - 1)
                    v.tensor_copy(e_gT[:, i % 2, :], bank(4 + i % 2, D)).then_inc(moe["gT"], 1)

                for i in range(4):
                    t = q * 4 + i
                    if not (is_first and i == 0):
                        g_out(t - 1, (i - 1) % 4 + (0 if i else 8))
                    dve.wait_ge(moe["th"], t + 1)
                    v.scalar_tensor_tensor(e_uu[:, i % 2, :], e_th[:, i % 2, :], 1.0, bank(2 + i % 2, D), ALU.add, ALU.mult).then_inc(moe["u"], 1)
                    dve.wait_ge(moe["u"], t + 1)
                    if not (is_first and i < 2):
                        dve.wait_ge(moe["gT_ps"], t - 1)
                    v.scalar_tensor_tensor(e_g[:, i % 2, :], e_uu[:, i % 2, :], 0.5, bank(2 + i % 2, D, D), ALU.mult, ALU.mult).then_inc(moe["g"], 1)
                if is_last:
                    g_out(t, 3)

            in_tiles(dve, tiles)
            dve.wait_ge(moe["dn_ps"], MT)

            with dve.Fori(0, B // 2, 1) as q:
                for i in range(2):
                    n = q * 2 + i
                    v.tensor_copy(gate_now[:, i, :], gate_all[:, span(n, 2 * T)]).then_inc(fin["gates"], 1)
                    dve.wait_ge(fin["gates"], n + 1)
                    dve.wait_ge(got[i], q * 16 + 16)
                    for t in range(T):
                        last = v.tensor_scalar(mixed[:, i, t, :], pair[:, i, t, 0, :], gate_now[:, i, 2 * t:2 * t + 1], None, ALU.mult)
                    last.then_inc(fin["sum"], 1)
                    dve.wait_ge(fin["sum"], n + 1)
                    for t in range(T):
                        last = v.scalar_tensor_tensor(mixed[:, i, t, :], pair[:, i, t, 1, :], gate_now[:, i, 2 * t + 1:2 * t + 2], mixed[:, i, t, :], ALU.mult, ALU.add)
                    last.then_inc(fin["mix"], 1)
                for i in range(2):
                    n = q * 2 + i
                    dve.wait_ge(fin["ri"], n + 1)
                    for t in range(T):
                        last = v.scalar_tensor_tensor(mixed[:, i, t, :], mixed[:, i, t, :], ri_e[:, i, t:t + 1], mw_bc[:, :], ALU.mult, ALU.mult)
                    last.then_inc(fin["scaled"], 1)
                    dve.wait_ge(fin["scaled"], n + 1)
                    dve.wait_ge(y_in[i], q * 16 + 16)
                    v.tensor_tensor(y_sb[:, i, :, :], y_sb[:, i, :, :], mixed[:, i, :, :], ALU.add).then_inc(fin["y"], 1)

        assert counted == {n: 2 * x for n, x in per.items()}, [(n, counted.get(n), 2 * per[n]) for n in per if counted.get(n) != 2 * per[n]]


_INS = ['x', 'ctx_1024', 'L0_xattn_Wq', 'L0_xattn_bq', 'L0_xattn_Wk', 'L0_xattn_bk', 'L0_xattn_Wv', 'L0_xattn_bv',
        'L0_xattn_Wo', 'L0_xattn_bo', 'L0_ffn_wq', 'L0_ffn_wk', 'L0_ffn_wv', 'L0_ffn_wo', 'L0_ffn_w1', 'L0_ffn_w2',
        'L0_ffn_w3', 'L0_ffn_attn_norm_w', 'L0_ffn_ff_norm_w', 'L0_ffn_moe_norm_w', 'L0_ffn_router_w', 'L0_ffn_ew1',
        'L0_ffn_ew2', 'L0_ffn_ew3']


def kernel(**inputs):
    import numpy as np
    import concourse.bacc as bacc
    from concourse.bass_utils import run_bass_kernel_spmd

    nc = bacc.Bacc("TRN2", target_bir_lowering=False, num_devices=1, dynamic_dma_scratch_size=8192)
    arrays, args = {}, {}
    for name in _INS:
        a = np.ascontiguousarray(inputs[name])
        arrays[f"in_{name}"] = a
        args[name] = nc.dram_tensor(f"in_{name}", a.shape, mybir.dt.from_np(a.dtype), kind="ExternalInput").ap()
    out = nc.dram_tensor("out_x", (B, S, D), F32, kind="ExternalOutput").ap()
    xattn_ffn(nc, args, out)
    r = run_bass_kernel_spmd(nc, [arrays], core_ids=[0])
    return r.results[0]["out_x"]
```
